# Optimizing a Trainium2 kernel written in Bass

```python
import numpy as np
import jax
import jax.numpy as jnp

def _softmax(x, axis=-1):
    return jax.nn.softmax(x, axis=axis)

def _gelu(x):
    return jax.nn.gelu(x, approximate=True)

def _silu(x):
    return jax.nn.silu(x)

def _sigmoid(x):
    return jax.nn.sigmoid(x)

def _layernorm(x, axis=-1, eps=1e-05):
    m = jnp.mean(x, axis=axis, keepdims=True)
    v = jnp.var(x, axis=axis, keepdims=True)
    return (x - m) / jnp.sqrt(v + eps)

def _scatter_add(tgt, idx, src, axis=0):
    return tgt.at[idx].add(src)

def _segment_sum(src, seg, n):
    return jax.ops.segment_sum(src, seg, n)
kernel_name = 'mk_gnn_resnorm_d4_gnn_r32_1f9c45'

def setup_inputs(seed: int=0):
    np.random.seed(seed)
    _w = jnp.asarray

    def _rec_inputs():
        import jax
        import jax.numpy as jnp
        _gk = jax.random.key(seed)
        x = -0.0005121 + 1.001 * jax.random.normal(jax.random.fold_in(_gk, 1), (3125, 32), jnp.float32)
        _s = jax.random.randint(jax.random.fold_in(_gk, 2), (25000,), 0, 3125, jnp.int32)
        _d = jax.random.randint(jax.random.fold_in(_gk, 3), (25000,), 0, 3125, jnp.int32)
        _loop = jnp.arange(3125, dtype=jnp.int32)
        src = jnp.concatenate([_s, _d, _loop])
        dst = jnp.concatenate([_d, _s, _loop])
        _o = jnp.argsort(dst, stable=True)
        src = src[_o]
        dst = dst[_o]
        edge_attr_10 = jax.random.uniform(jax.random.fold_in(_gk, 12), (53125, 10), jnp.float32, 0.0, 1)
        edge_attr_3 = 0.00109039 + 0.999626 * jax.random.normal(jax.random.fold_in(_gk, 13), (53125, 3), jnp.float32)
        edge_attr_32 = -9.77346e-05 + 0.999888 * jax.random.normal(jax.random.fold_in(_gk, 14), (53125, 32), jnp.float32)
        edge_weight = jax.random.uniform(jax.random.fold_in(_gk, 16), (53125,), jnp.float32, 0.0, 0.999997)
        return (x, src, dst, edge_attr_10, edge_attr_3, edge_attr_32, edge_weight)
    x, src, dst, edge_attr_10, edge_attr_3, edge_attr_32, edge_weight = _rec_inputs()

    def _L0_gnn_setup():
        import jax, jax.numpy as jnp
        import numpy as np
        EPS_DENOM = 1e-07
        EPS_NORM = 1e-05

        def _fcnn(x, W1, b1, W2, b2):
            return jax.nn.relu(x @ W1 + b1) @ W2 + b2
        key = jax.random.key(seed)
        N, E, D, H = (3125, 50000, 32, 128)
        ks = jax.random.split(key, 11)
        node_features = jax.random.normal(ks[0], (N, D), jnp.float32)
        edge_features = jax.random.normal(ks[1], (E, D), jnp.float32)
        edge_index = jax.random.randint(ks[2], (2, E), 0, N, dtype=jnp.int64)
        sD = 1.0 / np.sqrt(D)
        sH = 1.0 / np.sqrt(H)
        W1a = jax.random.normal(ks[3], (D, H), jnp.float32) * sD
        b1a = jax.random.normal(ks[4], (H,), jnp.float32) * sD
        W2a = jax.random.normal(ks[5], (H, D), jnp.float32) * sH
        b2a = jax.random.normal(ks[6], (D,), jnp.float32) * sH
        W1b = jax.random.normal(ks[7], (D, H), jnp.float32) * sD
        b1b = jax.random.normal(ks[8], (H,), jnp.float32) * sD
        W2b = jax.random.normal(ks[9], (H, D), jnp.float32) * sH
        b2b = jax.random.normal(ks[10], (D,), jnp.float32) * sH
        return dict(node_features=node_features, edge_features=edge_features, W1a=W1a, b1a=b1a, W2a=W2a, b2a=b2a, W1b=W1b, b1b=b1b, W2b=W2b, b2b=b2b, edge_index=edge_index)
    _L0_gnn_all = _L0_gnn_setup()
    _L0_gnn_in = {k: v for k, v in _L0_gnn_all.items() if k in ('W1a', 'b1a', 'W2a', 'b2a', 'W1b', 'b1b', 'W2b', 'b2b')}
    del _L0_gnn_all

    def _L1_gnn_setup():
        import jax, jax.numpy as jnp
        import numpy as np
        MUL = 16
        MOUT = 8
        TANH_GAIN = 1.593
        INV_SQRT3 = 0.5773502691896258
        PW_S = 0.17677669529663687
        PW_V = 0.25

        def _w3j_121():
            s2, s6 = (2 ** 0.5, 6 ** 0.5)
            M = np.zeros((5, 3, 3))
            M[0, 0, 1] = M[0, 1, 0] = 1 / s2
            M[1, 1, 2] = M[1, 2, 1] = 1 / s2
            M[2] = np.diag([-1.0, -1.0, 2.0]) / s6
            M[3, 0, 2] = M[3, 2, 0] = 1 / s2
            M[4] = np.diag([1.0, -1.0, 0.0]) / s2
            return jnp.asarray(np.transpose(M, (1, 0, 2)) / 5 ** 0.5, jnp.float32)
        W3J121 = _w3j_121()

        def _sph(edge_vec):
            n = edge_vec / jnp.linalg.norm(edge_vec, axis=1, keepdims=True)
            x, y, z = (n[:, 0], n[:, 1], n[:, 2])
            y1 = 3.0 ** 0.5 * n
            s15 = 15.0 ** 0.5
            y2 = jnp.stack([s15 * x * y, s15 * y * z, 5.0 ** 0.5 / 2 * (3 * z * z - 1), s15 * x * z, s15 / 2 * (x * x - y * y)], axis=1)
            return (y1, y2)

        def _forward(x, edge_src, edge_dst, edge_vec, emb, norm, W1, W2):
            N, E = (x.shape[0], edge_src.shape[0])
            xs = jnp.concatenate([x[edge_src, :8], x[edge_dst, :8]], axis=1)
            xv = jnp.concatenate([x[edge_src, 8:].reshape(E, 8, 3), x[edge_dst, 8:].reshape(E, 8, 3)], axis=1)
            y1, y2 = _sph(edge_vec)
            h = 2.0 ** 0.5 * jax.nn.relu(emb @ W1 / 10.0 ** 0.5)
            w = (h @ W2 / 16.0 ** 0.5).reshape(E, 7, MUL, MOUT)
            wa_s, wb_s, wa_g, wb_g, wc, wd, we = [w[:, i] for i in range(7)]
            s_out = PW_S * (jnp.einsum('eu,euw->ew', xs, wa_s) + INV_SQRT3 * jnp.einsum('eui,ei,euw->ew', xv, y1, wb_s))
            g_out = PW_S * (jnp.einsum('eu,euw->ew', xs, wa_g) + INV_SQRT3 * jnp.einsum('eui,ei,euw->ew', xv, y1, wb_g))
            v_out = PW_V * (INV_SQRT3 * jnp.einsum('eu,ek,euw->ewk', xs, y1, wc) + INV_SQRT3 * jnp.einsum('eui,euw->ewi', xv, wd) + jnp.einsum('eui,ea,iak,euw->ewk', xv, y2, W3J121, we))
            s_act = TANH_GAIN * jnp.tanh(s_out)
            gates = TANH_GAIN * jnp.tanh(g_out)
            edge_ftr = jnp.concatenate([s_act, (gates[:, :, None] * v_out).reshape(E, 24)], axis=1) * norm[:, None]
            return jax.ops.segment_sum(edge_ftr, edge_dst, num_segments=N)
        key = jax.random.key(seed)
        ks = jax.random.split(key, 8)
        N, E = (50000, 9375)
        return {'x': jax.random.normal(ks[0], (N, 32), jnp.float32), 'edge_src': jax.random.randint(ks[1], (E,), 0, N), 'edge_dst': jax.random.randint(ks[2], (E,), 0, N), 'edge_vec': jax.random.normal(ks[3], (E, 3), jnp.float32), 'emb': jax.random.uniform(ks[4], (E, 10), jnp.float32), 'norm': jax.random.uniform(ks[5], (E,), jnp.float32), 'W1': jax.random.normal(ks[6], (10, 16), jnp.float32), 'W2': jax.random.normal(ks[7], (16, 896), jnp.float32)}
    _L1_gnn_all = _L1_gnn_setup()
    _L1_gnn_in = {k: v for k, v in _L1_gnn_all.items() if k in ('W1', 'W2')}
    del _L1_gnn_all

    def _L2_gnn_setup():
        import jax, jax.numpy as jnp
        import numpy as np
        N_NODES = 3125
        N_EDGES = 50000
        N_FEAT = 32
        key = jax.random.key(seed)
        k1, k2, k3, k4 = jax.random.split(key, 4)
        u = jax.random.normal(k1, (N_NODES, N_FEAT), dtype=jnp.float32)
        weights = jax.random.uniform(k2, (N_EDGES,), dtype=jnp.float32)
        row = jax.random.randint(k3, (N_EDGES,), 0, N_NODES)
        col = jax.random.randint(k4, (N_EDGES,), 0, N_NODES)
        edge_index = jnp.stack([row, col]).astype(jnp.int64)
        return {'u': u, 'weights': weights, 'edge_index': edge_index}
    _L2_gnn_all = _L2_gnn_setup()
    _L2_gnn_in = {k: v for k, v in _L2_gnn_all.items() if k in ()}
    del _L2_gnn_all

    def _L3_gnn_setup():
        import jax, jax.numpy as jnp
        import numpy as np
        H, C = (8, 32)
        N, E = (3125, 50000)
        NEG_SLOPE = 0.2
        LN_EPS = 1e-05

        def layer_norm(x, g, b):
            mu = jnp.mean(x, axis=-1, keepdims=True)
            var = jnp.mean((x - mu) ** 2, axis=-1, keepdims=True)
            return (x - mu) * jax.lax.rsqrt(var + LN_EPS) * g + b

        def gat_conv(x, edge_index, W_gat, att_src, att_dst, bias_gat):
            n = x.shape[0]
            loops = jnp.arange(n, dtype=edge_index.dtype)
            ei = jnp.concatenate([edge_index, jnp.stack([loops, loops])], axis=1)
            src, dst = (ei[0], ei[1])
            xp = (x @ W_gat).reshape(n, H, C)
            a_src = jnp.einsum('nhc,hc->nh', xp, att_src)
            a_dst = jnp.einsum('nhc,hc->nh', xp, att_dst)
            alpha = jax.nn.leaky_relu(a_src[src] + a_dst[dst], NEG_SLOPE)
            m = jax.ops.segment_max(alpha, dst, num_segments=n)
            ea = jnp.exp(alpha - m[dst])
            denom = jax.ops.segment_sum(ea, dst, num_segments=n)
            attn = ea / (denom[dst] + 1e-16)
            msg = xp[src] * attn[..., None]
            out = jax.ops.segment_sum(msg, dst, num_segments=n)
            return out.mean(axis=1) + bias_gat
        key = jax.random.key(seed)
        ks = jax.random.split(key, 8)
        x = jax.random.normal(ks[0], (N, C), dtype=jnp.float32)
        edge_index = jax.random.randint(ks[1], (2, E), 0, N, dtype=jnp.int64)
        s = 1.0 / np.sqrt(C)
        W_gat = jax.random.normal(ks[2], (C, H * C), dtype=jnp.float32) * s
        att_src = jax.random.normal(ks[3], (H, C), dtype=jnp.float32) * s
        att_dst = jax.random.normal(ks[4], (H, C), dtype=jnp.float32) * s
        bias_gat = jnp.zeros((C,), jnp.float32)
        w1 = jax.random.normal(ks[5], (C, 128), dtype=jnp.float32) * s
        b1 = jnp.zeros((128,), jnp.float32)
        w2 = jax.random.normal(ks[6], (128, C), dtype=jnp.float32) / np.sqrt(128)
        b2 = jnp.zeros((C,), jnp.float32)
        g1 = jnp.ones((C,), jnp.float32)
        be1 = jnp.zeros((C,), jnp.float32)
        g2 = jnp.ones((C,), jnp.float32)
        be2 = jnp.zeros((C,), jnp.float32)
        return dict(x=x, edge_index=edge_index, W_gat=W_gat, att_src=att_src, att_dst=att_dst, bias_gat=bias_gat, w1=w1, b1=b1, w2=w2, b2=b2, g1=g1, be1=be1, g2=g2, be2=be2)
    _L3_gnn_all = _L3_gnn_setup()
    _L3_gnn_in = {k: v for k, v in _L3_gnn_all.items() if k in ('W_gat', 'att_src', 'att_dst', 'bias_gat', 'w1', 'b1', 'w2', 'b2', 'g1', 'be1', 'g2', 'be2')}
    del _L3_gnn_all
    return {'x': x, 'src': src, 'dst': dst, 'edge_attr_10': edge_attr_10, 'edge_attr_3': edge_attr_3, 'edge_attr_32': edge_attr_32, 'edge_weight': edge_weight, 'L0_gnn_W1a': _L0_gnn_in['W1a'], 'L0_gnn_b1a': _L0_gnn_in['b1a'], 'L0_gnn_W2a': _L0_gnn_in['W2a'], 'L0_gnn_b2a': _L0_gnn_in['b2a'], 'L0_gnn_W1b': _L0_gnn_in['W1b'], 'L0_gnn_b1b': _L0_gnn_in['b1b'], 'L0_gnn_W2b': _L0_gnn_in['W2b'], 'L0_gnn_b2b': _L0_gnn_in['b2b'], 'L1_gnn_W1': _L1_gnn_in['W1'], 'L1_gnn_W2': _L1_gnn_in['W2'], 'L3_gnn_W_gat': _L3_gnn_in['W_gat'], 'L3_gnn_att_src': _L3_gnn_in['att_src'], 'L3_gnn_att_dst': _L3_gnn_in['att_dst'], 'L3_gnn_bias_gat': _L3_gnn_in['bias_gat'], 'L3_gnn_w1': _L3_gnn_in['w1'], 'L3_gnn_b1': _L3_gnn_in['b1'], 'L3_gnn_w2': _L3_gnn_in['w2'], 'L3_gnn_b2': _L3_gnn_in['b2'], 'L3_gnn_g1': _L3_gnn_in['g1'], 'L3_gnn_be1': _L3_gnn_in['be1'], 'L3_gnn_g2': _L3_gnn_in['g2'], 'L3_gnn_be2': _L3_gnn_in['be2']}

def reference(x, src, dst, edge_attr_10, edge_attr_3, edge_attr_32, edge_weight, L0_gnn_W1a, L0_gnn_b1a, L0_gnn_W2a, L0_gnn_b2a, L0_gnn_W1b, L0_gnn_b1b, L0_gnn_W2b, L0_gnn_b2b, L1_gnn_W1, L1_gnn_W2, L3_gnn_W_gat, L3_gnn_att_src, L3_gnn_att_dst, L3_gnn_bias_gat, L3_gnn_w1, L3_gnn_b1, L3_gnn_w2, L3_gnn_b2, L3_gnn_g1, L3_gnn_be1, L3_gnn_g2, L3_gnn_be2):
    import jax
    import jax.numpy as jnp

    def _L0_gnn_ref(node_features, edge_features, W1a, b1a, W2a, b2a, W1b, b1b, W2b, b2b, edge_index):
        import jax, jax.numpy as jnp
        import numpy as np
        EPS_DENOM = 1e-07
        EPS_NORM = 1e-05

        def _fcnn(x, W1, b1, W2, b2):
            return jax.nn.relu(x @ W1 + b1) @ W2 + b2
        x = node_features
        N = x.shape[0]
        h1 = _fcnn(x, W1a, b1a, W2a, b2a)
        h2 = _fcnn(x, W1b, b1b, W2b, b2b)
        s = jax.nn.sigmoid(edge_features)
        seg = jnp.concatenate([edge_index[0], edge_index[1]])
        nbr = jnp.concatenate([edge_index[1], edge_index[0]])
        s2 = jnp.concatenate([s, s], axis=0)
        denom = EPS_DENOM + jax.ops.segment_sum(s2, seg, num_segments=N)
        msg = s2 / denom[seg] * h2[nbr]
        agg = jax.ops.segment_sum(msg, seg, num_segments=N)
        h = h1 + agg
        mu = jnp.mean(h, axis=-1, keepdims=True)
        var = jnp.var(h, axis=-1, keepdims=True)
        hn = (h - mu) * jax.lax.rsqrt(var + EPS_NORM)
        return x + jax.nn.relu(hn)

    def _L1_gnn_ref(x, edge_src, edge_dst, edge_vec, emb, norm, W1, W2):
        import jax, jax.numpy as jnp
        import numpy as np
        MUL = 16
        MOUT = 8
        TANH_GAIN = 1.593
        INV_SQRT3 = 0.5773502691896258
        PW_S = 0.17677669529663687
        PW_V = 0.25

        def _w3j_121():
            s2, s6 = (2 ** 0.5, 6 ** 0.5)
            M = np.zeros((5, 3, 3))
            M[0, 0, 1] = M[0, 1, 0] = 1 / s2
            M[1, 1, 2] = M[1, 2, 1] = 1 / s2
            M[2] = np.diag([-1.0, -1.0, 2.0]) / s6
            M[3, 0, 2] = M[3, 2, 0] = 1 / s2
            M[4] = np.diag([1.0, -1.0, 0.0]) / s2
            return jnp.asarray(np.transpose(M, (1, 0, 2)) / 5 ** 0.5, jnp.float32)
        W3J121 = _w3j_121()

        def _sph(edge_vec):
            n = edge_vec / jnp.linalg.norm(edge_vec, axis=1, keepdims=True)
            x, y, z = (n[:, 0], n[:, 1], n[:, 2])
            y1 = 3.0 ** 0.5 * n
            s15 = 15.0 ** 0.5
            y2 = jnp.stack([s15 * x * y, s15 * y * z, 5.0 ** 0.5 / 2 * (3 * z * z - 1), s15 * x * z, s15 / 2 * (x * x - y * y)], axis=1)
            return (y1, y2)

        def _forward(x, edge_src, edge_dst, edge_vec, emb, norm, W1, W2):
            N, E = (x.shape[0], edge_src.shape[0])
            xs = jnp.concatenate([x[edge_src, :8], x[edge_dst, :8]], axis=1)
            xv = jnp.concatenate([x[edge_src, 8:].reshape(E, 8, 3), x[edge_dst, 8:].reshape(E, 8, 3)], axis=1)
            y1, y2 = _sph(edge_vec)
            h = 2.0 ** 0.5 * jax.nn.relu(emb @ W1 / 10.0 ** 0.5)
            w = (h @ W2 / 16.0 ** 0.5).reshape(E, 7, MUL, MOUT)
            wa_s, wb_s, wa_g, wb_g, wc, wd, we = [w[:, i] for i in range(7)]
            s_out = PW_S * (jnp.einsum('eu,euw->ew', xs, wa_s) + INV_SQRT3 * jnp.einsum('eui,ei,euw->ew', xv, y1, wb_s))
            g_out = PW_S * (jnp.einsum('eu,euw->ew', xs, wa_g) + INV_SQRT3 * jnp.einsum('eui,ei,euw->ew', xv, y1, wb_g))
            v_out = PW_V * (INV_SQRT3 * jnp.einsum('eu,ek,euw->ewk', xs, y1, wc) + INV_SQRT3 * jnp.einsum('eui,euw->ewi', xv, wd) + jnp.einsum('eui,ea,iak,euw->ewk', xv, y2, W3J121, we))
            s_act = TANH_GAIN * jnp.tanh(s_out)
            gates = TANH_GAIN * jnp.tanh(g_out)
            edge_ftr = jnp.concatenate([s_act, (gates[:, :, None] * v_out).reshape(E, 24)], axis=1) * norm[:, None]
            return jax.ops.segment_sum(edge_ftr, edge_dst, num_segments=N)
        return _forward(x, edge_src, edge_dst, edge_vec, emb, norm, W1, W2)

    def _L2_gnn_ref(u, weights, edge_index):
        import jax, jax.numpy as jnp
        import numpy as np
        N_NODES = 3125
        N_EDGES = 50000
        N_FEAT = 32
        row, col = (edge_index[0], edge_index[1])
        diff = u[col] - u[row]
        weighted_diff = weights[:, None] * diff
        laplacian = jax.ops.segment_sum(weighted_diff, row, num_segments=u.shape[0])
        return laplacian

    def _L3_gnn_ref(x, edge_index, W_gat, att_src, att_dst, bias_gat, w1, b1, w2, b2, g1, be1, g2, be2):
        import jax, jax.numpy as jnp
        import numpy as np
        H, C = (8, 32)
        N, E = (3125, 50000)
        NEG_SLOPE = 0.2
        LN_EPS = 1e-05

        def layer_norm(x, g, b):
            mu = jnp.mean(x, axis=-1, keepdims=True)
            var = jnp.mean((x - mu) ** 2, axis=-1, keepdims=True)
            return (x - mu) * jax.lax.rsqrt(var + LN_EPS) * g + b

        def gat_conv(x, edge_index, W_gat, att_src, att_dst, bias_gat):
            n = x.shape[0]
            loops = jnp.arange(n, dtype=edge_index.dtype)
            ei = jnp.concatenate([edge_index, jnp.stack([loops, loops])], axis=1)
            src, dst = (ei[0], ei[1])
            xp = (x @ W_gat).reshape(n, H, C)
            a_src = jnp.einsum('nhc,hc->nh', xp, att_src)
            a_dst = jnp.einsum('nhc,hc->nh', xp, att_dst)
            alpha = jax.nn.leaky_relu(a_src[src] + a_dst[dst], NEG_SLOPE)
            m = jax.ops.segment_max(alpha, dst, num_segments=n)
            ea = jnp.exp(alpha - m[dst])
            denom = jax.ops.segment_sum(ea, dst, num_segments=n)
            attn = ea / (denom[dst] + 1e-16)
            msg = xp[src] * attn[..., None]
            out = jax.ops.segment_sum(msg, dst, num_segments=n)
            return out.mean(axis=1) + bias_gat
        h = gat_conv(x, edge_index, W_gat, att_src, att_dst, bias_gat)
        h = layer_norm(h + x, g1, be1)
        ff = jax.nn.relu(h @ w1 + b1) @ w2 + b2
        return layer_norm(ff + h, g2, be2)
    edge_index = jnp.stack([src, dst])
    x = _layernorm(x + _L0_gnn_ref(x, edge_attr_32, L0_gnn_W1a, L0_gnn_b1a, L0_gnn_W2a, L0_gnn_b2a, L0_gnn_W1b, L0_gnn_b1b, L0_gnn_W2b, L0_gnn_b2b, edge_index), axis=-1)
    x = _layernorm(x + _L1_gnn_ref(x, src, dst, edge_attr_3, edge_attr_10, edge_weight, L1_gnn_W1, L1_gnn_W2), axis=-1)
    x = _layernorm(x + _L2_gnn_ref(x, edge_weight, edge_index), axis=-1)
    x = _layernorm(x + _L3_gnn_ref(x, edge_index, L3_gnn_W_gat, L3_gnn_att_src, L3_gnn_att_dst, L3_gnn_bias_gat, L3_gnn_w1, L3_gnn_b1, L3_gnn_w2, L3_gnn_b2, L3_gnn_g1, L3_gnn_be1, L3_gnn_g2, L3_gnn_be2), axis=-1)
    return x

_drawn_inputs = setup_inputs


def setup_inputs(seed=0):
    import zlib

    import numpy as np

    out = dict(_drawn_inputs(seed))
    spreads = {'L3_gnn_bias_gat': (0.0, 0.1),
     'L3_gnn_b1': (0.0, 0.1),
     'L3_gnn_b2': (0.0, 0.1),
     'L3_gnn_g1': (1.0, 0.2),
     'L3_gnn_be1': (0.0, 0.1),
     'L3_gnn_g2': (1.0, 0.2),
     'L3_gnn_be2': (0.0, 0.1)}
    factors = {'edge_attr_32': 2.743, 'L3_gnn_att_dst': 11.18}
    for name, (base, spread) in spreads.items():
        noise = np.random.default_rng([zlib.crc32(name.encode()), seed]).standard_normal(out[name].shape)
        drawn = base * np.exp(spread * noise) if base else spread * noise
        out[name] = jnp.asarray(drawn.astype(out[name].dtype))
    for name, factor in factors.items():
        out[name] = (out[name] * factor).astype(out[name].dtype)
    return out
```

```python
from contextlib import ExitStack

import numpy as np

import concourse.bass as bass
from concourse import mybir

ALU = mybir.AluOpType
ACT = mybir.ActivationFunctionType
F32 = mybir.dt.float32
BF16 = mybir.dt.bfloat16
I32 = mybir.dt.int32
AX = mybir.AxisListType

N, E, D = 3125, 53125, 32
HID = 128
HEADS = 8
P = 128
TILES = 8
GROUP = P * TILES
QUAD = 4
NG = -(-E // GROUP)
NGL = NG + 2
NITER = NG // 2
NB = -(-(N + 1 + P) // P)
NT = NB * P
SPILL = N + 1
CH = 2
assert NG % 2 == 0 and NB % CH == 0

MUL, MOUT, FEAT = 16, 8, 80
TANH_GAIN = 1.593
INV_SQRT3 = 3.0 ** -0.5
PW_S, PW_V = 0.17677669529663687, 0.25
HID_SCALE = 2.0 ** 0.5 / 10.0 ** 0.5 / 16.0 ** 0.5
EPS = 1e-5
LOWEST = -1.0e30


class Kit:

    def __init__(self, nc, ctx, ins):
        self.nc, self.ctx, self.ins = nc, ctx, ins
        self.layer_sems = []

    def sem(self, name):
        self.layer_sems.append(self.nc.alloc_semaphore(name))
        return self.layer_sems[-1]

    def next_layer(self):
        self.nc.clear_and_free_semaphores(self.layer_sems)
        self.layer_sems = []
        self.nc.all_engine_barrier()

    def sems(self, name, n):
        return [self.sem(f"{name}{i}") for i in range(n)]

    def sb(self, name, shape, dt=F32, ctx=None):
        return (ctx or self.ctx).enter_context(self.nc.sbuf_tensor(name, shape, dt))

    def ps(self, name, ctx, shape=(P, 512), dt=F32):
        return ctx.enter_context(self.nc.psum_tensor(name, list(shape), dt))

    def dram(self, name, shape, dt=F32):
        return self.nc.dram_tensor(name, shape, dt, kind="Internal")


def rows_of(table):
    return table[:, :].rearrange("(j p) w -> p j w", p=P)


def blank(tile, w):
    return over(tile[:, 0:w].unsqueeze(1), [P, NB, w])


def over(ap, shape):
    return ap.to_broadcast(shape)


def waited(eng, tick):
    eng.sem_inc(tick, 1)


def chained(sem):
    count = [0]

    def step(eng, ins):
        count[0] += 1
        ins.then_inc(sem, 1)
        eng.wait_ge(sem, count[0])

    return step


def layer_norm(dve, step, x, out, c, q, st, var_ready, std_ready, n):
    full = [P, NB, D]
    step(dve, dve.tensor_reduce(st[:, 0, :], x, AX.X, ALU.add))
    step(dve, dve.tensor_scalar(st[:, 0, :], st[:, 0, :], -1.0 / D, None, ALU.mult))
    step(dve, dve.tensor_tensor(c, x, over(st[:, 0, :].unsqueeze(2), full), ALU.add))
    step(dve, dve.tensor_tensor(q, c, c, ALU.mult))
    step(dve, dve.tensor_reduce(st[:, 1, :], q, AX.X, ALU.add))
    dve.tensor_scalar(st[:, 1, :], st[:, 1, :], 1.0 / D, EPS, ALU.mult, ALU.add).then_inc(var_ready, 1)
    dve.wait_ge(std_ready, n)
    step(dve, dve.reciprocal(st[:, 3, :], st[:, 2, :]))
    step(dve, dve.tensor_tensor(out, c, over(st[:, 3, :].unsqueeze(2), full), ALU.mult))


def std_of(act, st, var_ready, std_ready, n):
    act.wait_ge(var_ready, n)
    act.activation(st[:, 2, :], st[:, 1, :], ACT.Sqrt).then_inc(std_ready, 1)


def setup(k, t):
    nc, ins = k.nc, k.ins
    loaded, sq_ready, sqrt_done, dve_step = (
        k.sem("setup_loaded"), k.sem("norm2_ready"), k.sem("norm_ready"), k.sem("setup_dve"))
    with ExitStack() as ctx:
        sq = k.sb("sq", [P, NGL * TILES, 3], F32, ctx)
        n2 = k.sb("n2", [P, NGL * TILES], F32, ctx)
        block = ctx.enter_context(nc.Block())
        loads = [
            (t.ident[:], ins["ident"]), (t.tri[:], ins["tri"]), (t.spill[:], ins["spill"]),
            (t.nvec[:], ins["edge_vec"].rearrange("(g p u) i -> p g (u i)", p=P, u=TILES)),
            (t.wgt[:], ins["edge_w"].rearrange("(g p u) -> p g u", p=P, u=TILES)),
            (t.x[:], rows_of(ins["x_rows"])),
        ]

        @block.sync
        def _(sp):
            for dst, src in loads:
                sp.dma_start(dst, src).then_inc(loaded, 16)

        @block.scalar
        def _(act):
            act.wait_ge(sq_ready, 1)
            act.activation(n2[:], n2[:], ACT.Sqrt).then_inc(sqrt_done, 1)

        @block.vector
        def _(dve):
            step = chained(dve_step)
            dve.wait_ge(loaded, 16 * len(loads))
            step(dve, dve.memset(t.zero[:], 0.0))
            step(dve, dve.memset(t.lowest[:], LOWEST))
            nv = t.nvec[:].rearrange("p g (u i) -> p (g u) i", i=3)
            step(dve, dve.tensor_tensor(sq[:], nv, nv, ALU.mult))
            dve.tensor_reduce(n2[:], sq[:], AX.X, ALU.add).then_inc(sq_ready, 1)
            dve.wait_ge(sqrt_done, 1)
            step(dve, dve.reciprocal(n2[:], n2[:]))
            step(dve, dve.tensor_tensor(nv, nv, over(n2[:].unsqueeze(2), [P, NGL * TILES, 3]), ALU.mult))
            step(dve, dve.tensor_scalar(t.wgain[:], t.wgt[:], TANH_GAIN, None, ALU.mult))


def mlp(k, tag, xT_name, xT_ap, nets, prepare=None):
    nc = k.nc
    n = len(nets)
    loaded = k.sem(f"{tag}_loaded")
    hid_done, relu_done = k.sems(f"{tag}_hid", n), k.sems(f"{tag}_relu", n)
    out_done, add_done = k.sems(f"{tag}_out", n), k.sems(f"{tag}_add", n)
    with ExitStack() as ctx:
        w1 = [k.sb(f"{tag}_w1_{i}", [D, HID], F32, ctx) for i in range(n)]
        b1 = [k.sb(f"{tag}_b1_{i}", [HID, 1], F32, ctx) for i in range(n)]
        w2 = [k.sb(f"{tag}_w2_{i}", [HID, D], F32, ctx) for i in range(n)]
        b2 = [k.sb(f"{tag}_b2_{i}", [P, D], F32, ctx) for i in range(n)]
        hid = [k.sb(f"{tag}_h{i}", [HID, CH * P], F32, ctx) for i in range(n)]
        ph = [k.ps(f"{tag}_ph{i}", ctx) for i in range(n)]
        po = [k.ps(f"{tag}_po{i}", ctx) for i in range(n)]
        block = ctx.enter_context(nc.Block())
        n_loads = 4 * n + (xT_ap is None)
        xT = k.sb(f"{tag}_xT", [D, NT], F32, ctx) if xT_ap is None else xT_ap

        @block.sync
        def _(sp):
            if xT_ap is None:
                sp.dma_start(xT[:], k.ins[xT_name]).then_inc(loaded, 16)
            for i, (a, b, c, d, _) in enumerate(nets):
                sp.dma_start(w1[i][:], k.ins[a]).then_inc(loaded, 16)
                sp.dma_start(b1[i][:], k.ins[b].rearrange("(h o) -> h o", o=1)).then_inc(loaded, 16)
                sp.dma_start(w2[i][:], k.ins[c]).then_inc(loaded, 16)
                sp.dma_start(b2[i][:], k.ins[d].partition_broadcast(P)).then_inc(loaded, 16)

        @block.tensor
        def _(pe):
            pe.wait_ge(loaded, 16 * n_loads)
            for i in range(n):
                pe.sem_inc(out_done[i], 1)
            with pe.Fori(0, NB // CH) as c:
                for i in range(n):
                    pe.matmul(ph[i][:, 0:CH * P], w1[i][:], xT[:, bass.ds(c * (CH * P), CH * P)],
                              start=True, stop=True).then_inc(hid_done[i], 1)
                for i in range(n):
                    pe.wait_ge(relu_done[i], c + 1)
                    pe.wait_ge(add_done[i], c + 1)
                    for b in range(CH):
                        mm = pe.matmul(po[i][:, b * D:(b + 1) * D], hid[i][:, b * P:(b + 1) * P], w2[i][:],
                                       start=True, stop=True)
                    mm.then_inc(out_done[i], 1)

        @block.scalar
        def _(act):
            act.wait_ge(loaded, 16 * n_loads)
            with act.Fori(0, NB // CH) as c:
                for i in range(n):
                    act.wait_ge(hid_done[i], c + 1)
                    act.wait_ge(out_done[i], c + 1)
                    act.activation(hid[i][:], ph[i][:, 0:CH * P], ACT.Relu, bias=b1[i][:, 0:1]).then_inc(relu_done[i], 1)

        @block.vector
        def _(dve):
            dve.wait_ge(loaded, 16 * n_loads)
            for i in range(n):
                dve.sem_inc(add_done[i], 1)
            with dve.Fori(0, NB // CH) as c:
                for i in range(n):
                    dve.wait_ge(out_done[i], c + 2)
                    dve.tensor_tensor(nets[i][4][:, bass.ds(c * CH, CH), :],
                                      po[i][:, 0:CH * D].rearrange("p (b d) -> p b d", d=D),
                                      over(b2[i][:].unsqueeze(1), [P, CH, D]), ALU.add).then_inc(add_done[i], 1)


def store_rows(k, tag, pairs):
    stored = k.sem(f"{tag}_stored")
    with k.nc.Block() as block:
        @block.sync
        def _(sp):
            for table, rows in pairs:
                sp.dma_start(rows_of(table), rows).then_inc(stored, 16)
            sp.wait_ge(stored, 16 * len(pairs))


def l0_edges(k, t):
    nc, ins = k.nc, k.ins
    loaded, tick, sp_tick = k.sems("l0_loaded", 2), k.sem("l0_tick"), k.sem("l0_sp_tick")
    gathered, mul_done, mm_done = k.sems("l0_gathered", 4), k.sems("l0_mul", 4), k.sems("l0_mm", 4)
    rows_ready, rows_free = k.sems("l0_rows", 4), k.sems("l0_rows_free", 4)
    sig_done, eq_done = k.sems("l0_sig", 2), k.sems("l0_eq", 2)
    added = {"dst": k.sem("l0_added_dst"), "src": k.sem("l0_added_src")}
    dve_step = k.sem("l0_dve")
    LOADS = 5
    EQ_STEPS = 12
    with ExitStack() as ctx:
        feat = [k.sb(f"l0_feat{b}", [P, TILES * D], F32, ctx) for b in range(2)]
        idx = {s: [k.sb(f"l0_{s}_idx{b}", [P, TILES], I32, ctx) for b in range(2)] for s in ("dst", "src")}
        row = {s: [k.sb(f"l0_{s}_row{b}", [P, GROUP], I32, ctx) for b in range(2)] for s in ("dst", "src")}
        eq = {s: [k.sb(f"l0_{s}_eq{b}", [P, TILES, P], F32, ctx) for b in range(2)] for s in ("dst", "src")}
        to = {s: [k.sb(f"l0_{s}_to{b}", [P, TILES], I32, ctx) for b in range(2)] for s in ("dst", "src")}
        before = k.sb("l0_before", [P, TILES, P], F32, ctx)
        rank = k.sb("l0_rank", [P, TILES], F32, ctx)
        away = k.sb("l0_away", [P, TILES], F32, ctx)
        msg = [k.sb(f"l0_msg{b}", [P, TILES, 3 * D], F32, ctx) for b in range(2)]
        h2 = {s: [k.sb(f"l0_{s}_h2_{q}", [P, QUAD, D], F32, ctx) for q in range(4)] for s in ("dst", "src")}
        rows = [k.sb(f"l0_rows{q}", [P, 2, QUAD, 2 * D], F32, ctx) for q in range(4)]
        ps = [k.ps(f"l0_ps{q}", ctx, (P, 2, QUAD, 2 * D)) for q in range(4)]
        block = ctx.enter_context(nc.Block())
        idx_d = {s: ins[f"{s}_idx"].rearrange("(g p u) -> g p u", p=P, u=TILES) for s in ("dst", "src")}
        row_d = {s: ins[f"{s}_idx"].rearrange("(g n) -> g n", n=GROUP) for s in ("dst", "src")}
        feat_d = ins["edge_feat"].rearrange("(g p u) d -> g p (u d)", p=P, u=TILES)
        table = {"dst": t.l0_dst, "src": t.l0_src}
        side = {"dst": 0, "src": 1}

        @block.sync
        def _(sp):
            def load(g, b):
                sp.dma_start(feat[b][:], feat_d[g]).then_inc(loaded[b], 16)
                for s in ("src", "dst"):
                    sp.dma_start(idx[s][b][:], idx_d[s][g]).then_inc(loaded[b], 16)
                    sp.dma_start(row[s][b][:], row_d[s][g].partition_broadcast(P)).then_inc(loaded[b], 16)

            load(0, 0)
            load(1, 1)
            with sp.Fori(0, NITER) as i:
                for b in range(2):
                    sp.wait_ge(gathered[2 * b], (i + 1) * (32 * QUAD))
                    sp.wait_ge(gathered[2 * b + 1], (i + 1) * (32 * QUAD))
                    sp.wait_ge(eq_done[b], i + 1)
                    sp.wait_ge(sig_done[b], i + 1)
                    waited(sp, sp_tick)
                    load(i * 2 + (2 + b), b)
            for b in range(2):
                sp.wait_ge(loaded[b], 16 * LOADS * (NITER + 1))

        @block.gpsimd
        def _(pool):
            def gather(q, u):
                b = q // 2
                c = QUAD * (q % 2) + u
                for s, other in (("src", "src"), ("dst", "dst")):
                    pool.indirect_dma_start(
                        out=h2[s][q][:, u, :], out_offset=None, in_=t.h2[:],
                        in_offset=bass.IndirectOffsetOnAxis(ap=idx[s][b][:, c:c + 1], axis=0)).then_inc(gathered[q], 16)

            def add(s, q, u):
                b, c = q // 2, QUAD * (q % 2) + u
                pool.indirect_dma_start(
                    out=table[s][:], out_offset=bass.IndirectOffsetOnAxis(ap=to[s][b][:, c:c + 1], axis=0),
                    in_=rows[q][:, side[s], u, :], in_offset=None, compute_op=ALU.add).then_inc(added[s], 16)

            for s in ("dst", "src"):
                pool.dma_start(rows_of(table[s]), blank(t.zero, 2 * D)).then_inc(added[s], 16)
            pool.wait_ge(loaded[0], 16 * LOADS)
            for q in range(2):
                for u in range(QUAD):
                    gather(q, u)
            with pool.Fori(0, NITER) as i:
                for q in range(4):
                    ahead = (q + 2) % 4
                    pool.wait_ge(loaded[ahead // 2], (i + (2 if q >= 2 else 1)) * (16 * LOADS))
                    pool.wait_ge(mul_done[ahead], i + (2 if q >= 2 else 1))
                    waited(pool, tick)
                    for u in range(QUAD):
                        gather(ahead, u)
                        if u == 0:
                            pool.wait_ge(rows_ready[q], i + 2)
                        for s in ("dst", "src"):
                            pool.wait_ge(added[s], (i * (4 * QUAD) + (q * QUAD + u + 1)) * 16)
                        if u == 0:
                            pool.sem_inc(rows_free[(q - 1) % 4], 1)
                        else:
                            waited(pool, tick)
                        add("dst", q, u)
                        add("src", q, u)
            for s in ("dst", "src"):
                pool.wait_ge(added[s], 16 * (NG * TILES + 1))
            for q in range(2):
                pool.wait_ge(gathered[q], 32 * QUAD * (NITER + 1))

        @block.vector
        def _(dve):
            for q in range(4):
                dve.sem_inc(mul_done[q], 1)
            with dve.Fori(0, NITER) as i:
                for b in range(2):
                    count = [0]

                    def step(ins_):
                        count[0] += 1
                        ins_.then_inc(dve_step, 1)
                        dve.wait_ge(dve_step, i * (2 * EQ_STEPS) + (b * EQ_STEPS + count[0]))

                    dve.wait_ge(loaded[b], (i + 1) * (16 * LOADS))
                    dve.wait_ge(mm_done[2 * b + 1], i + 1)
                    dve.wait_ge(rows_free[2 * b + 1], i + 1)
                    full = [P, TILES, P]
                    for s, kept in (("dst", t.to_dst), ("src", t.to_src)):
                        step(dve.tensor_tensor(eq[s][b][:], row[s][b][:].rearrange("p (e u) -> p u e", u=TILES),
                                               over(idx[s][b][:].unsqueeze(2), full), ALU.is_equal))
                        step(dve.tensor_tensor(before[:], eq[s][b][:], over(t.tri[:].unsqueeze(1), full), ALU.mult))
                        step(dve.tensor_reduce(rank[:], before[:], AX.X, ALU.add))
                        step(dve.tensor_scalar(away[:], idx[s][b][:], -1.0, t.spill[:, 0:1], ALU.mult, ALU.add))
                        step(dve.scalar_tensor_tensor(out=away[:], in0=rank[:], scalar=0.0, in1=away[:],
                                                      op0=ALU.is_gt, op1=ALU.mult))
                        step(dve.tensor_tensor(to[s][b][:], away[:], idx[s][b][:], ALU.add))
                        last = dve.tensor_copy(kept[:, i * 2 + b, :], to[s][b][:])
                    last.then_inc(eq_done[b], 1)
                    dve.wait_ge(sig_done[b], i + 1)
                    for half in range(2):
                        q, c = 2 * b + half, QUAD * half
                        dve.wait_ge(gathered[q], (i + 1) * (32 * QUAD))
                        sig = msg[b][:, c:c + QUAD, D:2 * D]
                        dve.tensor_tensor(msg[b][:, c:c + QUAD, 0:D], sig, h2["src"][q][:], ALU.mult)
                        dve.tensor_tensor(msg[b][:, c:c + QUAD, 2 * D:3 * D], sig, h2["dst"][q][:],
                                          ALU.mult).then_inc(mul_done[q], 1)

        @block.scalar
        def _(act):
            for q in range(4):
                act.sem_inc(rows_ready[q], 1)
            for q in range(3):
                act.sem_inc(rows_free[q], 1)
            with act.Fori(0, NITER) as i:
                for b in range(2):
                    act.wait_ge(loaded[b], (i + 1) * (16 * LOADS))
                    act.wait_ge(mm_done[2 * b + 1], i + 1)
                    act.activation(msg[b][:, :, D:2 * D], feat[b][:].rearrange("p (u d) -> p u d", d=D),
                                   ACT.Sigmoid).then_inc(sig_done[b], 1)
                    for half in range(2):
                        q = 2 * b + half
                        act.wait_ge(mm_done[q], i + 2)
                        act.wait_ge(rows_free[q], i + 1)
                        act.copy(rows[q][:], ps[q][:]).then_inc(rows_ready[q], 1)

        @block.tensor
        def _(pe):
            for q in range(4):
                pe.sem_inc(mm_done[q], 1)
            with pe.Fori(0, NITER) as i:
                for q in range(4):
                    b, c = q // 2, QUAD * (q % 2)
                    pe.wait_ge(mul_done[q], i + 2)
                    pe.wait_ge(rows_ready[q], i + 1)
                    for u in range(QUAD):
                        for s, lo in (("dst", 0), ("src", D)):
                            mm = pe.matmul(ps[q][:, side[s], u, :], eq[s][b][:, c + u, :],
                                           msg[b][:, c + u, lo:lo + 2 * D], start=True, stop=True)
                    mm.then_inc(mm_done[q], 1)


def l0_nodes(k, t):
    nc = k.nc
    loaded, var_ready, std_ready, dve_step, stored, done = (
        k.sem("l0n_loaded"), k.sem("l0n_var"), k.sem("l0n_std"), k.sem("l0n_dve"), k.sem("l0n_stored"), k.sem("l0n_done"))
    with ExitStack() as ctx:
        a = k.sb("l0n_a", [P, NB, 2 * D], F32, ctx)
        b = k.sb("l0n_b", [P, NB, 2 * D], F32, ctx)
        c, q, h, st = (k.sb("l0n_c", [P, NB, D], F32, ctx), k.sb("l0n_q", [P, NB, D], F32, ctx),
                       k.sb("l0n_h", [P, NB, D], F32, ctx), k.sb("l0n_st", [P, 4, NB], F32, ctx))
        block = ctx.enter_context(nc.Block())

        @block.sync
        def _(sp):
            sp.dma_start(a[:], rows_of(t.l0_dst)).then_inc(loaded, 16)
            sp.dma_start(b[:], rows_of(t.l0_src)).then_inc(loaded, 16)
            sp.wait_ge(done, 1)
            sp.dma_start(rows_of(t.x1), t.x[:]).then_inc(stored, 16)
            sp.wait_ge(stored, 16)

        @block.scalar
        def _(act):
            for n in (1, 2):
                std_of(act, st, var_ready, std_ready, n)

        @block.vector
        def _(dve):
            step = chained(dve_step)
            dve.wait_ge(loaded, 32)
            step(dve, dve.tensor_tensor(c[:], a[:, :, D:2 * D], b[:, :, 0:D], ALU.add))
            step(dve, dve.tensor_scalar(c[:], c[:], 1e-7, None, ALU.add))
            step(dve, dve.reciprocal(c[:], c[:]))
            step(dve, dve.tensor_tensor(q[:], a[:, :, 0:D], b[:, :, D:2 * D], ALU.add))
            step(dve, dve.tensor_tensor(q[:], q[:], c[:], ALU.mult))
            step(dve, dve.tensor_tensor(h[:], q[:], t.h1[:], ALU.add))
            layer_norm(dve, step, h[:], h[:], c[:], q[:], st, var_ready, std_ready, 1)
            step(dve, dve.scalar_tensor_tensor(out=h[:], in0=h[:], scalar=0.0, in1=t.x[:], op0=ALU.max, op1=ALU.add))
            step(dve, dve.tensor_tensor(h[:], h[:], t.x[:], ALU.add))
            layer_norm(dve, step, h[:], t.x[:], c[:], q[:], st, var_ready, std_ready, 2)
            dve.sem_inc(done, 1)


def l1_edges(k, t):
    nc, ins = k.nc, k.ins
    loaded, tick, sp_tick = k.sems("l1_loaded", 2), k.sem("l1_tick"), k.sem("l1_sp_tick")
    wts, wts_done = k.sem("l1_weights"), k.sem("l1_weights_done")
    gathered, dots_done, comps_done = k.sems("l1_gathered", 4), k.sems("l1_dots", 4), k.sems("l1_comps", 4)
    turned, hid_done, turn_copied, relu_done = k.sem("l1_turned"), k.sem("l1_hid"), k.sem("l1_turn_copied"), k.sem("l1_relu")
    g_done, prod_done, sum_done = k.sem("l1_g"), k.sem("l1_prod"), k.sem("l1_sum")
    tanh_done, msg_done = k.sem("l1_tanh"), k.sem("l1_msg")
    mm_done, rows_ready, rows_free = k.sems("l1_mm", 4), k.sems("l1_rows", 4), k.sems("l1_rows_free", 4)
    eq_done, added, dve_step = k.sems("l1_eq", 2), k.sems("l1_added", 2), k.sem("l1_dve")
    LOADS = 4
    M = 6
    HALF = M * MOUT * MUL // 2
    Q_STEPS = 4
    with ExitStack() as ctx:
        idx = {s: [k.sb(f"l1_{s}_idx{b}", [P, TILES], I32, ctx) for b in range(2)] for s in ("dst", "src")}
        row = [k.sb(f"l1_row{b}", [P, GROUP], I32, ctx) for b in range(2)]
        emb = [k.sb(f"l1_emb{b}", [10, GROUP], F32, ctx) for b in range(2)]
        eq = [k.sb(f"l1_eq{b}", [P, TILES, P], F32, ctx) for b in range(2)]
        to = [k.sb(f"l1_to{b}", [P, TILES], I32, ctx) for b in range(2)]
        w1 = k.sb("l1_w1", [10, MUL], F32, ctx)
        wa = k.sb("l1_wa", [FEAT, M, MOUT, MUL], F32, ctx)
        wb = k.sb("l1_wb", [FEAT, M, MOUT, MUL], F32, ctx)
        xg = [k.sb(f"l1_xg{q}", [P, QUAD, 2, D], F32, ctx) for q in range(4)]
        pr = k.sb("l1_pr", [P, QUAD, 2, 8, 3], F32, ctx)
        feat = [k.sb(f"l1_feat{i}", [P, QUAD, 2, 40], F32, ctx) for i in range(2)]
        featT = [k.sb(f"l1_featT{i}", [FEAT, QUAD * P], F32, ctx) for i in range(2)]
        hid = [k.sb(f"l1_hid{i}", [P, QUAD, MUL], F32, ctx) for i in range(2)]
        prod = [k.sb(f"l1_prod{i}", [P, 2, HALF // MUL, MUL], F32, ctx) for i in range(QUAD)]
        out = [k.sb(f"l1_out{i}", [P, QUAD, M, MOUT], F32, ctx) for i in range(2)]
        th = [k.sb(f"l1_th{i}", [P, QUAD, 2 * MOUT], F32, ctx) for i in range(2)]
        gt = k.sb("l1_gt", [P, QUAD, 8], F32, ctx)
        vk = k.sb("l1_vk", [P, QUAD, 8, 3], F32, ctx)
        msg = [k.sb(f"l1_msg{i}", [P, QUAD, D], F32, ctx) for i in range(2)]
        rows = [k.sb(f"l1_rows{q}", [P, QUAD, D], F32, ctx) for q in range(4)]
        p_turn, p_hid, p_sum = (k.ps(f"l1_p{n}", ctx) for n in ("turn", "hid", "sum"))
        p_g = [k.ps(f"l1_pg{i}", ctx, (P, 2, 512)) for i in range(2)]
        block = ctx.enter_context(nc.Block())
        idx_d = {s: ins[f"{s}_idx"].rearrange("(g p u) -> g p u", p=P, u=TILES) for s in ("dst", "src")}
        row_d = ins["dst_idx"].rearrange("(g n) -> g n", n=GROUP)
        w2_d = ins["L1_W2"]
        parts = []
        for s in range(2):
            for kind, m, i in ((0, 0, 0), (1, 0, 1), (0, 1, 2), (1, 1, 3), (0, 2, 4)):
                parts.append((wa, 40 * s + 8 * kind, m, i, 8 * s))
            parts.append((wb, 40 * s + 8, 2, 6, 8 * s))
            for c in range(3):
                parts.append((wa, 40 * s + 16 + 8 * c, 3 + c, 5, 8 * s))
                parts.append((wb, 40 * s + 16 + 8 * c, 3 + c, 6, 8 * s))

        @block.sync
        def _(sp):
            def load(g, b):
                for s in ("src", "dst"):
                    sp.dma_start(idx[s][b][:], idx_d[s][g]).then_inc(loaded[b], 16)
                sp.dma_start(row[b][:], row_d[g].partition_broadcast(P)).then_inc(loaded[b], 16)
                sp.dma_start(emb[b][:], ins["embT"][g]).then_inc(loaded[b], 16)

            load(0, 0)
            load(1, 1)
            sp.dma_start(w1[:], ins["L1_W1"]).then_inc(wts, 16)
            sp.wait_ge(wts_done, 2)
            for target, r, m, i, u in parts:
                sp.dma_start(target[r:r + 8, m, :, :], w2_d[i, u:u + 8]).then_inc(wts, 16)
            with sp.Fori(0, NITER) as i:
                for b in range(2):
                    sp.wait_ge(gathered[2 * b], (i + 1) * (32 * QUAD))
                    sp.wait_ge(gathered[2 * b + 1], (i + 1) * (32 * QUAD))
                    sp.wait_ge(eq_done[b], i + 1)
                    waited(sp, sp_tick)
                    sp.wait_ge(hid_done, i * 4 + (2 * b + 2))
                    waited(sp, sp_tick)
                    load(i * 2 + (2 + b), b)
            for b in range(2):
                sp.wait_ge(loaded[b], 16 * LOADS * (NITER + 1))

        @block.gpsimd
        def _(pool):
            def gather(q, u):
                b, c = q // 2, QUAD * (q % 2) + u
                for s, at in (("src", 0), ("dst", 1)):
                    pool.indirect_dma_start(
                        out=xg[q][:, u, at, :], out_offset=None, in_=t.x1[:],
                        in_offset=bass.IndirectOffsetOnAxis(ap=idx[s][b][:, c:c + 1], axis=0)).then_inc(gathered[q], 16)

            def add(q, u):
                b, c = q // 2, QUAD * (q % 2) + u
                pool.indirect_dma_start(
                    out=t.l1_dst[u % 2][:], out_offset=bass.IndirectOffsetOnAxis(ap=to[b][:, c:c + 1], axis=0),
                    in_=rows[q][:, u, :], in_offset=None, compute_op=ALU.add).then_inc(added[u % 2], 16)

            for n in range(2):
                pool.dma_start(rows_of(t.l1_dst[n]), blank(t.zero, D)).then_inc(added[n], 16)
            pool.wait_ge(loaded[0], 16 * LOADS)
            for q in range(2):
                for u in range(QUAD):
                    gather(q, u)
            with pool.Fori(0, NITER) as i:
                for q in range(4):
                    ahead = (q + 2) % 4
                    pool.wait_ge(loaded[ahead // 2], (i + (2 if q >= 2 else 1)) * (16 * LOADS))
                    pool.wait_ge(dots_done[ahead], i + (2 if q >= 2 else 1))
                    pool.wait_ge(comps_done[ahead], i + (2 if q >= 2 else 1))
                    waited(pool, tick)
                    for u in range(QUAD):
                        gather(ahead, u)
                    pool.wait_ge(rows_ready[q], i + 2)
                    for u in range(QUAD):
                        pool.wait_ge(added[u % 2], (i * (2 * QUAD) + (q * (QUAD // 2) + u // 2 + 1)) * 16)
                        if u == 1:
                            pool.sem_inc(rows_free[(q - 1) % 4], 1)
                        else:
                            waited(pool, tick)
                        add(q, u)
            for n in range(2):
                pool.wait_ge(added[n], 16 * (NG * TILES // 2 + 1))
            for q in range(2):
                pool.wait_ge(gathered[q], 32 * QUAD * (NITER + 1))

        @block.vector
        def _(dve):
            step = chained(wts_done)
            step(dve, dve.memset(wa[:], 0.0))
            step(dve, dve.memset(wb[:], 0.0))
            dve.wait_ge(wts, 16 * (len(parts) + 1))
            step(dve, dve.tensor_scalar(wb[:, 2], wb[:, 2], 1.5 ** 0.5, None, ALU.mult))
            step(dve, dve.tensor_scalar(wb[:, 3:M], wb[:, 3:M], -(1.5 ** 0.5) / 3.0, None, ALU.mult))
            step(dve, dve.tensor_scalar(wa[:, 3:M], wa[:, 3:M], INV_SQRT3, None, ALU.mult))
            step(dve, dve.tensor_tensor(wa[:, 2:M], wa[:, 2:M], wb[:, 2:M], ALU.add))
            step(dve, dve.tensor_scalar(wa[:, 0:2], wa[:, 0:2], PW_S, None, ALU.mult))
            step(dve, dve.tensor_scalar(wa[:, 2:M], wa[:, 2:M], PW_V, None, ALU.mult))
            for q in range(4):
                dve.sem_inc(dots_done[q], 1)

            def dots(q, nth, g, turns, step):
                b, c = q // 2, QUAD * (q % 2)
                f = feat[nth % 2][:].rearrange("p t s f -> p (t s) f")
                dve.wait_ge(gathered[q], turns)
                nv = t.nvec[:, g, :].rearrange("p (u i) -> p u i", i=3)[:, c:c + QUAD, :]
                for s in range(2):
                    ins_ = dve.tensor_tensor(pr[:, :, s, :, :], xg[q][:, :, s, 8:D].rearrange("p t (u i) -> p t u i", i=3),
                                             over(nv.unsqueeze(2), [P, QUAD, 8, 3]), ALU.mult)
                step(ins_)
                dve.tensor_reduce(f[:, :, 8:16], pr[:].rearrange("p t s u i -> p (t s) u i"), AX.X,
                                  ALU.add).then_inc(dots_done[q], 1)

            first = [0]

            def first_step(ins_):
                first[0] += 1
                ins_.then_inc(dve_step, 1)
                dve.wait_ge(dve_step, first[0])

            dots(0, 0, 0, 32 * QUAD, first_step)
            with dve.Fori(0, NITER) as i:
                for q in range(4):
                    b, half, c = q // 2, q % 2, QUAD * (q % 2)
                    g = i * 2 + b
                    count = [1]

                    def step(ins_):
                        count[0] += 1
                        ins_.then_inc(dve_step, 1)
                        dve.wait_ge(dve_step, i * (4 * Q_STEPS) + (q * Q_STEPS + count[0]))

                    def multiply(u):
                        n = i * (4 * QUAD) + (q * QUAD + u)
                        dve.wait_ge(g_done, n + 1)
                        dve.tensor_tensor(prod[u][:], p_g[u % 2][:, :, 0:HALF].rearrange("p a (x c) -> p a x c", c=MUL),
                                          over(hid[q % 2][:, u, :].unsqueeze(1).unsqueeze(1), [P, 2, HALF // MUL, MUL]),
                                          ALU.mult).then_inc(prod_done, 1)

                    def contract(u):
                        n = i * (4 * QUAD) + (q * QUAD + u)
                        dve.wait_ge(prod_done, n + 1)
                        dve.tensor_reduce(out[q % 2][:, u].rearrange("p m w -> p (m w)"),
                                          prod[u][:].rearrange("p a x c -> p (a x) c"), AX.X, ALU.add).then_inc(sum_done, 1)

                    dve.wait_ge(relu_done, i * 4 + (q + 1))
                    multiply(0)
                    dots((q + 1) % 4, q + 1, i * 2 + (q + 1) // 2, (i + (2 if q == 3 else 1)) * (32 * QUAD), step)
                    multiply(1)
                    contract(0)
                    if half == 0:
                        dve.wait_ge(loaded[b], (i + 1) * (16 * LOADS))
                        dve.wait_ge(mm_done[2 * b + 1], i + 1)
                        dve.wait_ge(rows_free[2 * b + 1], i + 1)
                        dve.tensor_copy(to[b][:], t.to_dst[:, g, :])
                        dve.tensor_tensor(eq[b][:], row[b][:].rearrange("p (e u) -> p u e", u=TILES),
                                          over(idx["dst"][b][:].unsqueeze(2), [P, TILES, P]),
                                          ALU.is_equal).then_inc(eq_done[b], 1)
                    multiply(2)
                    contract(1)
                    multiply(3)
                    contract(2)
                    contract(3)
                    w = over(t.wgain[:, g, c:c + QUAD].unsqueeze(2), [P, QUAD, 8])
                    n3 = t.nvec[:, g, :].rearrange("p (u i) -> p u i", i=3)[:, c:c + QUAD, :]
                    o = out[q % 2]
                    dve.wait_ge(sum_done, i * (4 * QUAD) + (q + 1) * QUAD)
                    step(dve.tensor_tensor(vk[:], over(o[:, :, 2, :].unsqueeze(3), [P, QUAD, 8, 3]),
                                           over(n3.unsqueeze(2), [P, QUAD, 8, 3]), ALU.mult))
                    step(dve.tensor_tensor(vk[:], vk[:], o[:, :, 3:M, :].rearrange("p t k w -> p t w k"), ALU.add))
                    dve.wait_ge(tanh_done, i * 4 + (q + 1))
                    dve.wait_ge(mm_done[(q - 2) % 4], i + (1 if q < 2 else 2))
                    dve.tensor_tensor(msg[q % 2][:, :, 0:8], th[q % 2][:, :, 0:8], w, ALU.mult)
                    step(dve.tensor_tensor(gt[:], th[q % 2][:, :, 8:16], w, ALU.mult))
                    dve.tensor_tensor(msg[q % 2][:, :, 8:D].rearrange("p t (w k) -> p t w k", k=3), vk[:],
                                      over(gt[:].unsqueeze(3), [P, QUAD, 8, 3]), ALU.mult).then_inc(msg_done, 1)
                    assert count[0] == Q_STEPS + 1

        @block.scalar
        def _(act):
            for q in range(4):
                act.sem_inc(rows_ready[q], 1)
                act.sem_inc(comps_done[q], 1)
            for q in range(3):
                act.sem_inc(rows_free[q], 1)

            def components(q, nth, turns):
                act.wait_ge(gathered[q], turns)
                x = xg[q][:].rearrange("p t s d -> p (t s) d")
                f = feat[nth % 2][:].rearrange("p t s f -> p (t s) f")
                act.copy(f[:, :, 0:8], x[:, :, 0:8])
                act.copy(f[:, :, 16:40].rearrange("p a (i u) -> p a i u", i=3),
                         x[:, :, 8:D].rearrange("p a (u i) -> p a i u", i=3)).then_inc(comps_done[q], 1)

            def turn(nth, n):
                act.wait_ge(hid_done, n)
                act.activation(hid[nth % 2][:].rearrange("p t c -> p (t c)"), p_hid[:, 0:QUAD * MUL], ACT.Relu,
                               scale=HID_SCALE).then_inc(relu_done, 1)
                act.wait_ge(turned, n)
                act.copy(featT[nth % 2][:], p_turn[0:FEAT, :]).then_inc(turn_copied, 1)

            components(0, 0, 32 * QUAD)
            turn(0, 1)
            with act.Fori(0, NITER) as i:
                for q in range(4):
                    components((q + 1) % 4, q + 1, (i + (2 if q == 3 else 1)) * (32 * QUAD))
                    turn(q + 1, i * 4 + (q + 2))
                    act.wait_ge(sum_done, i * (4 * QUAD) + (q + 1) * QUAD)
                    act.activation(th[q % 2][:], out[q % 2][:, :, 0:2, :].rearrange("p t m w -> p t (m w)"),
                                   ACT.Tanh).then_inc(tanh_done, 1)
                    act.wait_ge(mm_done[q], i + 2)
                    act.wait_ge(rows_free[q], i + 1)
                    act.copy(rows[q][:], p_sum[:, 0:QUAD * D].rearrange("p (t d) -> p t d", d=D)).then_inc(rows_ready[q], 1)

        @block.tensor
        def _(pe):
            for q in range(4):
                pe.sem_inc(mm_done[q], 1)
            pe.wait_ge(wts_done, 8)

            def turn(q, nth, feat_turn):
                b, c = q // 2, q % 2
                for u in range(QUAD):
                    mm = pe.matmul(p_hid[:, u * MUL:(u + 1) * MUL], emb[b][:, (c * QUAD + u) * P:(c * QUAD + u + 1) * P],
                                   w1[:], start=True, stop=True)
                mm.then_inc(hid_done, 1)
                pe.wait_ge(dots_done[q], feat_turn)
                pe.wait_ge(comps_done[q], feat_turn)
                for u in range(QUAD):
                    mm = pe.transpose(p_turn[0:FEAT, u * P:(u + 1) * P],
                                      feat[nth % 2][:, u].rearrange("p s f -> p (s f)"), t.ident[:])
                mm.then_inc(turned, 1)

            def products(nth, u):
                for h in range(2):
                    mm = pe.matmul(p_g[u % 2][:, h, 0:HALF], featT[nth % 2][:, u * P:(u + 1) * P],
                                   wa[:, 3 * h:3 * h + 3].rearrange("k m w c -> k (m w c)"), start=True, stop=True)
                mm.then_inc(g_done, 1)

            pe.wait_ge(loaded[0], 16 * LOADS)
            turn(0, 0, 2)
            pe.wait_ge(turn_copied, 1)
            products(0, 0)
            products(0, 1)
            with pe.Fori(0, NITER) as i:
                for q in range(4):
                    b, c = q // 2, QUAD * (q % 2)
                    n = i * (4 * QUAD) + q * QUAD
                    pe.wait_ge(prod_done, n + 1)
                    products(q, 2)
                    if q % 2 == 1:
                        pe.wait_ge(loaded[(b + 1) % 2], (i + (2 if q == 3 else 1)) * (16 * LOADS))
                    turn((q + 1) % 4, q + 1, i + (3 if q == 3 else 2))
                    pe.wait_ge(prod_done, n + 2)
                    products(q, 3)
                    pe.wait_ge(turn_copied, i * 4 + (q + 2))
                    for u in range(2):
                        pe.wait_ge(prod_done, n + (3 + u))
                        products(q + 1, u)
                    pe.wait_ge(msg_done, i * 4 + (q + 1))
                    pe.wait_ge(rows_ready[(q - 1) % 4], i + (1 if q == 0 else 2))
                    for u in range(QUAD):
                        mm = pe.matmul(p_sum[:, u * D:(u + 1) * D], eq[b][:, c + u, :], msg[q % 2][:, u, :],
                                       start=True, stop=True)
                    mm.then_inc(mm_done[q], 1)


def residual_nodes(k, tag, t, load, combine, out):
    nc = k.nc
    loaded, var_ready, std_ready, dve_step, stored, done = (
        k.sem(f"{tag}_loaded"), k.sem(f"{tag}_var"), k.sem(f"{tag}_std"), k.sem(f"{tag}_dve"), k.sem(f"{tag}_stored"),
        k.sem(f"{tag}_done"))
    with ExitStack() as ctx:
        sums = [k.sb(f"{tag}_s{n}", [P, NB, table.shape[1]], F32, ctx) for n, table in enumerate(load)]
        c, q, st = (k.sb(f"{tag}_c", [P, NB, D], F32, ctx), k.sb(f"{tag}_q", [P, NB, D], F32, ctx),
                    k.sb(f"{tag}_st", [P, 4, NB], F32, ctx))
        block = ctx.enter_context(nc.Block())

        @block.sync
        def _(sp):
            for tile, table in zip(sums, load):
                sp.dma_start(tile[:], rows_of(table)).then_inc(loaded, 16)
            if out is not None:
                sp.wait_ge(done, 1)
                sp.dma_start(rows_of(out), t.x[:]).then_inc(stored, 16)
                sp.wait_ge(stored, 16)

        @block.scalar
        def _(act):
            std_of(act, st, var_ready, std_ready, 1)

        @block.vector
        def _(dve):
            step = chained(dve_step)
            dve.wait_ge(loaded, 16 * len(load))
            combine(dve, step, sums)
            step(dve, dve.tensor_tensor(t.x[:], t.x[:], sums[0][:, :, 0:D], ALU.add))
            layer_norm(dve, step, t.x[:], t.x[:], c[:], q[:], st, var_ready, std_ready, 1)
            dve.sem_inc(done, 1)


def l2_edges(k, t):
    nc, ins = k.nc, k.ins
    loaded, tick, sp_tick = k.sems("l2_loaded", 2), k.sem("l2_tick"), k.sem("l2_sp_tick")
    gathered, mul_done, mm_done = k.sems("l2_gathered", 4), k.sems("l2_mul", 4), k.sems("l2_mm", 4)
    rows_ready, rows_free, eq_done = k.sems("l2_rows", 4), k.sems("l2_rows_free", 4), k.sems("l2_eq", 2)
    added = k.sems("l2_added", 2)
    LOADS = 3
    W = D + 1
    with ExitStack() as ctx:
        idx = {s: [k.sb(f"l2_{s}_idx{b}", [P, TILES], I32, ctx) for b in range(2)] for s in ("dst", "src")}
        row = [k.sb(f"l2_row{b}", [P, GROUP], I32, ctx) for b in range(2)]
        eq = [k.sb(f"l2_eq{b}", [P, TILES, P], F32, ctx) for b in range(2)]
        to = [k.sb(f"l2_to{b}", [P, TILES], I32, ctx) for b in range(2)]
        xg = [k.sb(f"l2_xg{q}", [P, QUAD, D], F32, ctx) for q in range(4)]
        msg = [k.sb(f"l2_msg{q}", [P, QUAD, W], F32, ctx) for q in range(4)]
        rows = [k.sb(f"l2_rows{q}", [P, QUAD, W], F32, ctx) for q in range(4)]
        ps = [k.ps(f"l2_ps{q}", ctx) for q in range(4)]
        block = ctx.enter_context(nc.Block())
        idx_d = {s: ins[f"{s}_idx"].rearrange("(g p u) -> g p u", p=P, u=TILES) for s in ("dst", "src")}
        row_d = ins["src_idx"].rearrange("(g n) -> g n", n=GROUP)

        @block.sync
        def _(sp):
            def load(g, b):
                for s in ("src", "dst"):
                    sp.dma_start(idx[s][b][:], idx_d[s][g]).then_inc(loaded[b], 16)
                sp.dma_start(row[b][:], row_d[g].partition_broadcast(P)).then_inc(loaded[b], 16)

            load(0, 0)
            load(1, 1)
            with sp.Fori(0, NITER) as i:
                for b in range(2):
                    sp.wait_ge(gathered[2 * b], (i + 1) * (16 * QUAD))
                    sp.wait_ge(gathered[2 * b + 1], (i + 1) * (16 * QUAD))
                    sp.wait_ge(eq_done[b], i + 1)
                    waited(sp, sp_tick)
                    load(i * 2 + (2 + b), b)
            for b in range(2):
                sp.wait_ge(loaded[b], 16 * LOADS * (NITER + 1))

        @block.gpsimd
        def _(pool):
            def gather(q, u):
                c = QUAD * (q % 2) + u
                pool.indirect_dma_start(
                    out=xg[q][:, u, :], out_offset=None, in_=t.x2[:],
                    in_offset=bass.IndirectOffsetOnAxis(ap=idx["dst"][q // 2][:, c:c + 1], axis=0)).then_inc(gathered[q], 16)

            for n in range(2):
                pool.dma_start(rows_of(t.l2_src[n]), blank(t.zero, W)).then_inc(added[n], 16)
            pool.wait_ge(loaded[0], 16 * LOADS)
            for q in range(2):
                for u in range(QUAD):
                    gather(q, u)
            with pool.Fori(0, NITER) as i:
                for q in range(4):
                    ahead = (q + 2) % 4
                    pool.wait_ge(loaded[ahead // 2], (i + (2 if q >= 2 else 1)) * (16 * LOADS))
                    pool.wait_ge(mul_done[ahead], i + (2 if q >= 2 else 1))
                    waited(pool, tick)
                    for u in range(QUAD):
                        gather(ahead, u)
                        if u == 0:
                            pool.wait_ge(rows_ready[q], i + 2)
                        n, c = u % 2, QUAD * (q % 2) + u
                        pool.wait_ge(added[n], (i * (2 * QUAD) + (q * (QUAD // 2) + u // 2 + 1)) * 16)
                        if u == 1:
                            pool.sem_inc(rows_free[(q - 1) % 4], 1)
                        else:
                            waited(pool, tick)
                        pool.indirect_dma_start(
                            out=t.l2_src[n][:], out_offset=bass.IndirectOffsetOnAxis(ap=to[q // 2][:, c:c + 1], axis=0),
                            in_=rows[q][:, u, :], in_offset=None, compute_op=ALU.add).then_inc(added[n], 16)
            for n in range(2):
                pool.wait_ge(added[n], 16 * (NG * TILES // 2 + 1))
            for q in range(2):
                pool.wait_ge(gathered[q], 16 * QUAD * (NITER + 1))

        @block.vector
        def _(dve):
            for q in range(4):
                dve.sem_inc(mul_done[q], 1)
            with dve.Fori(0, NITER) as i:
                for b in range(2):
                    g = i * 2 + b
                    dve.wait_ge(loaded[b], (i + 1) * (16 * LOADS))
                    dve.wait_ge(mm_done[2 * b + 1], i + 1)
                    dve.wait_ge(rows_free[2 * b + 1], i + 1)
                    dve.tensor_copy(to[b][:], t.to_src[:, g, :])
                    dve.tensor_tensor(eq[b][:], row[b][:].rearrange("p (e u) -> p u e", u=TILES),
                                      over(idx["src"][b][:].unsqueeze(2), [P, TILES, P]), ALU.is_equal).then_inc(eq_done[b], 1)
                    for half in range(2):
                        q, c = 2 * b + half, QUAD * half
                        dve.wait_ge(gathered[q], (i + 1) * (16 * QUAD))
                        dve.wait_ge(mm_done[q], i + 1)
                        dve.tensor_copy(msg[q][:, :, D:W], t.wgt[:, g, c:c + QUAD].unsqueeze(2))
                        dve.tensor_tensor(msg[q][:, :, 0:D], xg[q][:],
                                          over(t.wgt[:, g, c:c + QUAD].unsqueeze(2), [P, QUAD, D]),
                                          ALU.mult).then_inc(mul_done[q], 1)

        @block.scalar
        def _(act):
            for q in range(4):
                act.sem_inc(rows_ready[q], 1)
            for q in range(3):
                act.sem_inc(rows_free[q], 1)
            with act.Fori(0, NITER) as i:
                for q in range(4):
                    act.wait_ge(mm_done[q], i + 2)
                    act.wait_ge(rows_free[q], i + 1)
                    act.copy(rows[q][:], ps[q][:, 0:QUAD * W].rearrange("p (u w) -> p u w", w=W)).then_inc(rows_ready[q], 1)

        @block.tensor
        def _(pe):
            for q in range(4):
                pe.sem_inc(mm_done[q], 1)
            with pe.Fori(0, NITER) as i:
                for q in range(4):
                    pe.wait_ge(mul_done[q], i + 2)
                    pe.wait_ge(rows_ready[q], i + 1)
                    for u in range(QUAD):
                        mm = pe.matmul(ps[q][:, u * W:(u + 1) * W], eq[q // 2][:, QUAD * (q % 2) + u, :],
                                       msg[q][:, u, :], start=True, stop=True)
                    mm.then_inc(mm_done[q], 1)


def turn_nodes(k, tag, t, x, xT):
    nc = k.nc
    picked, turned, copied = k.sem(f"{tag}_picked"), k.sem(f"{tag}_turned"), k.sem(f"{tag}_copied")
    with ExitStack() as ctx:
        part = k.sb(f"{tag}_part", [P, CH, D], F32, ctx)
        ps = k.ps(f"{tag}_ps", ctx)
        block = ctx.enter_context(nc.Block())

        @block.vector
        def _(dve):
            with dve.Fori(0, NB // CH) as c:
                dve.wait_ge(turned, c + 1)
                dve.tensor_copy(part[:], x[:, bass.ds(c * CH, CH), :]).then_inc(picked, 1)

        @block.tensor
        def _(pe):
            pe.sem_inc(turned, 1)
            with pe.Fori(0, NB // CH) as c:
                pe.wait_ge(picked, c + 1)
                pe.wait_ge(copied, c + 1)
                for b in range(CH):
                    mm = pe.transpose(ps[0:D, b * P:(b + 1) * P], part[:, b, :], t.ident[:])
                mm.then_inc(turned, 1)

        @block.scalar
        def _(act):
            act.sem_inc(copied, 1)
            with act.Fori(0, NB // CH) as c:
                act.wait_ge(turned, c + 2)
                act.copy(xT[:, bass.ds(c * (CH * P), CH * P)], ps[0:D, 0:CH * P]).then_inc(copied, 1)


def l3_scores(k, t, xT, a_all):
    nc, ins = k.nc, k.ins
    picked = k.sem("l3s_picked")
    loaded, dve_step, mm_done, copied, stored, done = (
        k.sem("l3s_loaded"), k.sem("l3s_dve"), k.sem("l3s_mm"), k.sem("l3s_copied"), k.sem("l3s_stored"), k.sem("l3s_done"))
    with ExitStack() as ctx:
        wg = k.sb("l3s_wg", [D, HEADS, D], F32, ctx)
        att = k.sb("l3s_att", [D, 2, HEADS, D], F32, ctx)
        va = k.sb("l3s_va", [D, 2, HEADS], F32, ctx)
        part = k.sb("l3s_part", [D, CH * P], F32, ctx)
        x_a = k.sb("l3s_x_a", [P, NB, D + HEADS], F32, ctx)
        ps = k.ps("l3s_ps", ctx)
        block = ctx.enter_context(nc.Block())

        @block.sync
        def _(sp):
            sp.dma_start(wg[:], ins["L3_W_gat"].rearrange("d (h c) -> d h c", c=D)).then_inc(loaded, 16)
            for n, name in enumerate(("att_src", "att_dst")):
                sp.dma_start(att[:, n].rearrange("d h c -> d (h c)"),
                             ins[f"L3_{name}"].rearrange("h c -> (h c)").partition_broadcast(D)).then_inc(loaded, 16)
            sp.wait_ge(done, 1)
            sp.dma_start(rows_of(t.x3), x_a[:]).then_inc(stored, 16)
            sp.wait_ge(stored, 16)

        @block.vector
        def _(dve):
            step = chained(dve_step)
            dve.wait_ge(loaded, 48)
            step(dve, dve.tensor_tensor(att[:], att[:], over(wg[:].unsqueeze(1), [D, 2, HEADS, D]), ALU.mult))
            step(dve, dve.tensor_reduce(va[:], att[:], AX.X, ALU.add))
            dve.sem_inc(copied, 1)
            with dve.Fori(0, NB // CH) as c:
                dve.wait_ge(mm_done, c + 2)
                dve.tensor_copy(a_all[:, bass.ds(c * CH, CH), :],
                                ps[:, 0:CH * 16].rearrange("p (b a) -> p b a", b=CH)).then_inc(copied, 1)
            dve.wait_ge(copied, NB // CH + 1)
            step(dve, dve.tensor_copy(x_a[:, :, 0:D], t.x[:]))
            step(dve, dve.tensor_copy(x_a[:, :, D:D + HEADS], a_all[:, :, 0:HEADS]))
            dve.sem_inc(done, 1)

        @block.scalar
        def _(act):
            act.sem_inc(mm_done, 1)
            with act.Fori(0, NB // CH) as c:
                act.wait_ge(mm_done, c + 1)
                act.copy(part[:], xT[:, bass.ds(c * (CH * P), CH * P)]).then_inc(picked, 1)

        @block.tensor
        def _(pe):
            pe.wait_ge(dve_step, 2)
            with pe.Fori(0, NB // CH) as c:
                pe.wait_ge(copied, c + 1)
                pe.wait_ge(picked, c + 1)
                for b in range(CH):
                    mm = pe.matmul(ps[:, b * 16:(b + 1) * 16], part[:, b * P:(b + 1) * P],
                                   va[:].rearrange("d s h -> d (s h)"), start=True, stop=True)
                mm.then_inc(mm_done, 1)


def l3_max(k, t):
    nc, ins = k.nc, k.ins
    loaded, tick, sp_tick = k.sems("l3m_loaded", 2), k.sem("l3m_tick"), k.sem("l3m_sp_tick")
    gathered, kept, spread = k.sems("l3m_gathered", 4), k.sems("l3m_kept", 4), k.sems("l3m_spread", 4)
    read, put = k.sem("l3m_read"), k.sems("l3m_put", QUAD)
    eq_done, diag_done, mm_done, red_done, new_done = (
        k.sems("l3m_eq", 2), k.sem("l3m_diag"), k.sem("l3m_mm"), k.sem("l3m_red"), k.sem("l3m_new"))
    consts, dve_step = k.sem("l3m_consts"), k.sem("l3m_step")
    LOADS = 3
    W = D + HEADS
    with ExitStack() as ctx:
        idx = {s: [k.sb(f"l3m_{s}_idx{b}", [P, TILES], I32, ctx) for b in range(2)] for s in ("dst", "src")}
        row = [k.sb(f"l3m_row{b}", [P, GROUP], I32, ctx) for b in range(2)]
        neq = [k.sb(f"l3m_neq{b}", [P, TILES, P], BF16, ctx) for b in range(2)]
        to = [k.sb(f"l3m_to{b}", [P, TILES], I32, ctx) for b in range(2)]
        ones = k.sb("l3m_ones", [P, P], F32, ctx)
        low = k.sb("l3m_low", [P, P], BF16, ctx)
        xg = [k.sb(f"l3m_xg{q}", [P, QUAD, W], F32, ctx) for q in range(4)]
        diag = [k.sb(f"l3m_diag{n}", [P, HEADS, P], F32, ctx) for n in range(2)]
        red = k.sb("l3m_red", [P, QUAD, HEADS], F32, ctx)
        cur = k.sb("l3m_cur", [P, QUAD, HEADS], F32, ctx)
        new = k.sb("l3m_new", [P, QUAD, HEADS], F32, ctx)
        ps = [k.ps(f"l3m_ps{n}", ctx, (P, HEADS, P)) for n in range(2)]
        block = ctx.enter_context(nc.Block())
        idx_d = {s: ins[f"{s}_idx"].rearrange("(g p u) -> g p u", p=P, u=TILES) for s in ("dst", "src")}
        row_d = ins["dst_idx"].rearrange("(g n) -> g n", n=GROUP)

        @block.sync
        def _(sp):
            def load(g, b):
                for s in ("src", "dst"):
                    sp.dma_start(idx[s][b][:], idx_d[s][g]).then_inc(loaded[b], 16)
                sp.dma_start(row[b][:], row_d[g].partition_broadcast(P)).then_inc(loaded[b], 16)

            load(0, 0)
            load(1, 1)
            with sp.Fori(0, NITER) as i:
                for b in range(2):
                    sp.wait_ge(gathered[2 * b], (i + 1) * (16 * QUAD))
                    sp.wait_ge(gathered[2 * b + 1], (i + 1) * (16 * QUAD))
                    sp.wait_ge(eq_done[b], i + 1)
                    waited(sp, sp_tick)
                    load(i * 2 + (2 + b), b)
            for b in range(2):
                sp.wait_ge(loaded[b], 16 * LOADS * (NITER + 1))

        @block.gpsimd
        def _(pool):
            def gather(q, u):
                c = QUAD * (q % 2) + u
                pool.indirect_dma_start(
                    out=xg[q][:, u, :], out_offset=None, in_=t.x3[:],
                    in_offset=bass.IndirectOffsetOnAxis(ap=idx["src"][q // 2][:, c:c + 1], axis=0)).then_inc(gathered[q], 16)

            for u in range(QUAD):
                pool.dma_start(rows_of(t.l3_max[u]), blank(t.lowest, HEADS)).then_inc(put[u], 16)
            pool.wait_ge(loaded[0], 16 * LOADS)
            for q in range(2):
                for u in range(QUAD):
                    gather(q, u)
            with pool.Fori(0, NITER) as i:
                for q in range(4):
                    b, ahead = q // 2, (q + 2) % 4
                    pool.wait_ge(eq_done[b], i + 1)
                    for u in range(QUAD):
                        c = QUAD * (q % 2) + u
                        pool.wait_ge(put[u], (i * 4 + (q + 1)) * 16)
                        waited(pool, tick)
                        pool.indirect_dma_start(
                            out=cur[:, u, :], out_offset=None, in_=t.l3_max[u][:],
                            in_offset=bass.IndirectOffsetOnAxis(ap=to[b][:, c:c + 1], axis=0)).then_inc(read, 16)
                    pool.wait_ge(loaded[ahead // 2], (i + (2 if q >= 2 else 1)) * (16 * LOADS))
                    pool.wait_ge(spread[ahead], i + (2 if q >= 2 else 1))
                    pool.wait_ge(kept[ahead], i + (2 if q >= 2 else 1))
                    waited(pool, tick)
                    for u in range(QUAD):
                        gather(ahead, u)
                    pool.wait_ge(new_done, i * 4 + (q + 1))
                    waited(pool, tick)
                    for u in range(QUAD):
                        c = QUAD * (q % 2) + u
                        pool.indirect_dma_start(
                            out=t.l3_max[u][:], out_offset=bass.IndirectOffsetOnAxis(ap=to[b][:, c:c + 1], axis=0),
                            in_=new[:, u, :], in_offset=None).then_inc(put[u], 16)
            for u in range(QUAD):
                pool.wait_ge(put[u], 16 * (4 * NITER + 1))
            for q in range(2):
                pool.wait_ge(gathered[q], 16 * QUAD * (NITER + 1))

        @block.vector
        def _(dve):
            step = chained(consts)
            step(dve, dve.memset(ones[:], 1.0))
            step(dve, dve.tensor_scalar(low[:], t.ident[:], LOWEST, None, ALU.mult))
            for q in range(4):
                dve.sem_inc(spread[q], 1)
            dve.sem_inc(red_done, 2)
            with dve.Fori(0, NITER) as i:
                for q in range(4):
                    b = q // 2
                    if q % 2 == 0:
                        dve.wait_ge(loaded[b], (i + 1) * (16 * LOADS))
                        dve.wait_ge(mm_done, i * 16 + (q * QUAD + 2))
                        dve.tensor_copy(to[b][:], t.to_dst[:, i * 2 + b, :])
                        dve.tensor_tensor(neq[b][:], row[b][:].rearrange("p (e u) -> p u e", u=TILES),
                                          over(idx["dst"][b][:].unsqueeze(2), [P, TILES, P]),
                                          ALU.not_equal).then_inc(eq_done[b], 1)
                    dve.wait_ge(gathered[q], (i + 1) * (16 * QUAD))

                    def spread_out(u):
                        n = i * 16 + (q * QUAD + u)
                        dve.wait_ge(mm_done, n + 1)
                        ins_ = dve.tensor_tensor(diag[u % 2][:], over(t.ident[:].unsqueeze(1), [P, HEADS, P]),
                                                 over(xg[q][:, u, D:W].unsqueeze(2), [P, HEADS, P]), ALU.mult)
                        ins_.then_inc(diag_done, 1)

                    def reduce(u):
                        dve.wait_ge(mm_done, i * 16 + (q * QUAD + u + 3))
                        dve.tensor_reduce(red[:, u, :], ps[u % 2][:], AX.X, ALU.max).then_inc(red_done, 1)

                    spread_out(0)
                    spread_out(1)
                    for u in range(2, QUAD):
                        reduce(u - 2)
                        spread_out(u)
                    dve.wait_ge(diag_done, i * 16 + (q * QUAD + QUAD))
                    dve.sem_inc(spread[q], 1)
                    reduce(QUAD - 2)
                    reduce(QUAD - 1)
                    dve.wait_ge(red_done, i * 16 + (q * QUAD + QUAD + 2))
                    dve.wait_ge(read, (i * 4 + (q + 1)) * (16 * QUAD))
                    dve.tensor_tensor(new[:], cur[:], red[:], ALU.max).then_inc(new_done, 1)

        @block.scalar
        def _(act):
            for q in range(4):
                act.sem_inc(kept[q], 1)
            with act.Fori(0, NITER) as i:
                for q in range(4):
                    act.wait_ge(gathered[q], (i + 1) * (16 * QUAD))
                    act.copy(t.x_edge[:, bass.ds(i * 16 + q * QUAD, QUAD), :], xg[q][:]).then_inc(kept[q], 1)

        @block.tensor
        def _(pe):
            pe.wait_ge(consts, 2)
            pe.sem_inc(mm_done, 2)
            with pe.Fori(0, NITER) as i:
                for q in range(4):
                    for u in range(QUAD):
                        n = i * 16 + (q * QUAD + u)
                        pe.wait_ge(diag_done, n + 1)
                        pe.wait_ge(red_done, n + 1)
                        for h in range(0, HEADS, 4):
                            pe.matmul(ps[u % 2][:, h:h + 4, :], ones[:], diag[u % 2][:, h:h + 4, :],
                                      start=True, stop=False)
                            mm = pe.matmul(ps[u % 2][:, h:h + 4, :], neq[q // 2][:, QUAD * (q % 2) + u, :],
                                           over(low[:].unsqueeze(1), [P, 4, P]), start=False, stop=True)
                        mm.then_inc(mm_done, 1)


def l3_bounds(k, t, a_all, self_w):
    nc = k.nc
    loaded, dve_step, done, stored, exp_done = (
        k.sem("l3b_loaded"), k.sem("l3b_dve"), k.sem("l3b_done"), k.sem("l3b_stored"), k.sem("l3b_exp"))
    with ExitStack() as ctx:
        mx = [k.sb(f"l3b_mx{u}", [P, NB, HEADS], F32, ctx) for u in range(QUAD)]
        dm = k.sb("l3b_dm", [P, NB, 2 * HEADS], F32, ctx)
        block = ctx.enter_context(nc.Block())

        @block.sync
        def _(sp):
            for u in range(QUAD):
                sp.dma_start(mx[u][:], rows_of(t.l3_max[u])).then_inc(loaded, 16)
            sp.wait_ge(done, 1)
            sp.dma_start(rows_of(t.l3_dm), dm[:]).then_inc(stored, 16)
            sp.wait_ge(stored, 16)

        @block.vector
        def _(dve):
            step = chained(dve_step)
            dve.wait_ge(loaded, 16 * QUAD)
            step(dve, dve.tensor_tensor(mx[0][:], mx[0][:], mx[1][:], ALU.max))
            step(dve, dve.tensor_tensor(mx[2][:], mx[2][:], mx[3][:], ALU.max))
            step(dve, dve.tensor_tensor(mx[0][:], mx[0][:], mx[2][:], ALU.max))
            step(dve, dve.tensor_tensor(mx[0][:], mx[0][:], a_all[:, :, 0:HEADS], ALU.max))
            step(dve, dve.tensor_tensor(mx[0][:], mx[0][:], a_all[:, :, HEADS:2 * HEADS], ALU.add))
            step(dve, dve.tensor_copy(dm[:, :, 0:HEADS], a_all[:, :, HEADS:2 * HEADS]))
            step(dve, dve.scalar_tensor_tensor(out=dm[:, :, HEADS:2 * HEADS], in0=mx[0][:], scalar=0.2, in1=mx[0][:],
                                               op0=ALU.mult, op1=ALU.max))
            step(dve, dve.tensor_tensor(mx[1][:], a_all[:, :, 0:HEADS], a_all[:, :, HEADS:2 * HEADS], ALU.add))
            step(dve, dve.scalar_tensor_tensor(out=mx[1][:], in0=mx[1][:], scalar=0.2, in1=mx[1][:],
                                               op0=ALU.mult, op1=ALU.max))
            step(dve, dve.tensor_tensor(mx[1][:], mx[1][:], dm[:, :, HEADS:2 * HEADS], ALU.subtract))
            dve.sem_inc(done, 1)

        @block.scalar
        def _(act):
            act.wait_ge(done, 1)
            act.activation(self_w[:], mx[1][:], ACT.Exp).then_inc(exp_done, 1)
            act.wait_ge(exp_done, 1)


def l3_edges(k, t):
    nc, ins = k.nc, k.ins
    loaded, tick, sp_tick = k.sems("l3_loaded", 2), k.sem("l3_tick"), k.sem("l3_sp_tick")
    gathered, used, mm_done = k.sems("l3_gathered", 4), k.sems("l3_used", 4), k.sems("l3_mm", 4)
    rows_ready, rows_free, eq_done = k.sems("l3_rows", 4), k.sems("l3_rows_free", 4), k.sems("l3_eq", 2)
    exp_done, msg_done, dve_step = k.sem("l3_exp"), k.sem("l3_msg"), k.sem("l3_dve")
    added = k.sems("l3_added", 2)
    LOADS = 2
    W = HEADS * D + HEADS
    STEPS = 2
    with ExitStack() as ctx:
        idx = [k.sb(f"l3_idx{b}", [P, TILES], I32, ctx) for b in range(2)]
        row = [k.sb(f"l3_row{b}", [P, GROUP], I32, ctx) for b in range(2)]
        eq = [k.sb(f"l3_eq{b}", [P, TILES, P], F32, ctx) for b in range(2)]
        to = [k.sb(f"l3_to{b}", [P, TILES], I32, ctx) for b in range(2)]
        dm = [k.sb(f"l3_dm{q}", [P, QUAD, 2 * HEADS], F32, ctx) for q in range(4)]
        al = k.sb("l3_al", [P, QUAD, HEADS], F32, ctx)
        ea = k.sb("l3_ea", [P, QUAD, HEADS], F32, ctx)
        msg = [k.sb(f"l3_msg{n}", [P, QUAD, W], F32, ctx) for n in range(2)]
        rows = [k.sb(f"l3_rows{q}", [P, QUAD, W], F32, ctx) for q in range(4)]
        ps = [k.ps(f"l3_ps{n}", ctx, (P, QUAD, 512)) for n in range(2)]
        block = ctx.enter_context(nc.Block())
        idx_d = ins["dst_idx"].rearrange("(g p u) -> g p u", p=P, u=TILES)
        row_d = ins["dst_idx"].rearrange("(g n) -> g n", n=GROUP)

        @block.sync
        def _(sp):
            def load(g, b):
                sp.dma_start(idx[b][:], idx_d[g]).then_inc(loaded[b], 16)
                sp.dma_start(row[b][:], row_d[g].partition_broadcast(P)).then_inc(loaded[b], 16)

            load(0, 0)
            load(1, 1)
            with sp.Fori(0, NITER) as i:
                for b in range(2):
                    sp.wait_ge(gathered[2 * b], (i + 1) * (16 * QUAD))
                    sp.wait_ge(gathered[2 * b + 1], (i + 1) * (16 * QUAD))
                    sp.wait_ge(eq_done[b], i + 1)
                    waited(sp, sp_tick)
                    load(i * 2 + (2 + b), b)
            for b in range(2):
                sp.wait_ge(loaded[b], 16 * LOADS * (NITER + 1))

        @block.gpsimd
        def _(pool):
            def gather(q, u):
                c = QUAD * (q % 2) + u
                pool.indirect_dma_start(
                    out=dm[q][:, u, :], out_offset=None, in_=t.l3_dm[:],
                    in_offset=bass.IndirectOffsetOnAxis(ap=idx[q // 2][:, c:c + 1], axis=0)).then_inc(gathered[q], 16)

            for n in range(2):
                pool.dma_start(rows_of(t.l3_dst[n]), blank(t.zero, W)).then_inc(added[n], 16)
            pool.wait_ge(loaded[0], 16 * LOADS)
            for q in range(2):
                for u in range(QUAD):
                    gather(q, u)
            with pool.Fori(0, NITER) as i:
                for q in range(4):
                    ahead = (q + 2) % 4
                    pool.wait_ge(loaded[ahead // 2], (i + (2 if q >= 2 else 1)) * (16 * LOADS))
                    pool.wait_ge(used[ahead], i + (2 if q >= 2 else 1))
                    waited(pool, tick)
                    for u in range(QUAD):
                        gather(ahead, u)
                        if u == 0:
                            pool.wait_ge(rows_ready[q], i + 2)
                        n, c = u % 2, QUAD * (q % 2) + u
                        pool.wait_ge(added[n], (i * (2 * QUAD) + (q * (QUAD // 2) + u // 2 + 1)) * 16)
                        if u == 1:
                            pool.sem_inc(rows_free[(q - 1) % 4], 1)
                        else:
                            waited(pool, tick)
                        pool.indirect_dma_start(
                            out=t.l3_dst[n][:], out_offset=bass.IndirectOffsetOnAxis(ap=to[q // 2][:, c:c + 1], axis=0),
                            in_=rows[q][:, u, :], in_offset=None, compute_op=ALU.add).then_inc(added[n], 16)
            for n in range(2):
                pool.wait_ge(added[n], 16 * (NG * TILES // 2 + 1))
            for q in range(2):
                pool.wait_ge(gathered[q], 16 * QUAD * (NITER + 1))

        @block.vector
        def _(dve):
            for q in range(4):
                dve.sem_inc(used[q], 1)
            dve.sem_inc(msg_done, 1)
            with dve.Fori(0, NITER) as i:
                for q in range(4):
                    b = q // 2
                    count = [0]

                    def step(ins_):
                        count[0] += 1
                        ins_.then_inc(dve_step, 1)
                        dve.wait_ge(dve_step, i * (4 * 3) + (q * 3 + count[0]))

                    x = t.x_edge[:, bass.ds(i * 16 + q * QUAD, QUAD), :]
                    dve.wait_ge(gathered[q], (i + 1) * (16 * QUAD))
                    step(dve.tensor_tensor(al[:], x[:, :, D:D + HEADS], dm[q][:, :, 0:HEADS], ALU.add))
                    step(dve.scalar_tensor_tensor(out=al[:], in0=al[:], scalar=0.2, in1=al[:], op0=ALU.mult, op1=ALU.max))
                    step(dve.tensor_tensor(al[:], al[:], dm[q][:, :, HEADS:2 * HEADS], ALU.subtract))
                    dve.sem_inc(used[q], 1)
                    if q % 2 == 0:
                        dve.wait_ge(loaded[b], (i + 1) * (16 * LOADS))
                        dve.wait_ge(mm_done[2 * b + 1], i + 1)
                        dve.wait_ge(rows_free[2 * b + 1], i + 1)
                        dve.tensor_copy(to[b][:], t.to_dst[:, i * 2 + b, :])
                        dve.tensor_tensor(eq[b][:], row[b][:].rearrange("p (e u) -> p u e", u=TILES),
                                          over(idx[b][:].unsqueeze(2), [P, TILES, P]), ALU.is_equal).then_inc(eq_done[b], 1)
                    dve.wait_ge(exp_done, i * 4 + (q + 1))
                    dve.wait_ge(mm_done[(q - 2) % 4], i + (1 if q < 2 else 2))
                    m = msg[q % 2]
                    dve.tensor_copy(m[:, :, HEADS * D:W], ea[:])
                    for u in range(QUAD):
                        ins_ = dve.tensor_tensor(m[:, u, 0:HEADS * D].rearrange("p (h d) -> p h d", d=D),
                                                 over(x[:, u, 0:D].unsqueeze(1), [P, HEADS, D]),
                                                 over(ea[:, u, :].unsqueeze(2), [P, HEADS, D]), ALU.mult)
                    ins_.then_inc(msg_done, 1)

        @block.scalar
        def _(act):
            for q in range(4):
                act.sem_inc(rows_ready[q], 1)
            for q in range(3):
                act.sem_inc(rows_free[q], 1)
            with act.Fori(0, NITER) as i:
                for q in range(4):
                    act.wait_ge(dve_step, i * 12 + (q * 3 + 3))
                    act.wait_ge(msg_done, i * 4 + (q + 1))
                    act.activation(ea[:], al[:], ACT.Exp).then_inc(exp_done, 1)
                    act.wait_ge(mm_done[q], i + 2)
                    act.wait_ge(rows_free[q], i + 1)
                    act.copy(rows[q][:], ps[q % 2][:, :, 0:W]).then_inc(rows_ready[q], 1)

        @block.tensor
        def _(pe):
            for q in range(4):
                pe.sem_inc(mm_done[q], 1)
            with pe.Fori(0, NITER) as i:
                for q in range(4):
                    pe.wait_ge(msg_done, i * 4 + (q + 2))
                    pe.wait_ge(rows_ready[(q - 2) % 4], i + (1 if q < 2 else 2))
                    for u in range(QUAD):
                        mm = pe.matmul(ps[q % 2][:, u, 0:W], eq[q // 2][:, QUAD * (q % 2) + u, :],
                                       msg[q % 2][:, u, :], start=True, stop=True)
                    mm.then_inc(mm_done[q], 1)


def l3_attend(k, t, h, self_w):
    nc, ins = k.nc, k.ins
    loaded, dve_step, norm_done = k.sem("l3a_loaded"), k.sem("l3a_dve"), k.sem("l3a_norm")
    picked, turned, copied, mm_done, out_done = (
        k.sem("l3a_picked"), k.sem("l3a_turned"), k.sem("l3a_copied"), k.sem("l3a_mm"), k.sem("l3a_out"))
    var_ready, std_ready = k.sem("l3a_var"), k.sem("l3a_std")
    HC = HEADS * D
    with ExitStack() as ctx:
        a = [k.sb(f"l3a_s{n}", [P, NB, HC + HEADS], F32, ctx) for n in range(2)]
        wg = k.sb("l3a_wg", [P, 2, D], F32, ctx)
        vecs = k.sb("l3a_vecs", [P, 3, D], F32, ctx)
        part = k.sb("l3a_part", [P, CH, HC], F32, ctx)
        aT = k.sb("l3a_aT", [P, CH * 2, P], F32, ctx)
        c, q, st = (k.sb("l3a_c", [P, NB, D], F32, ctx), k.sb("l3a_q", [P, NB, D], F32, ctx),
                    k.sb("l3a_st", [P, 4, NB], F32, ctx))
        pt, po = k.ps("l3a_pt", ctx, (P, CH * 2, P)), k.ps("l3a_po", ctx)
        block = ctx.enter_context(nc.Block())
        LOADS = 2 + HEADS + 3

        @block.sync
        def _(sp):
            for n in range(2):
                sp.dma_start(a[n][:], rows_of(t.l3_dst[n])).then_inc(loaded, 16)
            for hd in range(HEADS):
                sp.dma_start(wg[D * (hd % 4):D * (hd % 4 + 1), hd // 4, :],
                             ins["L3_W_gat"][:, hd * D:(hd + 1) * D]).then_inc(loaded, 16)
            for n, name in enumerate(("bias_gat", "g1", "be1")):
                sp.dma_start(vecs[:, n, :], ins[f"L3_{name}"].partition_broadcast(P)).then_inc(loaded, 16)

        @block.vector
        def _(dve):
            step = chained(dve_step)
            dve.wait_ge(loaded, 16 * LOADS)
            step(dve, dve.tensor_tensor(a[0][:], a[0][:], a[1][:], ALU.add))
            den = a[0][:, :, HC:HC + HEADS]
            step(dve, dve.tensor_tensor(den, den, self_w[:], ALU.add))
            for hd in range(HEADS):
                step(dve, dve.tensor_tensor(a[1][:, :, hd * D:(hd + 1) * D], t.x[:],
                                            over(self_w[:, :, hd:hd + 1], [P, NB, D]), ALU.mult))
            step(dve, dve.tensor_tensor(a[0][:, :, 0:HC], a[0][:, :, 0:HC], a[1][:, :, 0:HC], ALU.add))
            step(dve, dve.tensor_scalar(den, den, 1e-16, None, ALU.add))
            step(dve, dve.reciprocal(den, den))
            step(dve, dve.tensor_scalar(den, den, 1.0 / HEADS, None, ALU.mult))
            for hd in range(HEADS):
                step(dve, dve.tensor_tensor(a[1][:, :, hd * D:(hd + 1) * D], a[0][:, :, hd * D:(hd + 1) * D],
                                            over(a[0][:, :, HC + hd:HC + hd + 1], [P, NB, D]), ALU.mult))
            dve.sem_inc(norm_done, 1)
            dve.sem_inc(out_done, 1)
            with dve.Fori(0, NB // CH) as n:
                dve.wait_ge(mm_done, n + 2)
                dve.tensor_copy(h[:, bass.ds(n * CH, CH), :],
                                po[:, 0:CH * D].rearrange("p (b d) -> p b d", b=CH)).then_inc(out_done, 1)
            dve.wait_ge(out_done, NB // CH + 1)
            step(dve, dve.tensor_tensor(h[:], h[:], over(vecs[:, 0:1, :], [P, NB, D]), ALU.add))
            step(dve, dve.tensor_tensor(h[:], h[:], t.x[:], ALU.add))
            layer_norm(dve, step, h[:], h[:], c[:], q[:], st, var_ready, std_ready, 1)
            step(dve, dve.tensor_tensor(h[:], h[:], over(vecs[:, 1:2, :], [P, NB, D]), ALU.mult))
            step(dve, dve.tensor_tensor(h[:], h[:], over(vecs[:, 2:3, :], [P, NB, D]), ALU.add))

        @block.scalar
        def _(act):
            act.wait_ge(norm_done, 1)
            with act.Fori(0, NB // CH) as n:
                act.wait_ge(mm_done, n + 1)
                act.copy(part[:], a[1][:, bass.ds(n * CH, CH), 0:HC]).then_inc(picked, 1)
                act.wait_ge(turned, n + 1)
                act.copy(aT[:], pt[:]).then_inc(copied, 1)
            std_of(act, st, var_ready, std_ready, 1)

        @block.tensor
        def _(pe):
            pe.sem_inc(mm_done, 1)
            with pe.Fori(0, NB // CH) as n:
                pe.wait_ge(picked, n + 1)
                for b in range(CH):
                    for half in range(2):
                        mm = pe.transpose(pt[:, 2 * b + half, :], part[:, b, half * P:(half + 1) * P], t.ident[:])
                mm.then_inc(turned, 1)
                pe.wait_ge(copied, n + 1)
                pe.wait_ge(out_done, n + 1)
                for b in range(CH):
                    for half in range(2):
                        mm = pe.matmul(po[:, b * D:(b + 1) * D], aT[:, 2 * b + half, :], wg[:, half, :],
                                       start=(half == 0), stop=(half == 1))
                mm.then_inc(mm_done, 1)


def finish(k, t, h, ff, out):
    nc, ins = k.nc, k.ins
    loaded, dve_step, var_ready, std_ready, done, stored = (
        k.sem("fin_loaded"), k.sem("fin_dve"), k.sem("fin_var"), k.sem("fin_std"), k.sem("fin_done"), k.sem("fin_stored"))
    with ExitStack() as ctx:
        vecs = k.sb("fin_vecs", [P, 2, D], F32, ctx)
        c, q, st = (k.sb("fin_c", [P, NB, D], F32, ctx), k.sb("fin_q", [P, NB, D], F32, ctx),
                    k.sb("fin_st", [P, 4, NB], F32, ctx))
        block = ctx.enter_context(nc.Block())
        whole = N // P

        @block.sync
        def _(sp):
            for n, name in enumerate(("g2", "be2")):
                sp.dma_start(vecs[:, n, :], ins[f"L3_{name}"].partition_broadcast(P)).then_inc(loaded, 16)
            sp.wait_ge(done, 1)
            sp.dma_start(out[0:whole * P].rearrange("(j p) d -> p j d", p=P), t.x[:, 0:whole, :]).then_inc(stored, 16)
            sp.dma_start(out[whole * P:N], t.x[0:N - whole * P, whole, :]).then_inc(stored, 16)
            sp.wait_ge(stored, 32)

        @block.scalar
        def _(act):
            for n in (1, 2):
                std_of(act, st, var_ready, std_ready, n)

        @block.vector
        def _(dve):
            step = chained(dve_step)
            dve.wait_ge(loaded, 32)
            step(dve, dve.tensor_tensor(h[:], h[:], ff[:], ALU.add))
            layer_norm(dve, step, h[:], h[:], c[:], q[:], st, var_ready, std_ready, 1)
            step(dve, dve.tensor_tensor(h[:], h[:], over(vecs[:, 0:1, :], [P, NB, D]), ALU.mult))
            step(dve, dve.tensor_tensor(h[:], h[:], over(vecs[:, 1:2, :], [P, NB, D]), ALU.add))
            step(dve, dve.tensor_tensor(h[:], h[:], t.x[:], ALU.add))
            layer_norm(dve, step, h[:], t.x[:], c[:], q[:], st, var_ready, std_ready, 2)
            dve.sem_inc(done, 1)


def l3(k, t, out):
    t.l3_max = [k.dram(f"l3_max{u}", [NT, HEADS]) for u in range(QUAD)]
    t.l3_dm = k.dram("l3_dm", [NT, 2 * HEADS])
    t.l3_dst = [k.dram(f"l3_dst{n}", [NT, HEADS * D + HEADS]) for n in range(2)]
    outer = k.ctx.enter_context(ExitStack())
    with ExitStack() as ctx:
        self_w = k.sb("self_w", [P, NB, HEADS], F32, outer)
        t.x_edge = k.sb("x_edge", [P, NG * TILES, D + HEADS], F32, ctx)
        with ExitStack() as c0:
            a_all = k.sb("a_all", [P, NB, 2 * HEADS], F32, c0)
            with ExitStack() as c1:
                xT = k.sb("l3_xT", [D, NT], F32, c1)
                turn_nodes(k, "l3t", t, t.x, xT)
                l3_scores(k, t, xT, a_all)
            l3_max(k, t)
            l3_bounds(k, t, a_all, self_w)
        l3_edges(k, t)
    with ExitStack() as ctx:
        h, ff = k.sb("l3_h", [P, NB, D], F32, ctx), k.sb("l3_ff", [P, NB, D], F32, ctx)
        l3_attend(k, t, h, self_w)
        xT = k.sb("l3_hT", [D, NT], F32, ctx)
        turn_nodes(k, "l3u", t, h, xT)
        mlp(k, "l3f", None, xT, [("L3_w1", "L3_b1", "L3_w2", "L3_b2", ff)])
        finish(k, t, h, ff, out)


class Tables:
    pass


def program(nc, ins, out, upto=99):
    with ExitStack() as ctx:
        k = Kit(nc, ctx, ins)
        t = Tables()
        t.ident, t.tri = k.sb("ident", [P, P]), k.sb("tri", [P, P])
        t.spill = k.sb("spill", [P, 1])
        t.zero, t.lowest = k.sb("zero", [P, 264]), k.sb("lowest", [P, HEADS])
        t.x = k.sb("x", [P, NB, D])
        t.nvec = k.sb("nvec", [P, NGL, TILES * 3])
        t.wgt, t.wgain = k.sb("wgt", [P, NGL, TILES]), k.sb("wgain", [P, NGL, TILES])
        t.to_dst, t.to_src = k.sb("to_dst", [P, NG, TILES], I32), k.sb("to_src", [P, NG, TILES], I32)
        t.h2, t.x1, t.x2, t.x3 = (k.dram("t_h2", [NT, D]), k.dram("t_x1", [NT, D]), k.dram("t_x2", [NT, D]),
                                  k.dram("t_x3", [NT, D + HEADS]))
        t.l0_dst, t.l0_src = k.dram("l0_dst", [NT, 2 * D]), k.dram("l0_src", [NT, 2 * D])
        t.l1_dst = [k.dram(f"l1_dst{n}", [NT, D]) for n in range(2)]
        t.l2_src = [k.dram(f"l2_src{n}", [NT, D + 1]) for n in range(2)]
        setup(k, t)
        with ExitStack() as c0:
            t.h1, h2 = k.sb("h1", [P, NB, D], F32, c0), k.sb("h2", [P, NB, D], F32, c0)
            mlp(k, "l0m", "xT", None, [("L0_W1a", "L0_b1a", "L0_W2a", "L0_b2a", t.h1),
                                       ("L0_W1b", "L0_b1b", "L0_W2b", "L0_b2b", h2)])
            store_rows(k, "l0s", [(t.h2, h2[:])])
            l0_edges(k, t)
            l0_nodes(k, t)
        k.next_layer()
        if upto > 1:
            l1_edges(k, t)
            residual_nodes(k, "l1n", t, t.l1_dst, lambda dve, step, sums: step(dve, dve.tensor_tensor(
                sums[0][:], sums[0][:], sums[1][:], ALU.add)), t.x2)
        if upto > 2:
            k.next_layer()
            l2_edges(k, t)

            def laplacian(dve, step, sums):
                a, b = sums
                step(dve, dve.tensor_tensor(a[:], a[:], b[:], ALU.add))
                step(dve, dve.tensor_tensor(b[:, :, 0:D], t.x[:], over(a[:, :, D:D + 1], [P, NB, D]), ALU.mult))
                step(dve, dve.tensor_tensor(a[:, :, 0:D], a[:, :, 0:D], b[:, :, 0:D], ALU.subtract))

            residual_nodes(k, "l2n", t, t.l2_src, laplacian, None)
        if upto > 3:
            k.next_layer()
            l3(k, t, out)
        else:
            done = k.sem("done")
            with nc.Block() as block:
                @block.sync
                def _(sp):
                    sp.dma_start(out[0:24 * P].rearrange("(j p) d -> p j d", p=P), t.x[:, 0:24, :]).then_inc(done, 16)
                    sp.dma_start(out[24 * P:N], t.x[0:N - 24 * P, 24, :]).then_inc(done, 16)
                    sp.wait_ge(done, 32)


def layouts(inputs):
    def a(name):
        return np.ascontiguousarray(np.asarray(inputs[name]))

    def padded(x, n, value):
        full = np.full((n,) + x.shape[1:], value, x.dtype)
        full[:x.shape[0]] = x
        return full

    el = NGL * GROUP
    x = padded(a("x"), NT, 0)
    emb = padded(a("edge_attr_10"), el, 0)
    out = {
        "x_rows": x, "xT": np.ascontiguousarray(x.T),
        "src_idx": padded(a("src"), el, N), "dst_idx": padded(a("dst"), el, N),
        "edge_feat": padded(a("edge_attr_32"), el, 0), "edge_vec": padded(a("edge_attr_3"), el, 1),
        "edge_w": padded(a("edge_weight"), el, 0),
        "embT": np.ascontiguousarray(emb.reshape(NGL, P, TILES, 10).transpose(0, 3, 2, 1).reshape(NGL, 10, GROUP)),
        "ident": np.eye(P, dtype=np.float32), "tri": np.tril(np.ones((P, P), np.float32), -1),
        "spill": (SPILL + np.arange(P, dtype=np.float32))[:, None],
    }
    for name in ("W1a", "b1a", "W2a", "b2a", "W1b", "b1b", "W2b", "b2b"):
        out[f"L0_{name}"] = a(f"L0_gnn_{name}")
    out["L1_W1"] = a("L1_gnn_W1")
    out["L1_W2"] = np.ascontiguousarray(a("L1_gnn_W2").reshape(MUL, 7, MUL, MOUT).transpose(1, 2, 3, 0))
    for name in ("W_gat", "att_src", "att_dst", "bias_gat", "w1", "b1", "w2", "b2", "g1", "be1", "g2", "be2"):
        out[f"L3_{name}"] = a(f"L3_gnn_{name}")
    return out


def kernel(**inputs):
    import concourse.bacc as bacc
    from concourse.bass_utils import run_bass_kernel_spmd

    nc = bacc.Bacc("TRN2", target_bir_lowering=False, num_devices=1)
    arrays = {f"in_{name}": array for name, array in layouts(inputs).items()}
    ins = {name[3:]: nc.dram_tensor(name, a.shape, mybir.dt.from_np(a.dtype), kind="ExternalInput").ap()
           for name, a in arrays.items()}
    out = nc.dram_tensor("out_0", (N, D), F32, kind="ExternalOutput").ap()
    program(nc, ins, out)
    return run_bass_kernel_spmd(nc, [arrays], core_ids=[0]).results[0]["out_0"]
```

```python
from contextlib import ExitStack

import numpy as np

import concourse.bass as bass
from concourse import mybir

ALU = mybir.AluOpType
ACT = mybir.ActivationFunctionType
F32 = mybir.dt.float32
BF16 = mybir.dt.bfloat16
I32 = mybir.dt.int32
AX = mybir.AxisListType

N, E, D = 3125, 53125, 32
HID = 128
HEADS = 8
P = 128
TILES = 8
GROUP = P * TILES
QUAD = 4
NG = -(-E // GROUP)
NGL = NG + 3
NITER = NG // 2
NB = -(-(N + 1 + P) // P)
NT = NB * P
SPILL = N + 1
CH = 2
assert NG % 2 == 0 and NB % CH == 0

MUL, MOUT, FEAT = 16, 8, 80
TANH_GAIN = 1.593
INV_SQRT3 = 3.0 ** -0.5
PW_S, PW_V = 0.17677669529663687, 0.25
HID_SCALE = 2.0 ** 0.5 / 10.0 ** 0.5 / 16.0 ** 0.5
EPS = 1e-5
LOWEST = -1.0e30


class Kit:

    def __init__(self, nc, ctx, ins):
        self.nc, self.ctx, self.ins = nc, ctx, ins
        self.layer_sems = []

    def sem(self, name):
        self.layer_sems.append(self.nc.alloc_semaphore(name))
        return self.layer_sems[-1]

    def next_layer(self):
        self.nc.clear_and_free_semaphores(self.layer_sems)
        self.layer_sems = []
        self.nc.all_engine_barrier()

    def sems(self, name, n):
        return [self.sem(f"{name}{i}") for i in range(n)]

    def sb(self, name, shape, dt=F32, ctx=None):
        return (ctx or self.ctx).enter_context(self.nc.sbuf_tensor(name, shape, dt))

    def ps(self, name, ctx, shape=(P, 512), dt=F32):
        return ctx.enter_context(self.nc.psum_tensor(name, list(shape), dt))

    def dram(self, name, shape, dt=F32):
        return self.nc.dram_tensor(name, shape, dt, kind="Internal")


class Path:

    def __init__(self):
        self.engines = {}

    def sync(self, program):
        self.engines["sync"] = program

    def gpsimd(self, program):
        self.engines["gpsimd"] = program

    def vector(self, program):
        self.engines["vector"] = program

    def scalar(self, program):
        self.engines["scalar"] = program

    def tensor(self, program):
        self.engines["tensor"] = program


def either(k, t, windowed, general):
    paths = []
    for way in (windowed, general):
        with ExitStack() as ctx:
            paths.append(way(k, t, ctx).engines)

    def run(eng, name):
        flag = eng.value_load(t.flag[0:1, 0:1], min_val=0, max_val=1)
        with eng.If(flag == 1):
            if name in paths[0]:
                paths[0][name](eng)
        with eng.Else():
            if name in paths[1]:
                paths[1][name](eng)

    with k.nc.Block() as block:
        @block.sync
        def _(sp):
            run(sp, "sync")

        @block.gpsimd
        def _(pool):
            run(pool, "gpsimd")

        @block.vector
        def _(dve):
            run(dve, "vector")

        @block.scalar
        def _(act):
            run(act, "scalar")

        @block.tensor
        def _(pe):
            run(pe, "tensor")
    k.next_layer()


def rows_of(table):
    return table[:, :].rearrange("(j p) w -> p j w", p=P)


def blank(tile, w):
    return over(tile[:, 0:w].unsqueeze(1), [P, NB, w])


def over(ap, shape):
    return ap.to_broadcast(shape)


def waited(eng, tick):
    eng.sem_inc(tick, 1)


def chained(sem):
    count = [0]

    def step(eng, ins):
        count[0] += 1
        ins.then_inc(sem, 1)
        eng.wait_ge(sem, count[0])

    return step


def in_parts(dve, step, x, parts, rest):
    step(dve, dve.tensor_copy(parts[:, :, 0, :], x))
    step(dve, dve.tensor_tensor(rest[:, 0], x, parts[:, :, 0, :], ALU.subtract))
    step(dve, dve.tensor_copy(parts[:, :, 1, :], rest[:, 0]))
    step(dve, dve.tensor_tensor(rest[:, 1], rest[:, 0], parts[:, :, 1, :], ALU.subtract))
    step(dve, dve.tensor_copy(parts[:, :, 2, :], rest[:, 1]))


def act_match_at(act, t, at, row, g, off, step):
    step(act.activation(off[:].rearrange("p u e -> p (u e)"), row[:], ACT.Square, bias=t.node_neg[:, bass.ds(g, 1)]))
    return act.activation(at[:].rearrange("p u e -> p e u"), off[:].rearrange("p u e -> p (u e)").rearrange(
        "p (e u) -> p e u", u=TILES), ACT.Relu, bias=1.0, scale=-1.0)


def act_match_of(act, t, of, g, off, step):
    for u in range(TILES):
        ins = act.activation(off[:, u, :], t.iota_f[:], ACT.Square,
                             bias=t.rel_neg[:, bass.ds(g, 1), u:u + 1].rearrange("p g u -> p (g u)"))
    step(ins)
    return act.activation(of[:], off[:], ACT.Relu, bias=1.0, scale=-1.0)


def layer_norm(dve, step, x, out, c, q, st, var_ready, std_ready, n):
    full = [P, NB, D]
    step(dve, dve.tensor_reduce(st[:, 0, :], x, AX.X, ALU.add))
    step(dve, dve.tensor_scalar(st[:, 0, :], st[:, 0, :], -1.0 / D, None, ALU.mult))
    step(dve, dve.tensor_tensor(c, x, over(st[:, 0, :].unsqueeze(2), full), ALU.add))
    step(dve, dve.tensor_tensor(q, c, c, ALU.mult))
    step(dve, dve.tensor_reduce(st[:, 1, :], q, AX.X, ALU.add))
    dve.tensor_scalar(st[:, 1, :], st[:, 1, :], 1.0 / D, EPS, ALU.mult, ALU.add).then_inc(var_ready, 1)
    dve.wait_ge(std_ready, n)
    step(dve, dve.reciprocal(st[:, 3, :], st[:, 2, :]))
    step(dve, dve.tensor_tensor(out, c, over(st[:, 3, :].unsqueeze(2), full), ALU.mult))


def std_of(act, st, var_ready, std_ready, n):
    act.wait_ge(var_ready, n)
    act.activation(st[:, 2, :], st[:, 1, :], ACT.Sqrt).then_inc(std_ready, 1)


def setup(k, t):
    nc, ins = k.nc, k.ins
    loaded, sq_ready, sqrt_done, dve_step = (
        k.sem("setup_loaded"), k.sem("norm2_ready"), k.sem("norm_ready"), k.sem("setup_dve"))
    with ExitStack() as ctx:
        sq = k.sb("sq", [P, NGL * TILES, 3], F32, ctx)
        n2 = k.sb("n2", [P, NGL * TILES], F32, ctx)
        block = ctx.enter_context(nc.Block())
        loads = [
            (t.ident[:], ins["ident"]), (t.tri[:], ins["tri"]), (t.spill[:], ins["spill"]),
            (t.nvec[:], ins["edge_vec"].rearrange("(g p u) i -> p g (u i)", p=P, u=TILES)),
            (t.wgt[:], ins["edge_w"].rearrange("(g p u) -> p g u", p=P, u=TILES)),
            (t.x[:], rows_of(ins["x_rows"])),
        ]

        @block.sync
        def _(sp):
            for dst, src in loads:
                sp.dma_start(dst, src).then_inc(loaded, 16)

        @block.scalar
        def _(act):
            act.wait_ge(sq_ready, 1)
            act.activation(n2[:], n2[:], ACT.Sqrt).then_inc(sqrt_done, 1)

        @block.vector
        def _(dve):
            step = chained(dve_step)
            dve.wait_ge(loaded, 16 * len(loads))
            step(dve, dve.memset(t.zero[:], 0.0))
            step(dve, dve.memset(t.lowest[:], LOWEST))
            nv = t.nvec[:].rearrange("p g (u i) -> p (g u) i", i=3)
            step(dve, dve.tensor_tensor(sq[:], nv, nv, ALU.mult))
            dve.tensor_reduce(n2[:], sq[:], AX.X, ALU.add).then_inc(sq_ready, 1)
            dve.wait_ge(sqrt_done, 1)
            step(dve, dve.reciprocal(n2[:], n2[:]))
            step(dve, dve.tensor_tensor(nv, nv, over(n2[:].unsqueeze(2), [P, NGL * TILES, 3]), ALU.mult))
            step(dve, dve.tensor_scalar(t.wgain[:], t.wgt[:], TANH_GAIN, None, ALU.mult))


def windows(k, t):
    nc, ins = k.nc, k.ins
    loaded, spans_ready, stored, dve_step = k.sem("win_loaded"), k.sem("win_spans"), k.sem("win_stored"), k.sem("win_dve")
    ends_d = k.dram("win_ends_d", [NGL, 2])
    with ExitStack() as ctx:
        nodes = k.sb("win_nodes", [NGL, GROUP], I32, ctx)
        nodes_f = k.sb("win_nodes_f", [NGL, GROUP], F32, ctx)
        ends = k.sb("win_ends", [NGL, 2], F32, ctx)
        all_ends = k.sb("win_all_ends", [P, NGL, 2], F32, ctx)
        dst = k.sb("win_dst", [P, NGL, TILES], I32, ctx)
        span = k.sb("win_span", [P, NGL], F32, ctx)
        widest = k.sb("win_widest", [P, 1], F32, ctx)
        part = k.sb("win_part", [P, 1], F32, ctx)
        block = ctx.enter_context(nc.Block())

        @block.sync
        def _(sp):
            sp.dma_start(nodes[:], ins["dst_idx"].rearrange("(g n) -> g n", n=GROUP)).then_inc(loaded, 16)
            sp.dma_start(dst[:], ins["dst_idx"].rearrange("(g p u) -> p g u", p=P, u=TILES)).then_inc(loaded, 16)
            sp.dma_start(t.iota[:], ins["iota"].partition_broadcast(P)).then_inc(loaded, 16)
            sp.wait_ge(spans_ready, 1)
            sp.dma_start(ends_d[:, :], ends[:]).then_inc(stored, 16)
            sp.wait_ge(stored, 16)
            sp.dma_start(all_ends[:].rearrange("p g e -> p (g e)"),
                         ends_d[:, :].rearrange("g e -> (g e)").partition_broadcast(P)).then_inc(loaded, 16)

        @block.vector
        def _(dve):
            step = chained(dve_step)
            dve.wait_ge(loaded, 48)
            step(dve, dve.tensor_copy(nodes_f[:], nodes[:]))
            step(dve, dve.tensor_reduce(ends[:, 0:1], nodes_f[:], AX.X, ALU.min))
            step(dve, dve.tensor_reduce(ends[:, 1:2], nodes_f[:], AX.X, ALU.max))
            dve.sem_inc(spans_ready, 1)
            dve.wait_ge(loaded, 64)
            lo = all_ends[:, :, 0]
            step(dve, dve.tensor_tensor(span[:], all_ends[:, :, 1], lo, ALU.subtract))
            step(dve, dve.tensor_reduce(widest[:], span[:], AX.X, ALU.max))
            step(dve, dve.tensor_scalar(t.flag[:], widest[:], float(P), None, ALU.is_lt))
            step(dve, dve.tensor_copy(t.base[:], lo))
            step(dve, dve.tensor_scalar(part[:], t.spill[:], -float(SPILL), None, ALU.add))
            step(dve, dve.tensor_scalar(t.node[:], lo, part[:, 0:1], None, ALU.add))
            step(dve, dve.tensor_tensor(t.rel[:], dst[:], over(lo.unsqueeze(2), [P, NGL, TILES]), ALU.subtract))
            step(dve, dve.tensor_scalar(t.node_neg[:], t.node[:], -1.0, None, ALU.mult))
            step(dve, dve.tensor_scalar(t.rel_neg[:], t.rel[:], -1.0, None, ALU.mult))
            step(dve, dve.tensor_copy(t.iota_f[:], t.iota[:]))


def mlp(k, tag, xT_name, xT_ap, nets, prepare=None):
    nc = k.nc
    n = len(nets)
    loaded = k.sem(f"{tag}_loaded")
    hid_done, relu_done = k.sems(f"{tag}_hid", n), k.sems(f"{tag}_relu", n)
    out_done, add_done = k.sems(f"{tag}_out", n), k.sems(f"{tag}_add", n)
    with ExitStack() as ctx:
        w1 = [k.sb(f"{tag}_w1_{i}", [D, HID], F32, ctx) for i in range(n)]
        b1 = [k.sb(f"{tag}_b1_{i}", [HID, 1], F32, ctx) for i in range(n)]
        w2 = [k.sb(f"{tag}_w2_{i}", [HID, D], F32, ctx) for i in range(n)]
        b2 = [k.sb(f"{tag}_b2_{i}", [P, D], F32, ctx) for i in range(n)]
        hid = [k.sb(f"{tag}_h{i}", [HID, CH * P], F32, ctx) for i in range(n)]
        ph = [k.ps(f"{tag}_ph{i}", ctx) for i in range(n)]
        po = [k.ps(f"{tag}_po{i}", ctx) for i in range(n)]
        block = ctx.enter_context(nc.Block())
        n_loads = 4 * n + (xT_ap is None)
        xT = k.sb(f"{tag}_xT", [D, NT], F32, ctx) if xT_ap is None else xT_ap

        @block.sync
        def _(sp):
            if xT_ap is None:
                sp.dma_start(xT[:], k.ins[xT_name]).then_inc(loaded, 16)
            for i, (a, b, c, d, _) in enumerate(nets):
                sp.dma_start(w1[i][:], k.ins[a]).then_inc(loaded, 16)
                sp.dma_start(b1[i][:], k.ins[b].rearrange("(h o) -> h o", o=1)).then_inc(loaded, 16)
                sp.dma_start(w2[i][:], k.ins[c]).then_inc(loaded, 16)
                sp.dma_start(b2[i][:], k.ins[d].partition_broadcast(P)).then_inc(loaded, 16)

        @block.tensor
        def _(pe):
            pe.wait_ge(loaded, 16 * n_loads)
            for i in range(n):
                pe.sem_inc(out_done[i], 1)
            with pe.Fori(0, NB // CH) as c:
                for i in range(n):
                    pe.matmul(ph[i][:, 0:CH * P], w1[i][:], xT[:, bass.ds(c * (CH * P), CH * P)],
                              start=True, stop=True).then_inc(hid_done[i], 1)
                for i in range(n):
                    pe.wait_ge(relu_done[i], c + 1)
                    pe.wait_ge(add_done[i], c + 1)
                    for b in range(CH):
                        mm = pe.matmul(po[i][:, b * D:(b + 1) * D], hid[i][:, b * P:(b + 1) * P], w2[i][:],
                                       start=True, stop=True)
                    mm.then_inc(out_done[i], 1)

        @block.scalar
        def _(act):
            act.wait_ge(loaded, 16 * n_loads)
            with act.Fori(0, NB // CH) as c:
                for i in range(n):
                    act.wait_ge(hid_done[i], c + 1)
                    act.wait_ge(out_done[i], c + 1)
                    act.activation(hid[i][:], ph[i][:, 0:CH * P], ACT.Relu, bias=b1[i][:, 0:1]).then_inc(relu_done[i], 1)

        @block.vector
        def _(dve):
            dve.wait_ge(loaded, 16 * n_loads)
            for i in range(n):
                dve.sem_inc(add_done[i], 1)
            with dve.Fori(0, NB // CH) as c:
                for i in range(n):
                    dve.wait_ge(out_done[i], c + 2)
                    dve.tensor_tensor(nets[i][4][:, bass.ds(c * CH, CH), :],
                                      po[i][:, 0:CH * D].rearrange("p (b d) -> p b d", d=D),
                                      over(b2[i][:].unsqueeze(1), [P, CH, D]), ALU.add).then_inc(add_done[i], 1)


def store_rows(k, tag, pairs):
    stored = k.sem(f"{tag}_stored")
    with k.nc.Block() as block:
        @block.sync
        def _(sp):
            for table, rows in pairs:
                sp.dma_start(rows_of(table), rows).then_inc(stored, 16)
            sp.wait_ge(stored, 16 * len(pairs))


def l0_edges_general(k, t, ctx):
    nc, ins = k.nc, k.ins
    loaded, tick, sp_tick = k.sems("l0_loaded", 2), k.sem("l0_tick"), k.sem("l0_sp_tick")
    gathered, mul_done, mm_done = k.sems("l0_gathered", 4), k.sems("l0_mul", 4), k.sems("l0_mm", 4)
    rows_ready, rows_free = k.sems("l0_rows", 4), k.sems("l0_rows_free", 4)
    sig_done, eq_done = k.sems("l0_sig", 2), k.sems("l0_eq", 2)
    added = {"dst": k.sem("l0_added_dst"), "src": k.sem("l0_added_src")}
    dve_step, filled = k.sem("l0_dve"), k.sem("l0_filled")
    LOADS = 5
    EQ_STEPS = 12
    feat = [k.sb(f"l0_feat{b}", [P, TILES * D], F32, ctx) for b in range(2)]
    idx = {s: [k.sb(f"l0_{s}_idx{b}", [P, TILES], I32, ctx) for b in range(2)] for s in ("dst", "src")}
    row = {s: [k.sb(f"l0_{s}_row{b}", [P, GROUP], I32, ctx) for b in range(2)] for s in ("dst", "src")}
    eq = {s: [k.sb(f"l0_{s}_eq{b}", [P, TILES, P], F32, ctx) for b in range(2)] for s in ("dst", "src")}
    to = {s: [k.sb(f"l0_{s}_to{b}", [P, TILES], I32, ctx) for b in range(2)] for s in ("dst", "src")}
    before = k.sb("l0_before", [P, TILES, P], F32, ctx)
    rank = k.sb("l0_rank", [P, TILES], F32, ctx)
    away = k.sb("l0_away", [P, TILES], F32, ctx)
    msg = [k.sb(f"l0_msg{b}", [P, TILES, 3 * D], F32, ctx) for b in range(2)]
    h2 = {s: [k.sb(f"l0_{s}_h2_{q}", [P, QUAD, D], F32, ctx) for q in range(4)] for s in ("dst", "src")}
    rows = [k.sb(f"l0_rows{q}", [P, 2, QUAD, 2 * D], F32, ctx) for q in range(4)]
    ps = [k.ps(f"l0_ps{q}", ctx, (P, 2, QUAD, 2 * D)) for q in range(4)]
    block = Path()
    idx_d = {s: ins[f"{s}_idx"].rearrange("(g p u) -> g p u", p=P, u=TILES) for s in ("dst", "src")}
    row_d = {s: ins[f"{s}_idx"].rearrange("(g n) -> g n", n=GROUP) for s in ("dst", "src")}
    feat_d = ins["edge_feat"].rearrange("(g p u) d -> g p (u d)", p=P, u=TILES)
    table = {"dst": t.l0_dst, "src": t.l0_src[0]}
    side = {"dst": 0, "src": 1}

    @block.sync
    def _(sp):
        def load(g, b):
            sp.dma_start(feat[b][:], feat_d[g]).then_inc(loaded[b], 16)
            for s in ("src", "dst"):
                sp.dma_start(idx[s][b][:], idx_d[s][g]).then_inc(loaded[b], 16)
                sp.dma_start(row[s][b][:], row_d[s][g].partition_broadcast(P)).then_inc(loaded[b], 16)

        load(0, 0)
        load(1, 1)
        with sp.Fori(0, NITER) as i:
            for b in range(2):
                sp.wait_ge(gathered[2 * b], (i + 1) * (32 * QUAD))
                sp.wait_ge(gathered[2 * b + 1], (i + 1) * (32 * QUAD))
                sp.wait_ge(eq_done[b], i + 1)
                sp.wait_ge(sig_done[b], i + 1)
                waited(sp, sp_tick)
                load(i * 2 + (2 + b), b)
        for b in range(2):
            sp.wait_ge(loaded[b], 16 * LOADS * (NITER + 1))

    @block.gpsimd
    def _(pool):
        def gather(q, u):
            b = q // 2
            c = QUAD * (q % 2) + u
            for s, other in (("src", "src"), ("dst", "dst")):
                pool.indirect_dma_start(
                    out=h2[s][q][:, u, :], out_offset=None, in_=t.h2[:],
                    in_offset=bass.IndirectOffsetOnAxis(ap=idx[s][b][:, c:c + 1], axis=0)).then_inc(gathered[q], 16)

        def add(s, q, u):
            b, c = q // 2, QUAD * (q % 2) + u
            pool.indirect_dma_start(
                out=table[s][:], out_offset=bass.IndirectOffsetOnAxis(ap=to[s][b][:, c:c + 1], axis=0),
                in_=rows[q][:, side[s], u, :], in_offset=None, compute_op=ALU.add).then_inc(added[s], 16)

        for s in ("dst", "src"):
            pool.dma_start(rows_of(table[s]), blank(t.zero, 2 * D)).then_inc(added[s], 16)
        for n in range(1, 4):
            pool.dma_start(rows_of(t.l0_src[n]), blank(t.zero, 2 * D)).then_inc(filled, 16)
        pool.wait_ge(filled, 48)
        pool.wait_ge(loaded[0], 16 * LOADS)
        for q in range(2):
            for u in range(QUAD):
                gather(q, u)
        with pool.Fori(0, NITER) as i:
            for q in range(4):
                ahead = (q + 2) % 4
                pool.wait_ge(loaded[ahead // 2], (i + (2 if q >= 2 else 1)) * (16 * LOADS))
                pool.wait_ge(mul_done[ahead], i + (2 if q >= 2 else 1))
                waited(pool, tick)
                for u in range(QUAD):
                    gather(ahead, u)
                    if u == 0:
                        pool.wait_ge(rows_ready[q], i + 2)
                    for s in ("dst", "src"):
                        pool.wait_ge(added[s], (i * (4 * QUAD) + (q * QUAD + u + 1)) * 16)
                    if u == 0:
                        pool.sem_inc(rows_free[(q - 1) % 4], 1)
                    else:
                        waited(pool, tick)
                    add("dst", q, u)
                    add("src", q, u)
        for s in ("dst", "src"):
            pool.wait_ge(added[s], 16 * (NG * TILES + 1))
        for q in range(2):
            pool.wait_ge(gathered[q], 32 * QUAD * (NITER + 1))

    @block.vector
    def _(dve):
        for q in range(4):
            dve.sem_inc(mul_done[q], 1)
        with dve.Fori(0, NITER) as i:
            for b in range(2):
                count = [0]

                def step(ins_):
                    count[0] += 1
                    ins_.then_inc(dve_step, 1)
                    dve.wait_ge(dve_step, i * (2 * EQ_STEPS) + (b * EQ_STEPS + count[0]))

                dve.wait_ge(loaded[b], (i + 1) * (16 * LOADS))
                dve.wait_ge(mm_done[2 * b + 1], i + 1)
                dve.wait_ge(rows_free[2 * b + 1], i + 1)
                full = [P, TILES, P]
                for s, kept in (("dst", t.to_dst), ("src", t.to_src)):
                    step(dve.tensor_tensor(eq[s][b][:], row[s][b][:].rearrange("p (e u) -> p u e", u=TILES),
                                           over(idx[s][b][:].unsqueeze(2), full), ALU.is_equal))
                    step(dve.tensor_tensor(before[:], eq[s][b][:], over(t.tri[:].unsqueeze(1), full), ALU.mult))
                    step(dve.tensor_reduce(rank[:], before[:], AX.X, ALU.add))
                    step(dve.tensor_scalar(away[:], idx[s][b][:], -1.0, t.spill[:, 0:1], ALU.mult, ALU.add))
                    step(dve.scalar_tensor_tensor(out=away[:], in0=rank[:], scalar=0.0, in1=away[:],
                                                  op0=ALU.is_gt, op1=ALU.mult))
                    step(dve.tensor_tensor(to[s][b][:], away[:], idx[s][b][:], ALU.add))
                    last = dve.tensor_copy(kept[:, i * 2 + b, :], to[s][b][:])
                last.then_inc(eq_done[b], 1)
                dve.wait_ge(sig_done[b], i + 1)
                for half in range(2):
                    q, c = 2 * b + half, QUAD * half
                    dve.wait_ge(gathered[q], (i + 1) * (32 * QUAD))
                    sig = msg[b][:, c:c + QUAD, D:2 * D]
                    dve.tensor_tensor(msg[b][:, c:c + QUAD, 0:D], sig, h2["src"][q][:], ALU.mult)
                    dve.tensor_tensor(msg[b][:, c:c + QUAD, 2 * D:3 * D], sig, h2["dst"][q][:],
                                      ALU.mult).then_inc(mul_done[q], 1)

    @block.scalar
    def _(act):
        for q in range(4):
            act.sem_inc(rows_ready[q], 1)
        for q in range(3):
            act.sem_inc(rows_free[q], 1)
        with act.Fori(0, NITER) as i:
            for b in range(2):
                act.wait_ge(loaded[b], (i + 1) * (16 * LOADS))
                act.wait_ge(mm_done[2 * b + 1], i + 1)
                act.activation(msg[b][:, :, D:2 * D], feat[b][:].rearrange("p (u d) -> p u d", d=D),
                               ACT.Sigmoid).then_inc(sig_done[b], 1)
                for half in range(2):
                    q = 2 * b + half
                    act.wait_ge(mm_done[q], i + 2)
                    act.wait_ge(rows_free[q], i + 1)
                    act.copy(rows[q][:], ps[q][:]).then_inc(rows_ready[q], 1)

    @block.tensor
    def _(pe):
        for q in range(4):
            pe.sem_inc(mm_done[q], 1)
        with pe.Fori(0, NITER) as i:
            for q in range(4):
                b, c = q // 2, QUAD * (q % 2)
                pe.wait_ge(mul_done[q], i + 2)
                pe.wait_ge(rows_ready[q], i + 1)
                for u in range(QUAD):
                    for s, lo in (("dst", 0), ("src", D)):
                        mm = pe.matmul(ps[q][:, side[s], u, :], eq[s][b][:, c + u, :],
                                       msg[b][:, c + u, lo:lo + 2 * D], start=True, stop=True)
                mm.then_inc(mm_done[q], 1)

    return block


def l0_edges_windows(k, t, ctx):
    nc, ins = k.nc, k.ins
    loaded, tick, sp_tick = k.sems("w0_loaded", 2), k.sem("w0_tick"), k.sem("w0_sp_tick")
    gathered, used, at_done, eq_done, of_done = (
        k.sems("w0_gathered", 2), k.sems("w0_used", 2), k.sem("w0_at"), k.sem("w0_eq"), k.sem("w0_of"))
    fetched, sig_done, mul_done, mm_done = k.sem("w0_fetched"), k.sem("w0_sig"), k.sem("w0_mul"), k.sem("w0_mm")
    hid_done, relu_done = k.sem("w0_hid"), k.sem("w0_relu")
    rows_ready, rows_free, dve_step = k.sem("w0_rows"), k.sem("w0_rows_free"), k.sem("w0_dve")
    wts, read, put, added_src = k.sem("w0_wts"), k.sem("w0_read"), k.sem("w0_put"), k.sems("w0_added_src", 4)
    LOADS = 6
    TABLES = 4
    STEPS = 4
    feat = [k.sb(f"w0_feat{b}", [P, TILES * D], F32, ctx) for b in range(2)]
    idx = [k.sb(f"w0_idx{b}", [P, TILES], I32, ctx) for b in range(2)]
    row_s = [k.sb(f"w0_row_s{b}", [P, GROUP], I32, ctx) for b in range(2)]
    row_d = [k.sb(f"w0_row_d{b}", [P, GROUP], I32, ctx) for b in range(2)]
    emb = [k.sb(f"w0_emb{b}", [10, GROUP], F32, ctx) for b in range(2)]
    w1 = k.sb("w0_w1", [10, MUL], F32, ctx)
    win = [k.sb(f"w0_win{b}", [P, D], F32, ctx) for b in range(2)]
    at, of, eq = ([k.sb(f"w0_{name}{b}", [P, TILES, P], F32, ctx) for b in range(2)] for name in ("at", "of", "eq"))
    to = [k.sb(f"w0_to{b}", [P, TILES], I32, ctx) for b in range(2)]
    before = k.sb("w0_before", [P, TILES, P], F32, ctx)
    rank, away = k.sb("w0_rank", [P, TILES], F32, ctx), k.sb("w0_away", [P, TILES], F32, ctx)
    h2s = [k.sb(f"w0_h2s{b}", [P, TILES, D], F32, ctx) for b in range(2)]
    msg = [k.sb(f"w0_msg{b}", [P, TILES, 3 * D], F32, ctx) for b in range(2)]
    rows_s = [k.sb(f"w0_rows_s{b}", [P, TILES, 2 * D], F32, ctx) for b in range(2)]
    cur = [k.sb(f"w0_cur{b}", [P, 2 * D], F32, ctx) for b in range(2)]
    rows_d = [k.sb(f"w0_rows_d{b}", [P, 2 * D], F32, ctx) for b in range(2)]
    p_fetch = [k.ps(f"w0_p_fetch{b}", ctx) for b in range(2)]
    p_src = [k.ps(f"w0_p_src{b}", ctx) for b in range(2)]
    p_dst = [k.ps(f"w0_p_dst{b}", ctx) for b in range(2)]
    p_hid = [k.ps(f"w0_p_hid{b}", ctx) for b in range(2)]
    block = Path()
    idx_d = ins["src_idx"].rearrange("(g p u) -> g p u", p=P, u=TILES)
    rows_in = {s: ins[f"{s}_idx"].rearrange("(g n) -> g n", n=GROUP) for s in ("dst", "src")}
    feat_d = ins["edge_feat"].rearrange("(g p u) d -> g p (u d)", p=P, u=TILES)

    @block.sync
    def _(sp):
        def load(g, b):
            w = sp.value_load(t.base[0:1, bass.ds(g, 1)], min_val=0, max_val=N)
            sp.dma_start(idx[b][:], idx_d[g]).then_inc(loaded[b], 16)
            sp.dma_start(row_d[b][:], rows_in["dst"][g].partition_broadcast(P)).then_inc(loaded[b], 16)
            sp.dma_start(win[b][:], t.h2[bass.ds(w, P), :]).then_inc(loaded[b], 16)
            sp.dma_start(row_s[b][:], rows_in["src"][g].partition_broadcast(P)).then_inc(loaded[b], 16)
            sp.dma_start(feat[b][:], feat_d[g]).then_inc(loaded[b], 16)
            sp.dma_start(emb[b][:], ins["embT"][g]).then_inc(loaded[b], 16)

        sp.dma_start(rows_of(t.l0_dst), blank(t.zero, 2 * D)).then_inc(put, 16)
        sp.dma_start(w1[:], ins["L1_W1"]).then_inc(wts, 16)
        load(0, 0)
        load(1, 1)
        with sp.Fori(0, NITER) as i:
            for b in range(2):
                g = i * 2 + b
                sp.wait_ge(put, (g + 1) * 16)
                waited(sp, sp_tick)
                w = sp.value_load(t.base[0:1, bass.ds(g, 1)], min_val=0, max_val=N)
                sp.dma_start(cur[b][:], t.l0_dst[bass.ds(w, P), :]).then_inc(read, 16)
                sp.wait_ge(gathered[b], (i + 1) * (16 * TILES))
                sp.wait_ge(eq_done, g + 1)
                sp.wait_ge(fetched, g + 1)
                waited(sp, sp_tick)
                sp.wait_ge(sig_done, g + 1)
                sp.wait_ge(hid_done, g + 1)
                waited(sp, sp_tick)
                load(g + 2, b)
                sp.wait_ge(rows_ready, g + 3)
                waited(sp, sp_tick)
                sp.dma_start(t.l0_dst[bass.ds(w, P), :], rows_d[b][:]).then_inc(put, 16)
        sp.wait_ge(put, 16 * (NG + 1))
        for b in range(2):
            sp.wait_ge(loaded[b], 16 * LOADS * (NITER + 1))

    @block.gpsimd
    def _(pool):
        def gather(b, u):
            pool.indirect_dma_start(
                out=h2s[b][:, u, :], out_offset=None, in_=t.h2[:],
                in_offset=bass.IndirectOffsetOnAxis(ap=idx[b][:, u:u + 1], axis=0)).then_inc(gathered[b], 16)

        for n in range(TABLES):
            pool.dma_start(rows_of(t.l0_src[n]), blank(t.zero, 2 * D)).then_inc(added_src[n], 16)
        for b in range(2):
            pool.wait_ge(loaded[b], 16 * LOADS)
            for u in range(TILES):
                gather(b, u)
        with pool.Fori(0, NITER) as i:
            for b in range(2):
                g = i * 2 + b
                pool.wait_ge(loaded[b], (i + 2) * (16 * LOADS))
                pool.wait_ge(used[b], i + 1)
                waited(pool, tick)
                for u in range(TILES):
                    gather(b, u)
                    if u == 0:
                        pool.wait_ge(rows_ready, g + 3)
                    n = u % TABLES
                    pool.wait_ge(added_src[n], (g * (TILES // TABLES) + (u // TABLES + 1)) * 16)
                    if u == TABLES - 1:
                        pool.sem_inc(rows_free, 1)
                    else:
                        waited(pool, tick)
                    pool.indirect_dma_start(
                        out=t.l0_src[n][:], out_offset=bass.IndirectOffsetOnAxis(ap=to[b][:, u:u + 1], axis=0),
                        in_=rows_s[b][:, u, :], in_offset=None, compute_op=ALU.add).then_inc(added_src[n], 16)
        for n in range(TABLES):
            pool.wait_ge(added_src[n], 16 * (NG * TILES // TABLES + 1))
        for b in range(2):
            pool.wait_ge(gathered[b], 16 * TILES * (NITER + 1))

    @block.vector
    def _(dve):
        with dve.Fori(0, NITER) as i:
            for b in range(2):
                g = i * 2 + b
                count = [0]

                def step(ins_):
                    count[0] += 1
                    ins_.then_inc(dve_step, 1)
                    dve.wait_ge(dve_step, g * STEPS + count[0])

                full = [P, TILES, P]
                dve.wait_ge(loaded[b], (i + 1) * (16 * LOADS))
                dve.wait_ge(mm_done, g + 1)
                dve.tensor_tensor(at[b][:], row_d[b][:].rearrange("p (e u) -> p u e", u=TILES),
                                  over(t.node[:, bass.ds(g, 1)].unsqueeze(2), full), ALU.is_equal).then_inc(at_done, 1)
                step(dve.tensor_tensor(eq[b][:], row_s[b][:].rearrange("p (e u) -> p u e", u=TILES),
                                       over(idx[b][:].unsqueeze(2), full), ALU.is_equal))
                step(dve.tensor_tensor(before[:], eq[b][:], over(t.tri[:].unsqueeze(1), full), ALU.mult))
                dve.tensor_scalar(away[:], idx[b][:], -1.0, t.spill[:, 0:1], ALU.mult, ALU.add)
                step(dve.tensor_reduce(rank[:], before[:], AX.X, ALU.add))
                step(dve.scalar_tensor_tensor(out=away[:], in0=rank[:], scalar=0.0, in1=away[:],
                                              op0=ALU.is_gt, op1=ALU.mult))
                dve.tensor_tensor(t.to_src[:, bass.ds(g, 1), :].rearrange("p g u -> p (g u)"), away[:], idx[b][:],
                                  ALU.add).then_inc(eq_done, 1)
                dve.tensor_tensor(of[b][:], over(t.iota[:].unsqueeze(1), full),
                                  over(t.rel[:, bass.ds(g, 1), :].rearrange("p g u -> p u g"), full),
                                  ALU.is_equal).then_inc(of_done, 1)
                dve.wait_ge(sig_done, g + 1)
                dve.wait_ge(gathered[b], (i + 1) * (16 * TILES))
                sig = msg[b][:, :, D:2 * D]
                dve.tensor_tensor(msg[b][:, :, 0:D], sig, h2s[b][:], ALU.mult).then_inc(used[b], 1)
                dve.wait_ge(fetched, g + 1)
                dve.tensor_tensor(msg[b][:, :, 2 * D:3 * D], sig,
                                  p_fetch[b][:, 0:TILES * D].rearrange("p (u d) -> p u d", d=D), ALU.mult).then_inc(mul_done, 1)

    @block.scalar
    def _(act):
        act.sem_inc(rows_free, 1)
        act.sem_inc(rows_ready, 2)
        act.sem_inc(relu_done, 2)

        def sigmoid(g, b, turn):
            act.wait_ge(loaded[b], turn * (16 * LOADS))
            act.wait_ge(mm_done, g + 1)
            act.activation(msg[b][:, :, D:2 * D], feat[b][:].rearrange("p (u d) -> p u d", d=D),
                           ACT.Sigmoid).then_inc(sig_done, 1)

        sigmoid(0, 0, 1)
        with act.Fori(0, NITER) as i:
            for b in range(2):
                g = i * 2 + b
                sigmoid(g + 1, 1 - b, i + (b + 1))
                act.wait_ge(hid_done, g + 1)
                act.activation(t.hid[:, bass.ds(g * TILES, TILES), :],
                               p_hid[b][:, 0:TILES * MUL].rearrange("p (u c) -> p u c", c=MUL), ACT.Relu,
                               scale=HID_SCALE).then_inc(relu_done, 1)
                act.wait_ge(mm_done, g + 3)
                act.wait_ge(rows_free, g + 1)
                act.wait_ge(eq_done, g + 1)
                act.copy(to[b][:], t.to_src[:, bass.ds(g, 1), :].rearrange("p g u -> p (g u)"))
                act.wait_ge(put, g * 16 + 16)
                act.copy(rows_d[b][:], p_dst[b][:, 0:2 * D])
                act.copy(rows_s[b][:], p_src[b][:].rearrange("p (u d) -> p u d", d=2 * D)).then_inc(rows_ready, 1)

    @block.tensor
    def _(pe):
        pe.sem_inc(mm_done, 2)
        pe.wait_ge(wts, 16)
        with pe.Fori(0, NITER) as i:
            for b in range(2):
                g = i * 2 + b
                pe.wait_ge(at_done, g + 1)
                for u in range(TILES):
                    mm = pe.matmul(p_fetch[b][:, u * D:(u + 1) * D], at[b][:, u, :], win[b][:], start=True, stop=True)
                mm.then_inc(fetched, 1)
                pe.wait_ge(relu_done, g + 1)
                for u in range(TILES):
                    mm = pe.matmul(p_hid[b][:, u * MUL:(u + 1) * MUL], emb[b][:, u * P:(u + 1) * P], w1[:],
                                   start=True, stop=True)
                mm.then_inc(hid_done, 1)
                pe.wait_ge(of_done, g + 1)
                pe.wait_ge(mul_done, g + 1)
                pe.wait_ge(rows_ready, g + 1)
                for u in range(TILES):
                    pe.matmul(p_src[b][:, u * 2 * D:(u + 1) * 2 * D], eq[b][:, u, :], msg[b][:, u, D:3 * D],
                              start=True, stop=True)
                for u in range(TILES):
                    pe.matmul(p_dst[b][:, 0:2 * D], of[b][:, u, :], msg[b][:, u, 0:2 * D], start=(u == 0), stop=False)
                pe.wait_ge(read, (g + 1) * 16)
                pe.matmul(p_dst[b][:, 0:2 * D], t.ident[:], cur[b][:], start=False, stop=True).then_inc(mm_done, 1)

    return block


def l0_nodes(k, t):
    nc = k.nc
    loaded, var_ready, std_ready, dve_step, stored, done = (
        k.sem("l0n_loaded"), k.sem("l0n_var"), k.sem("l0n_std"), k.sem("l0n_dve"), k.sem("l0n_stored"), k.sem("l0n_done"))
    with ExitStack() as ctx:
        a = k.sb("l0n_a", [P, NB, 2 * D], F32, ctx)
        src = [k.sb(f"l0n_src{n}", [P, NB, 2 * D], F32, ctx) for n in range(4)]
        b = src[0]
        c, q, h, st = (k.sb("l0n_c", [P, NB, D], F32, ctx), k.sb("l0n_q", [P, NB, D], F32, ctx),
                       k.sb("l0n_h", [P, NB, D], F32, ctx), k.sb("l0n_st", [P, 4, NB], F32, ctx))
        parts = k.sb("l0n_parts", [P, NB, 3, D], BF16, ctx)
        rest = k.sb("l0n_rest", [P, 2, NB, D], F32, ctx)
        block = ctx.enter_context(nc.Block())

        @block.sync
        def _(sp):
            sp.dma_start(a[:], rows_of(t.l0_dst)).then_inc(loaded, 16)
            for n in range(4):
                sp.dma_start(src[n][:], rows_of(t.l0_src[n])).then_inc(loaded, 16)
            sp.wait_ge(done, 1)
            sp.dma_start(rows_of(t.x1), t.x[:]).then_inc(stored, 16)
            sp.dma_start(rows_of(t.x1_parts), parts[:].rearrange("p j a d -> p j (a d)")).then_inc(stored, 16)
            sp.wait_ge(stored, 32)

        @block.scalar
        def _(act):
            for n in (1, 2):
                std_of(act, st, var_ready, std_ready, n)

        @block.vector
        def _(dve):
            step = chained(dve_step)
            dve.wait_ge(loaded, 80)
            for n in range(1, 4):
                step(dve, dve.tensor_tensor(b[:], b[:], src[n][:], ALU.add))
            step(dve, dve.tensor_tensor(c[:], a[:, :, D:2 * D], b[:, :, 0:D], ALU.add))
            step(dve, dve.tensor_scalar(c[:], c[:], 1e-7, None, ALU.add))
            step(dve, dve.reciprocal(c[:], c[:]))
            step(dve, dve.tensor_tensor(q[:], a[:, :, 0:D], b[:, :, D:2 * D], ALU.add))
            step(dve, dve.tensor_tensor(q[:], q[:], c[:], ALU.mult))
            step(dve, dve.tensor_tensor(h[:], q[:], t.h1[:], ALU.add))
            layer_norm(dve, step, h[:], h[:], c[:], q[:], st, var_ready, std_ready, 1)
            step(dve, dve.scalar_tensor_tensor(out=h[:], in0=h[:], scalar=0.0, in1=t.x[:], op0=ALU.max, op1=ALU.add))
            step(dve, dve.tensor_tensor(h[:], h[:], t.x[:], ALU.add))
            layer_norm(dve, step, h[:], t.x[:], c[:], q[:], st, var_ready, std_ready, 2)
            in_parts(dve, step, t.x[:], parts, rest)
            dve.sem_inc(done, 1)


def l1_weight_parts(wa, wb):
    parts = []
    for s in range(2):
        for kind, m, i in ((0, 0, 0), (1, 0, 1), (0, 1, 2), (1, 1, 3), (0, 2, 4)):
            parts.append((wa, 40 * s + 8 * kind, m, i, 8 * s))
        parts.append((wb, 40 * s + 8, 2, 6, 8 * s))
        for c in range(3):
            parts.append((wa, 40 * s + 16 + 8 * c, 3 + c, 5, 8 * s))
            parts.append((wb, 40 * s + 16 + 8 * c, 3 + c, 6, 8 * s))
    return parts


def l1_weight_scales(dve, step, wa, wb, n_outputs):
    step(dve, dve.tensor_scalar(wb[:, 2], wb[:, 2], 1.5 ** 0.5, None, ALU.mult))
    step(dve, dve.tensor_scalar(wb[:, 3:n_outputs], wb[:, 3:n_outputs], -(1.5 ** 0.5) / 3.0, None, ALU.mult))
    step(dve, dve.tensor_scalar(wa[:, 3:n_outputs], wa[:, 3:n_outputs], INV_SQRT3, None, ALU.mult))
    step(dve, dve.tensor_tensor(wa[:, 2:n_outputs], wa[:, 2:n_outputs], wb[:, 2:n_outputs], ALU.add))
    step(dve, dve.tensor_scalar(wa[:, 0:2], wa[:, 0:2], PW_S, None, ALU.mult))
    step(dve, dve.tensor_scalar(wa[:, 2:n_outputs], wa[:, 2:n_outputs], PW_V, None, ALU.mult))


def l1_edges_general(k, t, ctx):
    nc, ins = k.nc, k.ins
    loaded, tick, sp_tick = k.sems("l1_loaded", 2), k.sem("l1_tick"), k.sem("l1_sp_tick")
    wts, wts_done = k.sem("l1_weights"), k.sem("l1_weights_done")
    gathered, dots_done, comps_done = k.sems("l1_gathered", 4), k.sems("l1_dots", 4), k.sems("l1_comps", 4)
    turned, hid_done, turn_copied, relu_done = k.sem("l1_turned"), k.sem("l1_hid"), k.sem("l1_turn_copied"), k.sem("l1_relu")
    g_done, prod_done, sum_done = k.sem("l1_g"), k.sem("l1_prod"), k.sem("l1_sum")
    tanh_done, msg_done = k.sem("l1_tanh"), k.sem("l1_msg")
    mm_done, rows_ready, rows_free = k.sems("l1_mm", 4), k.sems("l1_rows", 4), k.sems("l1_rows_free", 4)
    eq_done, added, dve_step = k.sems("l1_eq", 2), k.sem("l1_added"), k.sem("l1_dve")
    LOADS = 4
    M = 6
    HALF = M * MOUT * MUL // 2
    Q_STEPS = 4
    idx = {s: [k.sb(f"l1_{s}_idx{b}", [P, TILES], I32, ctx) for b in range(2)] for s in ("dst", "src")}
    row = [k.sb(f"l1_row{b}", [P, GROUP], I32, ctx) for b in range(2)]
    emb = [k.sb(f"l1_emb{b}", [10, GROUP], F32, ctx) for b in range(2)]
    eq = [k.sb(f"l1_eq{b}", [P, TILES, P], F32, ctx) for b in range(2)]
    to = [k.sb(f"l1_to{b}", [P, TILES], I32, ctx) for b in range(2)]
    w1 = k.sb("l1_w1", [10, MUL], F32, ctx)
    wa = k.sb("l1_wa", [P, M, MOUT, MUL], F32, ctx)
    wb = k.sb("l1_wb", [P, M, MOUT, MUL], F32, ctx)
    xg = [k.sb(f"l1_xg{q}", [P, QUAD, 2, D], F32, ctx) for q in range(4)]
    pr = k.sb("l1_pr", [P, QUAD, 2, 8, 3], F32, ctx)
    feat = [k.sb(f"l1_feat{i}", [P, QUAD, 2, 40], F32, ctx) for i in range(2)]
    featT = [k.sb(f"l1_featT{i}", [P, QUAD * P], F32, ctx) for i in range(2)]
    hid = [k.sb(f"l1_hid{i}", [P, QUAD, MUL], F32, ctx) for i in range(2)]
    prod = [k.sb(f"l1_prod{i}", [P, 2, HALF // MUL, MUL], F32, ctx) for i in range(QUAD)]
    out = [k.sb(f"l1_out{i}", [P, QUAD, M, MOUT], F32, ctx) for i in range(2)]
    th = [k.sb(f"l1_th{i}", [P, QUAD, 2 * MOUT], F32, ctx) for i in range(2)]
    gt = k.sb("l1_gt", [P, QUAD, 8], F32, ctx)
    vk = k.sb("l1_vk", [P, QUAD, 8, 3], F32, ctx)
    msg = [k.sb(f"l1_msg{i}", [P, QUAD, D], F32, ctx) for i in range(2)]
    rows = [k.sb(f"l1_rows{q}", [P, QUAD, D], F32, ctx) for q in range(4)]
    p_turn, p_hid, p_sum = (k.ps(f"l1_p{n}", ctx) for n in ("turn", "hid", "sum"))
    p_g = [k.ps(f"l1_pg{i}", ctx, (P, 2, 512)) for i in range(2)]
    block = Path()
    idx_d = {s: ins[f"{s}_idx"].rearrange("(g p u) -> g p u", p=P, u=TILES) for s in ("dst", "src")}
    row_d = ins["dst_idx"].rearrange("(g n) -> g n", n=GROUP)
    w2_d = ins["L1_W2"]
    parts = l1_weight_parts(wa, wb)

    @block.sync
    def _(sp):
        def load(g, b):
            for s in ("src", "dst"):
                sp.dma_start(idx[s][b][:], idx_d[s][g]).then_inc(loaded[b], 16)
            sp.dma_start(row[b][:], row_d[g].partition_broadcast(P)).then_inc(loaded[b], 16)
            sp.dma_start(emb[b][:], ins["embT"][g]).then_inc(loaded[b], 16)

        load(0, 0)
        load(1, 1)
        sp.dma_start(w1[:], ins["L1_W1"]).then_inc(wts, 16)
        sp.wait_ge(wts_done, 2)
        for target, r, m, i, u in parts:
            sp.dma_start(target[r:r + 8, m, :, :], w2_d[i, u:u + 8]).then_inc(wts, 16)
        with sp.Fori(0, NITER) as i:
            for b in range(2):
                sp.wait_ge(gathered[2 * b], (i + 1) * (32 * QUAD))
                sp.wait_ge(gathered[2 * b + 1], (i + 1) * (32 * QUAD))
                sp.wait_ge(eq_done[b], i + 1)
                waited(sp, sp_tick)
                sp.wait_ge(hid_done, i * 4 + (2 * b + 2))
                waited(sp, sp_tick)
                load(i * 2 + (2 + b), b)
        for b in range(2):
            sp.wait_ge(loaded[b], 16 * LOADS * (NITER + 1))

    @block.gpsimd
    def _(pool):
        def gather(q, u):
            b, c = q // 2, QUAD * (q % 2) + u
            for s, at in (("src", 0), ("dst", 1)):
                pool.indirect_dma_start(
                    out=xg[q][:, u, at, :], out_offset=None, in_=t.x1[:],
                    in_offset=bass.IndirectOffsetOnAxis(ap=idx[s][b][:, c:c + 1], axis=0)).then_inc(gathered[q], 16)

        def add(q, u):
            b, c = q // 2, QUAD * (q % 2) + u
            pool.indirect_dma_start(
                out=t.l1_dst[:], out_offset=bass.IndirectOffsetOnAxis(ap=to[b][:, c:c + 1], axis=0),
                in_=rows[q][:, u, :], in_offset=None, compute_op=ALU.add).then_inc(added, 16)

        pool.dma_start(rows_of(t.l1_dst), blank(t.zero, D)).then_inc(added, 16)
        pool.wait_ge(loaded[0], 16 * LOADS)
        for q in range(2):
            for u in range(QUAD):
                gather(q, u)
        with pool.Fori(0, NITER) as i:
            for q in range(4):
                ahead = (q + 2) % 4
                pool.wait_ge(loaded[ahead // 2], (i + (2 if q >= 2 else 1)) * (16 * LOADS))
                pool.wait_ge(dots_done[ahead], i + (2 if q >= 2 else 1))
                pool.wait_ge(comps_done[ahead], i + (2 if q >= 2 else 1))
                waited(pool, tick)
                for u in range(QUAD):
                    gather(ahead, u)
                pool.wait_ge(rows_ready[q], i + 2)
                for u in range(QUAD):
                    pool.wait_ge(added, (i * (4 * QUAD) + (q * QUAD + u + 1)) * 16)
                    if u == 0:
                        pool.sem_inc(rows_free[(q - 1) % 4], 1)
                    else:
                        waited(pool, tick)
                    add(q, u)
        pool.wait_ge(added, 16 * (NG * TILES + 1))
        for q in range(2):
            pool.wait_ge(gathered[q], 32 * QUAD * (NITER + 1))

    @block.vector
    def _(dve):
        step = chained(wts_done)
        step(dve, dve.memset(wa[:], 0.0))
        step(dve, dve.memset(wb[:], 0.0))
        for i in range(2):
            step(dve, dve.memset(featT[i][:], 0.0))
        dve.wait_ge(wts, 16 * (len(parts) + 1))
        l1_weight_scales(dve, step, wa, wb, M)
        for q in range(4):
            dve.sem_inc(dots_done[q], 1)

        def dots(q, nth, g, turns, step):
            b, c = q // 2, QUAD * (q % 2)
            f = feat[nth % 2][:].rearrange("p t s f -> p (t s) f")
            dve.wait_ge(gathered[q], turns)
            nv = t.nvec[:, g, :].rearrange("p (u i) -> p u i", i=3)[:, c:c + QUAD, :]
            for s in range(2):
                ins_ = dve.tensor_tensor(pr[:, :, s, :, :], xg[q][:, :, s, 8:D].rearrange("p t (u i) -> p t u i", i=3),
                                         over(nv.unsqueeze(2), [P, QUAD, 8, 3]), ALU.mult)
            step(ins_)
            dve.tensor_reduce(f[:, :, 8:16], pr[:].rearrange("p t s u i -> p (t s) u i"), AX.X,
                              ALU.add).then_inc(dots_done[q], 1)

        first = [0]

        def first_step(ins_):
            first[0] += 1
            ins_.then_inc(dve_step, 1)
            dve.wait_ge(dve_step, first[0])

        dots(0, 0, 0, 32 * QUAD, first_step)
        with dve.Fori(0, NITER) as i:
            for q in range(4):
                b, half, c = q // 2, q % 2, QUAD * (q % 2)
                g = i * 2 + b
                count = [1]

                def step(ins_):
                    count[0] += 1
                    ins_.then_inc(dve_step, 1)
                    dve.wait_ge(dve_step, i * (4 * Q_STEPS) + (q * Q_STEPS + count[0]))

                def multiply(u):
                    n = i * (4 * QUAD) + (q * QUAD + u)
                    dve.wait_ge(g_done, n + 1)
                    dve.tensor_tensor(prod[u][:], p_g[u % 2][:, :, 0:HALF].rearrange("p a (x c) -> p a x c", c=MUL),
                                      over(hid[q % 2][:, u, :].unsqueeze(1).unsqueeze(1), [P, 2, HALF // MUL, MUL]),
                                      ALU.mult).then_inc(prod_done, 1)

                def contract(u):
                    n = i * (4 * QUAD) + (q * QUAD + u)
                    dve.wait_ge(prod_done, n + 1)
                    dve.tensor_reduce(out[q % 2][:, u].rearrange("p m w -> p (m w)"),
                                      prod[u][:].rearrange("p a x c -> p (a x) c"), AX.X, ALU.add).then_inc(sum_done, 1)

                dve.wait_ge(relu_done, i * 4 + (q + 1))
                multiply(0)
                dots((q + 1) % 4, q + 1, i * 2 + (q + 1) // 2, (i + (2 if q == 3 else 1)) * (32 * QUAD), step)
                multiply(1)
                contract(0)
                if half == 0:
                    dve.wait_ge(loaded[b], (i + 1) * (16 * LOADS))
                    dve.wait_ge(mm_done[2 * b + 1], i + 1)
                    dve.wait_ge(rows_free[2 * b + 1], i + 1)
                    dve.tensor_copy(to[b][:], t.to_dst[:, g, :])
                    dve.tensor_tensor(eq[b][:], row[b][:].rearrange("p (e u) -> p u e", u=TILES),
                                      over(idx["dst"][b][:].unsqueeze(2), [P, TILES, P]),
                                      ALU.is_equal).then_inc(eq_done[b], 1)
                multiply(2)
                contract(1)
                multiply(3)
                contract(2)
                contract(3)
                w = over(t.wgain[:, g, c:c + QUAD].unsqueeze(2), [P, QUAD, 8])
                n3 = t.nvec[:, g, :].rearrange("p (u i) -> p u i", i=3)[:, c:c + QUAD, :]
                o = out[q % 2]
                dve.wait_ge(sum_done, i * (4 * QUAD) + (q + 1) * QUAD)
                step(dve.tensor_tensor(vk[:], over(o[:, :, 2, :].unsqueeze(3), [P, QUAD, 8, 3]),
                                       over(n3.unsqueeze(2), [P, QUAD, 8, 3]), ALU.mult))
                step(dve.tensor_tensor(vk[:], vk[:], o[:, :, 3:M, :].rearrange("p t k w -> p t w k"), ALU.add))
                dve.wait_ge(tanh_done, i * 4 + (q + 1))
                dve.wait_ge(mm_done[(q - 2) % 4], i + (1 if q < 2 else 2))
                dve.tensor_tensor(msg[q % 2][:, :, 0:8], th[q % 2][:, :, 0:8], w, ALU.mult)
                step(dve.tensor_tensor(gt[:], th[q % 2][:, :, 8:16], w, ALU.mult))
                dve.tensor_tensor(msg[q % 2][:, :, 8:D].rearrange("p t (w k) -> p t w k", k=3), vk[:],
                                  over(gt[:].unsqueeze(3), [P, QUAD, 8, 3]), ALU.mult).then_inc(msg_done, 1)
                assert count[0] == Q_STEPS + 1

    @block.scalar
    def _(act):
        for q in range(4):
            act.sem_inc(rows_ready[q], 1)
            act.sem_inc(comps_done[q], 1)
        for q in range(3):
            act.sem_inc(rows_free[q], 1)

        def components(q, nth, turns):
            act.wait_ge(gathered[q], turns)
            x = xg[q][:].rearrange("p t s d -> p (t s) d")
            f = feat[nth % 2][:].rearrange("p t s f -> p (t s) f")
            act.copy(f[:, :, 0:8], x[:, :, 0:8])
            act.copy(f[:, :, 16:40].rearrange("p a (i u) -> p a i u", i=3),
                     x[:, :, 8:D].rearrange("p a (u i) -> p a i u", i=3)).then_inc(comps_done[q], 1)

        def turn(nth, n):
            act.wait_ge(hid_done, n)
            act.activation(hid[nth % 2][:].rearrange("p t c -> p (t c)"), p_hid[:, 0:QUAD * MUL], ACT.Relu,
                           scale=HID_SCALE).then_inc(relu_done, 1)
            act.wait_ge(turned, n)
            act.copy(featT[nth % 2][0:FEAT], p_turn[0:FEAT, :]).then_inc(turn_copied, 1)

        components(0, 0, 32 * QUAD)
        act.wait_ge(wts_done, 4)
        turn(0, 1)
        with act.Fori(0, NITER) as i:
            for q in range(4):
                components((q + 1) % 4, q + 1, (i + (2 if q == 3 else 1)) * (32 * QUAD))
                turn(q + 1, i * 4 + (q + 2))
                act.wait_ge(sum_done, i * (4 * QUAD) + (q + 1) * QUAD)
                act.activation(th[q % 2][:], out[q % 2][:, :, 0:2, :].rearrange("p t m w -> p t (m w)"),
                               ACT.Tanh).then_inc(tanh_done, 1)
                act.wait_ge(mm_done[q], i + 2)
                act.wait_ge(rows_free[q], i + 1)
                act.copy(rows[q][:], p_sum[:, 0:QUAD * D].rearrange("p (t d) -> p t d", d=D)).then_inc(rows_ready[q], 1)

    @block.tensor
    def _(pe):
        for q in range(4):
            pe.sem_inc(mm_done[q], 1)
        pe.wait_ge(wts_done, 10)

        def turn(q, nth, feat_turn):
            b, c = q // 2, q % 2
            for u in range(QUAD):
                mm = pe.matmul(p_hid[:, u * MUL:(u + 1) * MUL], emb[b][:, (c * QUAD + u) * P:(c * QUAD + u + 1) * P],
                               w1[:], start=True, stop=True)
            mm.then_inc(hid_done, 1)
            pe.wait_ge(dots_done[q], feat_turn)
            pe.wait_ge(comps_done[q], feat_turn)
            for u in range(QUAD):
                mm = pe.transpose(p_turn[0:FEAT, u * P:(u + 1) * P],
                                  feat[nth % 2][:, u].rearrange("p s f -> p (s f)"), t.ident[:])
            mm.then_inc(turned, 1)

        def products(nth, u):
            for h in range(2):
                mm = pe.matmul(p_g[u % 2][:, h, 0:HALF], featT[nth % 2][:, u * P:(u + 1) * P],
                               wa[:, 3 * h:3 * h + 3].rearrange("k m w c -> k (m w c)"), start=True, stop=True)
            mm.then_inc(g_done, 1)

        pe.wait_ge(loaded[0], 16 * LOADS)
        turn(0, 0, 2)
        pe.wait_ge(turn_copied, 1)
        products(0, 0)
        products(0, 1)
        with pe.Fori(0, NITER) as i:
            for q in range(4):
                b, c = q // 2, QUAD * (q % 2)
                n = i * (4 * QUAD) + q * QUAD
                pe.wait_ge(prod_done, n + 1)
                products(q, 2)
                if q % 2 == 1:
                    pe.wait_ge(loaded[(b + 1) % 2], (i + (2 if q == 3 else 1)) * (16 * LOADS))
                turn((q + 1) % 4, q + 1, i + (3 if q == 3 else 2))
                pe.wait_ge(prod_done, n + 2)
                products(q, 3)
                pe.wait_ge(turn_copied, i * 4 + (q + 2))
                for u in range(2):
                    pe.wait_ge(prod_done, n + (3 + u))
                    products(q + 1, u)
                pe.wait_ge(msg_done, i * 4 + (q + 1))
                pe.wait_ge(rows_ready[(q - 1) % 4], i + (1 if q == 0 else 2))
                for u in range(QUAD):
                    mm = pe.matmul(p_sum[:, u * D:(u + 1) * D], eq[b][:, c + u, :], msg[q % 2][:, u, :],
                                   start=True, stop=True)
                mm.then_inc(mm_done[q], 1)

    return block


def l1_edges_windows(k, t, ctx):
    nc, ins = k.nc, k.ins
    loaded, tick, sp_tick = k.sems("w1_loaded", 2), k.sem("w1_tick"), k.sem("w1_sp_tick")
    wts, wts_done = k.sem("w1_weights"), k.sem("w1_weights_done")
    gathered, dots_done, comps_done = k.sems("w1_gathered", 4), k.sems("w1_dots", 4), k.sems("w1_comps", 4)
    at_done, of_done, fetched, placed = k.sem("w1_at"), k.sem("w1_of"), k.sem("w1_fetched"), k.sem("w1_placed")
    turned, turn_copied, g_done, prod_done, sum_done = (
        k.sem("w1_turned"), k.sem("w1_turn_copied"), k.sem("w1_g"), k.sem("w1_prod"), k.sem("w1_sum"))
    tanh_done, msg_done, mm_done, dve_step = k.sem("w1_tanh"), k.sem("w1_msg"), k.sem("w1_mm"), k.sem("w1_dve")
    act_step = k.sem("w1_act")
    rows_ready, rows_free, added = k.sem("w1_rows"), k.sem("w1_rows_free"), k.sem("w1_added")
    LOADS = 3
    M = 6
    HALF = M * MOUT * MUL // 2
    Q_STEPS = 4
    idx = [k.sb(f"w1_idx{b}", [P, TILES], I32, ctx) for b in range(2)]
    row = [k.sb(f"w1_row{b}", [P, GROUP], I32, ctx) for b in range(2)]
    win = [k.sb(f"w1_win{b}", [P, 3, D], BF16, ctx) for b in range(2)]
    at = [k.sb(f"w1_at{b}", [P, TILES, P], BF16, ctx) for b in range(2)]
    of = [k.sb(f"w1_of{b}", [P, TILES, P], F32, ctx) for b in range(2)]
    wa = k.sb("w1_wa", [P, M, MOUT, MUL], F32, ctx)
    wb = k.sb("w1_wb", [P, M, MOUT, MUL], F32, ctx)
    xg = [k.sb(f"w1_xg{q}", [P, QUAD, 2, D], F32, ctx) for q in range(4)]
    pr = k.sb("w1_pr", [P, QUAD, 2, 8, 3], F32, ctx)
    feat = [k.sb(f"w1_feat{i}", [P, QUAD, 2, 40], F32, ctx) for i in range(2)]
    featT = [k.sb(f"w1_featT{i}", [P, QUAD * P], F32, ctx) for i in range(2)]
    off = k.sb("w1_off", [P, TILES, P], F32, ctx)
    prod = [k.sb(f"w1_prod{i}", [P, 2, HALF // MUL, MUL], F32, ctx) for i in range(QUAD)]
    out = [k.sb(f"w1_out{i}", [P, QUAD, M, MOUT], F32, ctx) for i in range(2)]
    th = [k.sb(f"w1_th{i}", [P, QUAD, 2 * MOUT], F32, ctx) for i in range(2)]
    gt = k.sb("w1_gt", [P, QUAD, 8], F32, ctx)
    vk = k.sb("w1_vk", [P, QUAD, 8, 3], F32, ctx)
    msg = [k.sb(f"w1_msg{i}", [P, QUAD, D], F32, ctx) for i in range(2)]
    rows = [k.sb(f"w1_rows{b}", [P, D], F32, ctx) for b in range(2)]
    p_turn, p_sum = k.ps("w1_pturn", ctx), k.ps("w1_psum", ctx)
    p_fetch = [k.ps(f"w1_pfetch{i}", ctx) for i in range(2)]
    p_g = [k.ps(f"w1_pg{i}", ctx, (P, 2, 512)) for i in range(2)]
    block = Path()
    idx_d = ins["src_idx"].rearrange("(g p u) -> g p u", p=P, u=TILES)
    row_d = ins["dst_idx"].rearrange("(g n) -> g n", n=GROUP)
    w2_d = ins["L1_W2"]
    parts = l1_weight_parts(wa, wb)

    @block.sync
    def _(sp):
        def load(g, b):
            w = sp.value_load(t.base[0:1, bass.ds(g, 1)], min_val=0, max_val=N)
            sp.dma_start(idx[b][:], idx_d[g]).then_inc(loaded[b], 16)
            sp.dma_start(row[b][:], row_d[g].partition_broadcast(P)).then_inc(loaded[b], 16)
            sp.dma_start(win[b][:].rearrange("p a d -> p (a d)"), t.x1_parts[bass.ds(w, P), :]).then_inc(loaded[b], 16)

        load(0, 0)
        load(1, 1)
        sp.wait_ge(wts_done, 2)
        for target, r, m, i, u in parts:
            sp.dma_start(target[r:r + 8, m, :, :], w2_d[i, u:u + 8]).then_inc(wts, 16)
        with sp.Fori(0, NITER) as i:
            for b in range(2):
                sp.wait_ge(gathered[2 * b], (i + 1) * (16 * QUAD))
                sp.wait_ge(gathered[2 * b + 1], (i + 1) * (16 * QUAD))
                waited(sp, sp_tick)
                sp.wait_ge(fetched, i * 4 + (2 * b + 2))
                waited(sp, sp_tick)
                load(i * 2 + (2 + b), b)
        for b in range(2):
            sp.wait_ge(loaded[b], 16 * LOADS * (NITER + 1))

    @block.gpsimd
    def _(pool):
        def gather(q, u):
            b, c = q // 2, QUAD * (q % 2) + u
            pool.indirect_dma_start(
                out=xg[q][:, u, 0, :], out_offset=None, in_=t.x1[:],
                in_offset=bass.IndirectOffsetOnAxis(ap=idx[b][:, c:c + 1], axis=0)).then_inc(gathered[q], 16)

        pool.dma_start(rows_of(t.l1_dst), blank(t.zero, D)).then_inc(added, 16)
        pool.wait_ge(loaded[0], 16 * LOADS)
        for q in range(2):
            for u in range(QUAD):
                gather(q, u)
        with pool.Fori(0, NITER) as i:
            for q in range(4):
                b, ahead = q // 2, (q + 2) % 4
                pool.wait_ge(loaded[ahead // 2], (i + (2 if q >= 2 else 1)) * (16 * LOADS))
                pool.wait_ge(dots_done[ahead], i + (2 if q >= 2 else 1))
                pool.wait_ge(comps_done[ahead], i + (2 if q >= 2 else 1))
                waited(pool, tick)
                for u in range(QUAD):
                    gather(ahead, u)
                if q % 2 == 1:
                    g = i * 2 + b
                    w = pool.value_load(t.base[0:1, bass.ds(g, 1)], min_val=0, max_val=N)
                    pool.wait_ge(rows_ready, g + 3)
                    pool.wait_ge(added, (g + 1) * 16)
                    pool.sem_inc(rows_free, 1)
                    pool.dma_start(t.l1_dst[bass.ds(w, P), :], rows[b][:], accum_op=ALU.add).then_inc(added, 16)
        pool.wait_ge(added, 16 * (NG + 1))
        for q in range(2):
            pool.wait_ge(gathered[q], 16 * QUAD * (NITER + 1))

    @block.vector
    def _(dve):
        step = chained(wts_done)
        step(dve, dve.memset(wa[:], 0.0))
        step(dve, dve.memset(wb[:], 0.0))
        for i in range(2):
            step(dve, dve.memset(featT[i][:], 0.0))
        dve.wait_ge(wts, 16 * len(parts))
        l1_weight_scales(dve, step, wa, wb, M)
        for q in range(4):
            dve.sem_inc(dots_done[q], 1)

        def dots(q, nth, g, turns, n_placed, step):
            b, c = q // 2, QUAD * (q % 2)
            f = feat[nth % 2][:].rearrange("p t s f -> p (t s) f")
            dve.wait_ge(gathered[q], turns)
            dve.wait_ge(placed, n_placed)
            nv = t.nvec[:, g, :].rearrange("p (u i) -> p u i", i=3)[:, c:c + QUAD, :]
            for s in range(2):
                ins_ = dve.tensor_tensor(pr[:, :, s, :, :], xg[q][:, :, s, 8:D].rearrange("p t (u i) -> p t u i", i=3),
                                         over(nv.unsqueeze(2), [P, QUAD, 8, 3]), ALU.mult)
            step(ins_)
            dve.tensor_reduce(f[:, :, 8:16], pr[:].rearrange("p t s u i -> p (t s) u i"), AX.X,
                              ALU.add).then_inc(dots_done[q], 1)

        first = [0]

        def first_step(ins_):
            first[0] += 1
            ins_.then_inc(dve_step, 1)
            dve.wait_ge(dve_step, first[0])

        dots(0, 0, 0, 16 * QUAD, 1, first_step)
        with dve.Fori(0, NITER) as i:
            for q in range(4):
                b, half, c = q // 2, q % 2, QUAD * (q % 2)
                g = i * 2 + b
                count = [1]

                def step(ins_):
                    count[0] += 1
                    ins_.then_inc(dve_step, 1)
                    dve.wait_ge(dve_step, i * (4 * Q_STEPS) + (q * Q_STEPS + count[0]))

                def multiply(u):
                    n = i * (4 * QUAD) + (q * QUAD + u)
                    dve.wait_ge(g_done, n + 1)
                    dve.tensor_tensor(prod[u][:], p_g[u % 2][:, :, 0:HALF].rearrange("p a (x c) -> p a x c", c=MUL),
                                      over(t.hid[:, bass.ds(n, 1), :].unsqueeze(1), [P, 2, HALF // MUL, MUL]),
                                      ALU.mult).then_inc(prod_done, 1)

                def contract(u):
                    n = i * (4 * QUAD) + (q * QUAD + u)
                    dve.wait_ge(prod_done, n + 1)
                    dve.tensor_reduce(out[q % 2][:, u].rearrange("p m w -> p (m w)"),
                                      prod[u][:].rearrange("p a x c -> p (a x) c"), AX.X, ALU.add).then_inc(sum_done, 1)

                multiply(0)
                dots((q + 1) % 4, q + 1, i * 2 + (q + 1) // 2, (i + (2 if q == 3 else 1)) * (16 * QUAD),
                     i * 4 + (q + 2), step)
                multiply(1)
                contract(0)
                multiply(2)
                contract(1)
                multiply(3)
                contract(2)
                contract(3)
                w = over(t.wgain[:, g, c:c + QUAD].unsqueeze(2), [P, QUAD, 8])
                n3 = t.nvec[:, g, :].rearrange("p (u i) -> p u i", i=3)[:, c:c + QUAD, :]
                o = out[q % 2]
                dve.wait_ge(sum_done, i * (4 * QUAD) + (q + 1) * QUAD)
                step(dve.tensor_tensor(vk[:], over(o[:, :, 2, :].unsqueeze(3), [P, QUAD, 8, 3]),
                                       over(n3.unsqueeze(2), [P, QUAD, 8, 3]), ALU.mult))
                step(dve.tensor_tensor(vk[:], vk[:], o[:, :, 3:M, :].rearrange("p t k w -> p t w k"), ALU.add))
                dve.wait_ge(tanh_done, i * 4 + (q + 1))
                dve.wait_ge(mm_done, i * 4 + (q + 1))
                dve.tensor_tensor(msg[q % 2][:, :, 0:8], th[q % 2][:, :, 0:8], w, ALU.mult)
                step(dve.tensor_tensor(gt[:], th[q % 2][:, :, 8:16], w, ALU.mult))
                dve.tensor_tensor(msg[q % 2][:, :, 8:D].rearrange("p t (w k) -> p t w k", k=3), vk[:],
                                  over(gt[:].unsqueeze(3), [P, QUAD, 8, 3]), ALU.mult).then_inc(msg_done, 1)
                assert count[0] == Q_STEPS + 1

    @block.scalar
    def _(act):
        for q in range(4):
            act.sem_inc(comps_done[q], 1)
        act.sem_inc(rows_ready, 2)
        act.sem_inc(rows_free, 1)

        def place(q, nth):
            act.wait_ge(fetched, nth)
            act.copy(xg[q][:, :, 1, :], p_fetch[q % 2][:, 0:QUAD * D].rearrange("p (t d) -> p t d", d=D)).then_inc(placed, 1)

        def components(q, nth, turns):
            act.wait_ge(gathered[q], turns)
            x = xg[q][:].rearrange("p t s d -> p (t s) d")
            f = feat[nth % 2][:].rearrange("p t s f -> p (t s) f")
            act.copy(f[:, :, 0:8], x[:, :, 0:8])
            act.copy(f[:, :, 16:40].rearrange("p a (i u) -> p a i u", i=3),
                     x[:, :, 8:D].rearrange("p a (u i) -> p a i u", i=3)).then_inc(comps_done[q], 1)

        def turn(nth, n):
            act.wait_ge(turned, n)
            act.copy(featT[nth % 2][0:FEAT], p_turn[0:FEAT, :]).then_inc(turn_copied, 1)

        def match_at(g, b, turn, n):
            def step(ins_):
                ins_.then_inc(act_step, 1)
                act.wait_ge(act_step, n)

            act.wait_ge(loaded[b], turn * (16 * LOADS))
            act_match_at(act, t, at[b], row[b], g, off, step).then_inc(at_done, 1)

        def match_of(g, b, n):
            def step(ins_):
                ins_.then_inc(act_step, 1)
                act.wait_ge(act_step, n)

            act.wait_ge(at_done, g + 1)
            act_match_of(act, t, of[b], g, off, step).then_inc(of_done, 1)

        match_at(0, 0, 1, 1)
        match_of(0, 0, 2)
        place(0, 1)
        place(1, 2)
        act.wait_ge(placed, 2)
        components(0, 0, 16 * QUAD)
        act.wait_ge(wts_done, 4)
        turn(0, 1)
        with act.Fori(0, NITER) as i:
            for q in range(4):
                act.wait_ge(placed, i * 4 + (q + 2))
                components((q + 1) % 4, q + 1, (i + (2 if q == 3 else 1)) * (16 * QUAD))
                turn(q + 1, i * 4 + (q + 2))
                g, b = i * 2 + q // 2, q // 2
                if q % 2 == 0:
                    act.wait_ge(of_done, g + 1)
                    match_at(g + 1, 1 - b, i + (b + 1), g * 2 + 3)
                place((q + 2) % 4, i * 4 + (q + 3))
                if q % 2 == 1:
                    act.wait_ge(mm_done, i * 4 + (q + 1))
                    match_of(g + 1, 1 - b, g * 2 + 4)
                act.wait_ge(sum_done, i * (4 * QUAD) + (q + 1) * QUAD)
                act.activation(th[q % 2][:], out[q % 2][:, :, 0:2, :].rearrange("p t m w -> p t (m w)"),
                               ACT.Tanh).then_inc(tanh_done, 1)
                if q % 2 == 1:
                    act.wait_ge(mm_done, i * 4 + (q + 3))
                    act.wait_ge(rows_free, i * 2 + (b + 1))
                    act.copy(rows[b][:], p_sum[:, b * D:(b + 1) * D]).then_inc(rows_ready, 1)

    @block.tensor
    def _(pe):
        pe.sem_inc(mm_done, 2)
        pe.wait_ge(wts_done, 10)

        def fetch(q, at_turn):
            b, c = q // 2, QUAD * (q % 2)
            pe.wait_ge(at_done, at_turn)
            for u in range(QUAD):
                for part in range(3):
                    mm = pe.matmul(p_fetch[q % 2][:, u * D:(u + 1) * D], at[b][:, c + u, :], win[b][:, part, :],
                                   start=(part == 0), stop=(part == 2))
            mm.then_inc(fetched, 1)

        def turn(q, nth, feat_turn):
            pe.wait_ge(dots_done[q], feat_turn)
            pe.wait_ge(comps_done[q], feat_turn)
            for u in range(QUAD):
                mm = pe.transpose(p_turn[0:FEAT, u * P:(u + 1) * P],
                                  feat[nth % 2][:, u].rearrange("p s f -> p (s f)"), t.ident[:])
            mm.then_inc(turned, 1)

        def products(nth, u):
            for h in range(2):
                mm = pe.matmul(p_g[u % 2][:, h, 0:HALF], featT[nth % 2][:, u * P:(u + 1) * P],
                               wa[:, 3 * h:3 * h + 3].rearrange("k m w c -> k (m w c)"), start=True, stop=True)
            mm.then_inc(g_done, 1)

        fetch(0, 1)
        fetch(1, 1)
        turn(0, 0, 2)
        pe.wait_ge(turn_copied, 1)
        products(0, 0)
        products(0, 1)
        with pe.Fori(0, NITER) as i:
            for q in range(4):
                b, c = q // 2, QUAD * (q % 2)
                n = i * (4 * QUAD) + q * QUAD
                pe.wait_ge(prod_done, n + 1)
                products(q, 2)
                turn((q + 1) % 4, q + 1, i + (3 if q == 3 else 2))
                pe.wait_ge(prod_done, n + 2)
                products(q, 3)
                pe.wait_ge(placed, i * 4 + (q + 1))
                fetch((q + 2) % 4, i * 2 + (b + 2))
                pe.wait_ge(turn_copied, i * 4 + (q + 2))
                for u in range(2):
                    pe.wait_ge(prod_done, n + (3 + u))
                    products(q + 1, u)
                pe.wait_ge(msg_done, i * 4 + (q + 1))
                if q % 2 == 0:
                    pe.wait_ge(of_done, i * 2 + (b + 1))
                    pe.wait_ge(rows_ready, i * 2 + (b + 1))
                for u in range(QUAD):
                    mm = pe.matmul(p_sum[:, b * D:(b + 1) * D], of[b][:, c + u, :], msg[q % 2][:, u, :],
                                   start=(c + u == 0), stop=(c + u == TILES - 1))
                mm.then_inc(mm_done, 1)

    return block


def residual_nodes(k, tag, t, load, combine, out):
    nc = k.nc
    loaded, var_ready, std_ready, dve_step, stored, done = (
        k.sem(f"{tag}_loaded"), k.sem(f"{tag}_var"), k.sem(f"{tag}_std"), k.sem(f"{tag}_dve"), k.sem(f"{tag}_stored"),
        k.sem(f"{tag}_done"))
    with ExitStack() as ctx:
        sums = [k.sb(f"{tag}_s{n}", [P, NB, table.shape[1]], F32, ctx) for n, table in enumerate(load)]
        c, q, st = (k.sb(f"{tag}_c", [P, NB, D], F32, ctx), k.sb(f"{tag}_q", [P, NB, D], F32, ctx),
                    k.sb(f"{tag}_st", [P, 4, NB], F32, ctx))
        block = ctx.enter_context(nc.Block())

        @block.sync
        def _(sp):
            for tile, table in zip(sums, load):
                sp.dma_start(tile[:], rows_of(table)).then_inc(loaded, 16)
            if out is not None:
                sp.wait_ge(done, 1)
                sp.dma_start(rows_of(out), t.x[:]).then_inc(stored, 16)
                sp.wait_ge(stored, 16)

        @block.scalar
        def _(act):
            std_of(act, st, var_ready, std_ready, 1)

        @block.vector
        def _(dve):
            step = chained(dve_step)
            dve.wait_ge(loaded, 16 * len(load))
            combine(dve, step, sums)
            step(dve, dve.tensor_tensor(t.x[:], t.x[:], sums[0][:, :, 0:D], ALU.add))
            layer_norm(dve, step, t.x[:], t.x[:], c[:], q[:], st, var_ready, std_ready, 1)
            dve.sem_inc(done, 1)


def l2_edges_general(k, t, ctx):
    nc, ins = k.nc, k.ins
    loaded, tick, sp_tick = k.sems("l2_loaded", 2), k.sem("l2_tick"), k.sem("l2_sp_tick")
    gathered, mul_done, mm_done = k.sems("l2_gathered", 4), k.sems("l2_mul", 4), k.sems("l2_mm", 4)
    rows_ready, rows_free, eq_done = k.sems("l2_rows", 4), k.sems("l2_rows_free", 4), k.sems("l2_eq", 2)
    added, filled = k.sems("l2_added", 2), k.sem("l2_filled")
    LOADS = 3
    W = D + 1
    idx = {s: [k.sb(f"l2_{s}_idx{b}", [P, TILES], I32, ctx) for b in range(2)] for s in ("dst", "src")}
    row = [k.sb(f"l2_row{b}", [P, GROUP], I32, ctx) for b in range(2)]
    eq = [k.sb(f"l2_eq{b}", [P, TILES, P], F32, ctx) for b in range(2)]
    to = [k.sb(f"l2_to{b}", [P, TILES], I32, ctx) for b in range(2)]
    xg = [k.sb(f"l2_xg{q}", [P, QUAD, D], F32, ctx) for q in range(4)]
    msg = [k.sb(f"l2_msg{q}", [P, QUAD, W], F32, ctx) for q in range(4)]
    rows = [k.sb(f"l2_rows{q}", [P, QUAD, W], F32, ctx) for q in range(4)]
    ps = [k.ps(f"l2_ps{q}", ctx) for q in range(4)]
    block = Path()
    idx_d = {s: ins[f"{s}_idx"].rearrange("(g p u) -> g p u", p=P, u=TILES) for s in ("dst", "src")}
    row_d = ins["src_idx"].rearrange("(g n) -> g n", n=GROUP)

    @block.sync
    def _(sp):
        def load(g, b):
            for s in ("src", "dst"):
                sp.dma_start(idx[s][b][:], idx_d[s][g]).then_inc(loaded[b], 16)
            sp.dma_start(row[b][:], row_d[g].partition_broadcast(P)).then_inc(loaded[b], 16)

        load(0, 0)
        load(1, 1)
        with sp.Fori(0, NITER) as i:
            for b in range(2):
                sp.wait_ge(gathered[2 * b], (i + 1) * (16 * QUAD))
                sp.wait_ge(gathered[2 * b + 1], (i + 1) * (16 * QUAD))
                sp.wait_ge(eq_done[b], i + 1)
                waited(sp, sp_tick)
                load(i * 2 + (2 + b), b)
        for b in range(2):
            sp.wait_ge(loaded[b], 16 * LOADS * (NITER + 1))

    @block.gpsimd
    def _(pool):
        def gather(q, u):
            c = QUAD * (q % 2) + u
            pool.indirect_dma_start(
                out=xg[q][:, u, :], out_offset=None, in_=t.x2[:],
                in_offset=bass.IndirectOffsetOnAxis(ap=idx["dst"][q // 2][:, c:c + 1], axis=0)).then_inc(gathered[q], 16)

        for n in (2, 3):
            pool.dma_start(rows_of(t.l2_src[n]), blank(t.zero, W)).then_inc(filled, 16)
        pool.wait_ge(filled, 32)
        for n in range(2):
            pool.dma_start(rows_of(t.l2_src[n]), blank(t.zero, W)).then_inc(added[n], 16)
        pool.wait_ge(loaded[0], 16 * LOADS)
        for q in range(2):
            for u in range(QUAD):
                gather(q, u)
        with pool.Fori(0, NITER) as i:
            for q in range(4):
                ahead = (q + 2) % 4
                pool.wait_ge(loaded[ahead // 2], (i + (2 if q >= 2 else 1)) * (16 * LOADS))
                pool.wait_ge(mul_done[ahead], i + (2 if q >= 2 else 1))
                waited(pool, tick)
                for u in range(QUAD):
                    gather(ahead, u)
                    if u == 0:
                        pool.wait_ge(rows_ready[q], i + 2)
                    n, c = u % 2, QUAD * (q % 2) + u
                    pool.wait_ge(added[n], (i * (2 * QUAD) + (q * (QUAD // 2) + u // 2 + 1)) * 16)
                    if u == 1:
                        pool.sem_inc(rows_free[(q - 1) % 4], 1)
                    else:
                        waited(pool, tick)
                    pool.indirect_dma_start(
                        out=t.l2_src[n][:], out_offset=bass.IndirectOffsetOnAxis(ap=to[q // 2][:, c:c + 1], axis=0),
                        in_=rows[q][:, u, :], in_offset=None, compute_op=ALU.add).then_inc(added[n], 16)
        for n in range(2):
            pool.wait_ge(added[n], 16 * (NG * TILES // 2 + 1))
        for q in range(2):
            pool.wait_ge(gathered[q], 16 * QUAD * (NITER + 1))

    @block.vector
    def _(dve):
        for q in range(4):
            dve.sem_inc(mul_done[q], 1)
        with dve.Fori(0, NITER) as i:
            for b in range(2):
                g = i * 2 + b
                dve.wait_ge(loaded[b], (i + 1) * (16 * LOADS))
                dve.wait_ge(mm_done[2 * b + 1], i + 1)
                dve.wait_ge(rows_free[2 * b + 1], i + 1)
                dve.tensor_copy(to[b][:], t.to_src[:, g, :])
                dve.tensor_tensor(eq[b][:], row[b][:].rearrange("p (e u) -> p u e", u=TILES),
                                  over(idx["src"][b][:].unsqueeze(2), [P, TILES, P]), ALU.is_equal).then_inc(eq_done[b], 1)
                for half in range(2):
                    q, c = 2 * b + half, QUAD * half
                    dve.wait_ge(gathered[q], (i + 1) * (16 * QUAD))
                    dve.wait_ge(mm_done[q], i + 1)
                    dve.tensor_copy(msg[q][:, :, D:W], t.wgt[:, g, c:c + QUAD].unsqueeze(2))
                    dve.tensor_tensor(msg[q][:, :, 0:D], xg[q][:],
                                      over(t.wgt[:, g, c:c + QUAD].unsqueeze(2), [P, QUAD, D]),
                                      ALU.mult).then_inc(mul_done[q], 1)

    @block.scalar
    def _(act):
        for q in range(4):
            act.sem_inc(rows_ready[q], 1)
        for q in range(3):
            act.sem_inc(rows_free[q], 1)
        with act.Fori(0, NITER) as i:
            for q in range(4):
                act.wait_ge(mm_done[q], i + 2)
                act.wait_ge(rows_free[q], i + 1)
                act.copy(rows[q][:], ps[q][:, 0:QUAD * W].rearrange("p (u w) -> p u w", w=W)).then_inc(rows_ready[q], 1)

    @block.tensor
    def _(pe):
        for q in range(4):
            pe.sem_inc(mm_done[q], 1)
        with pe.Fori(0, NITER) as i:
            for q in range(4):
                pe.wait_ge(mul_done[q], i + 2)
                pe.wait_ge(rows_ready[q], i + 1)
                for u in range(QUAD):
                    mm = pe.matmul(ps[q][:, u * W:(u + 1) * W], eq[q // 2][:, QUAD * (q % 2) + u, :],
                                   msg[q][:, u, :], start=True, stop=True)
                mm.then_inc(mm_done[q], 1)

    return block


def l2_edges_windows(k, t, ctx):
    nc, ins = k.nc, k.ins
    loaded, tick, sp_tick = k.sems("w2_loaded", 2), k.sem("w2_tick"), k.sem("w2_sp_tick")
    at_done, eq_done, fetched, mul_done, mm_done = (
        k.sem("w2_at"), k.sem("w2_eq"), k.sem("w2_fetched"), k.sem("w2_mul"), k.sem("w2_mm"))
    rows_ready, rows_free, added = k.sem("w2_rows"), k.sem("w2_rows_free"), k.sems("w2_added", 4)
    LOADS = 4
    TABLES = 4
    W = D + 1
    idx = [k.sb(f"w2_idx{b}", [P, TILES], I32, ctx) for b in range(2)]
    row_s = [k.sb(f"w2_row_s{b}", [P, GROUP], I32, ctx) for b in range(2)]
    row_d = [k.sb(f"w2_row_d{b}", [P, GROUP], I32, ctx) for b in range(2)]
    win = [k.sb(f"w2_win{b}", [P, D], F32, ctx) for b in range(2)]
    at, eq = ([k.sb(f"w2_{name}{b}", [P, TILES, P], F32, ctx) for b in range(2)] for name in ("at", "eq"))
    to = [k.sb(f"w2_to{b}", [P, TILES], I32, ctx) for b in range(2)]
    msg = [k.sb(f"w2_msg{b}", [P, TILES, W], F32, ctx) for b in range(2)]
    rows = [k.sb(f"w2_rows{b}", [P, TILES, W], F32, ctx) for b in range(2)]
    p_fetch = [k.ps(f"w2_p_fetch{b}", ctx) for b in range(2)]
    p_src = [k.ps(f"w2_p_src{b}", ctx) for b in range(2)]
    block = Path()
    idx_d = ins["src_idx"].rearrange("(g p u) -> g p u", p=P, u=TILES)
    rows_in = {s: ins[f"{s}_idx"].rearrange("(g n) -> g n", n=GROUP) for s in ("dst", "src")}

    @block.sync
    def _(sp):
        def load(g, b):
            w = sp.value_load(t.base[0:1, bass.ds(g, 1)], min_val=0, max_val=N)
            sp.dma_start(idx[b][:], idx_d[g]).then_inc(loaded[b], 16)
            sp.dma_start(row_d[b][:], rows_in["dst"][g].partition_broadcast(P)).then_inc(loaded[b], 16)
            sp.dma_start(win[b][:], t.x2[bass.ds(w, P), :]).then_inc(loaded[b], 16)
            sp.dma_start(row_s[b][:], rows_in["src"][g].partition_broadcast(P)).then_inc(loaded[b], 16)

        load(0, 0)
        load(1, 1)
        with sp.Fori(0, NITER) as i:
            for b in range(2):
                g = i * 2 + b
                sp.wait_ge(eq_done, g + 1)
                sp.wait_ge(fetched, g + 1)
                waited(sp, sp_tick)
                load(g + 2, b)
        for b in range(2):
            sp.wait_ge(loaded[b], 16 * LOADS * (NITER + 1))

    @block.gpsimd
    def _(pool):
        for n in range(TABLES):
            pool.dma_start(rows_of(t.l2_src[n]), blank(t.zero, W)).then_inc(added[n], 16)
        with pool.Fori(0, NITER) as i:
            for b in range(2):
                g = i * 2 + b
                pool.wait_ge(rows_ready, g + 3)
                for u in range(TILES):
                    n = u % TABLES
                    pool.wait_ge(added[n], (g * (TILES // TABLES) + (u // TABLES + 1)) * 16)
                    if u == TABLES - 1:
                        pool.sem_inc(rows_free, 1)
                    else:
                        waited(pool, tick)
                    pool.indirect_dma_start(
                        out=t.l2_src[n][:], out_offset=bass.IndirectOffsetOnAxis(ap=to[b][:, u:u + 1], axis=0),
                        in_=rows[b][:, u, :], in_offset=None, compute_op=ALU.add).then_inc(added[n], 16)
        for n in range(TABLES):
            pool.wait_ge(added[n], 16 * (NG * TILES // TABLES + 1))

    @block.vector
    def _(dve):
        with dve.Fori(0, NITER) as i:
            for b in range(2):
                g = i * 2 + b
                full = [P, TILES, P]
                dve.wait_ge(loaded[b], (i + 1) * (16 * LOADS))
                dve.wait_ge(mm_done, g + 1)
                dve.tensor_tensor(at[b][:], row_d[b][:].rearrange("p (e u) -> p u e", u=TILES),
                                  over(t.node[:, bass.ds(g, 1)].unsqueeze(2), full), ALU.is_equal).then_inc(at_done, 1)
                dve.tensor_tensor(eq[b][:], row_s[b][:].rearrange("p (e u) -> p u e", u=TILES),
                                  over(idx[b][:].unsqueeze(2), full), ALU.is_equal).then_inc(eq_done, 1)
                w = t.wgt[:, bass.ds(g, 1), :].rearrange("p g u -> p u g")
                dve.tensor_copy(msg[b][:, :, D:W], w)
                dve.wait_ge(fetched, g + 1)
                dve.tensor_tensor(msg[b][:, :, 0:D], p_fetch[b][:, 0:TILES * D].rearrange("p (u d) -> p u d", d=D),
                                  over(w, [P, TILES, D]), ALU.mult).then_inc(mul_done, 1)

    @block.scalar
    def _(act):
        act.sem_inc(rows_ready, 2)
        act.sem_inc(rows_free, 1)
        with act.Fori(0, NITER) as i:
            for b in range(2):
                g = i * 2 + b
                act.wait_ge(mm_done, g + 3)
                act.wait_ge(rows_free, g + 1)
                act.copy(to[b][:], t.to_src[:, bass.ds(g, 1), :].rearrange("p g u -> p (g u)"))
                act.copy(rows[b][:], p_src[b][:, 0:TILES * W].rearrange("p (u w) -> p u w", w=W)).then_inc(rows_ready, 1)

    @block.tensor
    def _(pe):
        pe.sem_inc(mm_done, 2)

        def fetch(b, nth):
            pe.wait_ge(at_done, nth)
            for u in range(TILES):
                mm = pe.matmul(p_fetch[b][:, u * D:(u + 1) * D], at[b][:, u, :], win[b][:], start=True, stop=True)
            mm.then_inc(fetched, 1)

        with pe.Fori(0, NITER) as i:
            for b in range(2):
                g = i * 2 + b
                fetch(b, g + 1)
                pe.wait_ge(mul_done, g + 1)
                pe.wait_ge(rows_ready, g + 1)
                for u in range(TILES):
                    mm = pe.matmul(p_src[b][:, u * W:(u + 1) * W], eq[b][:, u, :], msg[b][:, u, :], start=True, stop=True)
                mm.then_inc(mm_done, 1)

    return block


def turn_nodes(k, tag, t, x, xT):
    nc = k.nc
    picked, turned, copied = k.sem(f"{tag}_picked"), k.sem(f"{tag}_turned"), k.sem(f"{tag}_copied")
    with ExitStack() as ctx:
        part = k.sb(f"{tag}_part", [P, CH, D], F32, ctx)
        ps = k.ps(f"{tag}_ps", ctx)
        block = ctx.enter_context(nc.Block())

        @block.vector
        def _(dve):
            with dve.Fori(0, NB // CH) as c:
                dve.wait_ge(turned, c + 1)
                dve.tensor_copy(part[:], x[:, bass.ds(c * CH, CH), :]).then_inc(picked, 1)

        @block.tensor
        def _(pe):
            pe.sem_inc(turned, 1)
            with pe.Fori(0, NB // CH) as c:
                pe.wait_ge(picked, c + 1)
                pe.wait_ge(copied, c + 1)
                for b in range(CH):
                    mm = pe.transpose(ps[0:D, b * P:(b + 1) * P], part[:, b, :], t.ident[:])
                mm.then_inc(turned, 1)

        @block.scalar
        def _(act):
            act.sem_inc(copied, 1)
            with act.Fori(0, NB // CH) as c:
                act.wait_ge(turned, c + 2)
                act.copy(xT[:, bass.ds(c * (CH * P), CH * P)], ps[0:D, 0:CH * P]).then_inc(copied, 1)


def l3_scores(k, t, xT, a_all):
    nc, ins = k.nc, k.ins
    picked = k.sem("l3s_picked")
    loaded, dve_step, mm_done, copied, stored, done = (
        k.sem("l3s_loaded"), k.sem("l3s_dve"), k.sem("l3s_mm"), k.sem("l3s_copied"), k.sem("l3s_stored"), k.sem("l3s_done"))
    with ExitStack() as ctx:
        wg = k.sb("l3s_wg", [D, HEADS, D], F32, ctx)
        att = k.sb("l3s_att", [D, 2, HEADS, D], F32, ctx)
        va = k.sb("l3s_va", [D, 2, HEADS], F32, ctx)
        part = k.sb("l3s_part", [D, CH * P], F32, ctx)
        x_a = k.sb("l3s_x_a", [P, NB, D + HEADS], F32, ctx)
        ps = k.ps("l3s_ps", ctx)
        block = ctx.enter_context(nc.Block())

        @block.sync
        def _(sp):
            sp.dma_start(wg[:], ins["L3_W_gat"].rearrange("d (h c) -> d h c", c=D)).then_inc(loaded, 16)
            for n, name in enumerate(("att_src", "att_dst")):
                sp.dma_start(att[:, n].rearrange("d h c -> d (h c)"),
                             ins[f"L3_{name}"].rearrange("h c -> (h c)").partition_broadcast(D)).then_inc(loaded, 16)
            sp.wait_ge(done, 1)
            sp.dma_start(rows_of(t.x3), x_a[:]).then_inc(stored, 16)
            sp.wait_ge(stored, 16)

        @block.vector
        def _(dve):
            step = chained(dve_step)
            dve.wait_ge(loaded, 48)
            step(dve, dve.tensor_tensor(att[:], att[:], over(wg[:].unsqueeze(1), [D, 2, HEADS, D]), ALU.mult))
            step(dve, dve.tensor_reduce(va[:], att[:], AX.X, ALU.add))
            dve.sem_inc(copied, 1)
            with dve.Fori(0, NB // CH) as c:
                dve.wait_ge(mm_done, c + 2)
                dve.tensor_copy(a_all[:, bass.ds(c * CH, CH), :],
                                ps[:, 0:CH * 16].rearrange("p (b a) -> p b a", b=CH)).then_inc(copied, 1)
            dve.wait_ge(copied, NB // CH + 1)
            step(dve, dve.tensor_copy(x_a[:, :, 0:D], t.x[:]))
            step(dve, dve.tensor_copy(x_a[:, :, D:D + HEADS], a_all[:, :, 0:HEADS]))
            dve.sem_inc(done, 1)

        @block.scalar
        def _(act):
            act.sem_inc(mm_done, 1)
            with act.Fori(0, NB // CH) as c:
                act.wait_ge(mm_done, c + 1)
                act.copy(part[:], xT[:, bass.ds(c * (CH * P), CH * P)]).then_inc(picked, 1)

        @block.tensor
        def _(pe):
            pe.wait_ge(dve_step, 2)
            with pe.Fori(0, NB // CH) as c:
                pe.wait_ge(copied, c + 1)
                pe.wait_ge(picked, c + 1)
                for b in range(CH):
                    mm = pe.matmul(ps[:, b * 16:(b + 1) * 16], part[:, b * P:(b + 1) * P],
                                   va[:].rearrange("d s h -> d (s h)"), start=True, stop=True)
                mm.then_inc(mm_done, 1)


def l3_max_general(k, t, ctx):
    nc, ins = k.nc, k.ins
    loaded, tick, sp_tick = k.sems("l3m_loaded", 2), k.sem("l3m_tick"), k.sem("l3m_sp_tick")
    gathered, kept, spread = k.sems("l3m_gathered", 4), k.sems("l3m_kept", 4), k.sems("l3m_spread", 4)
    read, put = k.sem("l3m_read"), k.sems("l3m_put", QUAD)
    eq_done, diag_done, mm_done, red_done, new_done = (
        k.sems("l3m_eq", 2), k.sem("l3m_diag"), k.sem("l3m_mm"), k.sem("l3m_red"), k.sem("l3m_new"))
    consts, dve_step = k.sem("l3m_consts"), k.sem("l3m_step")
    LOADS = 3
    W = D + HEADS
    idx = {s: [k.sb(f"l3m_{s}_idx{b}", [P, TILES], I32, ctx) for b in range(2)] for s in ("dst", "src")}
    row = [k.sb(f"l3m_row{b}", [P, GROUP], I32, ctx) for b in range(2)]
    neq = [k.sb(f"l3m_neq{b}", [P, TILES, P], BF16, ctx) for b in range(2)]
    to = [k.sb(f"l3m_to{b}", [P, TILES], I32, ctx) for b in range(2)]
    ones = k.sb("l3m_ones", [P, P], F32, ctx)
    low = k.sb("l3m_low", [P, P], BF16, ctx)
    xg = [k.sb(f"l3m_xg{q}", [P, QUAD, W], F32, ctx) for q in range(4)]
    diag = [k.sb(f"l3m_diag{n}", [P, HEADS, P], F32, ctx) for n in range(2)]
    red = k.sb("l3m_red", [P, QUAD, HEADS], F32, ctx)
    cur = k.sb("l3m_cur", [P, QUAD, HEADS], F32, ctx)
    new = k.sb("l3m_new", [P, QUAD, HEADS], F32, ctx)
    ps = [k.ps(f"l3m_ps{n}", ctx, (P, HEADS, P)) for n in range(2)]
    block = Path()
    idx_d = {s: ins[f"{s}_idx"].rearrange("(g p u) -> g p u", p=P, u=TILES) for s in ("dst", "src")}
    row_d = ins["dst_idx"].rearrange("(g n) -> g n", n=GROUP)

    @block.sync
    def _(sp):
        def load(g, b):
            for s in ("src", "dst"):
                sp.dma_start(idx[s][b][:], idx_d[s][g]).then_inc(loaded[b], 16)
            sp.dma_start(row[b][:], row_d[g].partition_broadcast(P)).then_inc(loaded[b], 16)

        load(0, 0)
        load(1, 1)
        with sp.Fori(0, NITER) as i:
            for b in range(2):
                sp.wait_ge(gathered[2 * b], (i + 1) * (16 * QUAD))
                sp.wait_ge(gathered[2 * b + 1], (i + 1) * (16 * QUAD))
                sp.wait_ge(eq_done[b], i + 1)
                waited(sp, sp_tick)
                load(i * 2 + (2 + b), b)
        for b in range(2):
            sp.wait_ge(loaded[b], 16 * LOADS * (NITER + 1))

    @block.gpsimd
    def _(pool):
        def gather(q, u):
            c = QUAD * (q % 2) + u
            pool.indirect_dma_start(
                out=xg[q][:, u, :], out_offset=None, in_=t.x3[:],
                in_offset=bass.IndirectOffsetOnAxis(ap=idx["src"][q // 2][:, c:c + 1], axis=0)).then_inc(gathered[q], 16)

        for u in range(QUAD):
            pool.dma_start(rows_of(t.l3_max[u]), blank(t.lowest, HEADS)).then_inc(put[u], 16)
        pool.wait_ge(loaded[0], 16 * LOADS)
        for q in range(2):
            for u in range(QUAD):
                gather(q, u)
        with pool.Fori(0, NITER) as i:
            for q in range(4):
                b, ahead = q // 2, (q + 2) % 4
                pool.wait_ge(eq_done[b], i + 1)
                for u in range(QUAD):
                    c = QUAD * (q % 2) + u
                    pool.wait_ge(put[u], (i * 4 + (q + 1)) * 16)
                    waited(pool, tick)
                    pool.indirect_dma_start(
                        out=cur[:, u, :], out_offset=None, in_=t.l3_max[u][:],
                        in_offset=bass.IndirectOffsetOnAxis(ap=to[b][:, c:c + 1], axis=0)).then_inc(read, 16)
                pool.wait_ge(loaded[ahead // 2], (i + (2 if q >= 2 else 1)) * (16 * LOADS))
                pool.wait_ge(spread[ahead], i + (2 if q >= 2 else 1))
                pool.wait_ge(kept[ahead], i + (2 if q >= 2 else 1))
                waited(pool, tick)
                for u in range(QUAD):
                    gather(ahead, u)
                pool.wait_ge(new_done, i * 4 + (q + 1))
                waited(pool, tick)
                for u in range(QUAD):
                    c = QUAD * (q % 2) + u
                    pool.indirect_dma_start(
                        out=t.l3_max[u][:], out_offset=bass.IndirectOffsetOnAxis(ap=to[b][:, c:c + 1], axis=0),
                        in_=new[:, u, :], in_offset=None).then_inc(put[u], 16)
        for u in range(QUAD):
            pool.wait_ge(put[u], 16 * (4 * NITER + 1))
        for q in range(2):
            pool.wait_ge(gathered[q], 16 * QUAD * (NITER + 1))

    @block.vector
    def _(dve):
        step = chained(consts)
        step(dve, dve.memset(ones[:], 1.0))
        step(dve, dve.tensor_scalar(low[:], t.ident[:], LOWEST, None, ALU.mult))
        for q in range(4):
            dve.sem_inc(spread[q], 1)
        dve.sem_inc(red_done, 2)
        with dve.Fori(0, NITER) as i:
            for q in range(4):
                b = q // 2
                if q % 2 == 0:
                    dve.wait_ge(loaded[b], (i + 1) * (16 * LOADS))
                    dve.wait_ge(mm_done, i * 16 + (q * QUAD + 2))
                    dve.tensor_copy(to[b][:], t.to_dst[:, i * 2 + b, :])
                    dve.tensor_tensor(neq[b][:], row[b][:].rearrange("p (e u) -> p u e", u=TILES),
                                      over(idx["dst"][b][:].unsqueeze(2), [P, TILES, P]),
                                      ALU.not_equal).then_inc(eq_done[b], 1)
                dve.wait_ge(gathered[q], (i + 1) * (16 * QUAD))

                def spread_out(u):
                    n = i * 16 + (q * QUAD + u)
                    dve.wait_ge(mm_done, n + 1)
                    ins_ = dve.tensor_tensor(diag[u % 2][:], over(t.ident[:].unsqueeze(1), [P, HEADS, P]),
                                             over(xg[q][:, u, D:W].unsqueeze(2), [P, HEADS, P]), ALU.mult)
                    ins_.then_inc(diag_done, 1)

                def reduce(u):
                    dve.wait_ge(mm_done, i * 16 + (q * QUAD + u + 3))
                    dve.tensor_reduce(red[:, u, :], ps[u % 2][:], AX.X, ALU.max).then_inc(red_done, 1)

                spread_out(0)
                spread_out(1)
                for u in range(2, QUAD):
                    reduce(u - 2)
                    spread_out(u)
                dve.wait_ge(diag_done, i * 16 + (q * QUAD + QUAD))
                dve.sem_inc(spread[q], 1)
                reduce(QUAD - 2)
                reduce(QUAD - 1)
                dve.wait_ge(red_done, i * 16 + (q * QUAD + QUAD + 2))
                dve.wait_ge(read, (i * 4 + (q + 1)) * (16 * QUAD))
                dve.tensor_tensor(new[:], cur[:], red[:], ALU.max).then_inc(new_done, 1)

    @block.scalar
    def _(act):
        for q in range(4):
            act.sem_inc(kept[q], 1)
        with act.Fori(0, NITER) as i:
            for q in range(4):
                act.wait_ge(gathered[q], (i + 1) * (16 * QUAD))
                act.copy(t.x_edge[:, bass.ds(i * 16 + q * QUAD, QUAD), :], xg[q][:]).then_inc(kept[q], 1)

    @block.tensor
    def _(pe):
        pe.wait_ge(consts, 2)
        pe.sem_inc(mm_done, 2)
        with pe.Fori(0, NITER) as i:
            for q in range(4):
                for u in range(QUAD):
                    n = i * 16 + (q * QUAD + u)
                    pe.wait_ge(diag_done, n + 1)
                    pe.wait_ge(red_done, n + 1)
                    for h in range(0, HEADS, 4):
                        pe.matmul(ps[u % 2][:, h:h + 4, :], ones[:], diag[u % 2][:, h:h + 4, :],
                                  start=True, stop=False)
                        mm = pe.matmul(ps[u % 2][:, h:h + 4, :], neq[q // 2][:, QUAD * (q % 2) + u, :],
                                       over(low[:].unsqueeze(1), [P, 4, P]), start=False, stop=True)
                    mm.then_inc(mm_done, 1)

    return block


def l3_max_windows(k, t, ctx):
    nc, ins = k.nc, k.ins
    loaded, tick, sp_tick, w_tick = k.sems("m_loaded", 2), k.sem("m_tick"), k.sem("m_sp_tick"), k.sem("m_w_tick")
    gathered, kept, split_done = k.sems("m_gathered", 2), k.sems("m_kept", 2), k.sems("m_split", 2)
    neq_done, turned, copied, mm_done, red_done = (
        k.sem("m_neq"), k.sem("m_turned"), k.sem("m_copied"), k.sem("m_mm"), k.sem("m_red"))
    read, new_done, put, filled = k.sem("m_read"), k.sem("m_new"), k.sem("m_put"), k.sem("m_filled")
    consts, dve_step = k.sem("m_consts"), k.sem("m_step")
    LOADS = 2
    W = D + HEADS
    PARTS = 3
    K = PARTS * HEADS
    idx = [k.sb(f"m_idx{b}", [P, TILES], I32, ctx) for b in range(2)]
    row = [k.sb(f"m_row{b}", [P, GROUP], I32, ctx) for b in range(2)]
    neq = [k.sb(f"m_neq{b}", [P, TILES, P], BF16, ctx) for b in range(2)]
    low, ident = k.sb("m_low", [P, P], BF16, ctx), k.sb("m_ident", [P, P], BF16, ctx)
    pick_f, pick = k.sb("m_pick_f", [K, HEADS], F32, ctx), k.sb("m_pick", [P, HEADS, P], BF16, ctx)
    xg = [k.sb(f"m_xg{b}", [P, TILES, W], F32, ctx) for b in range(2)]
    rest = k.sb("m_rest", [P, 2, TILES, HEADS], F32, ctx)
    parts = [k.sb(f"m_parts{b}", [P, TILES, PARTS, HEADS], BF16, ctx) for b in range(2)]
    aT = [k.sb(f"m_aT{b}", [P, GROUP], BF16, ctx) for b in range(2)]
    red = [k.sb(f"m_red{b}", [P, HEADS], F32, ctx) for b in range(2)]
    cur = [k.sb(f"m_cur{b}", [P, HEADS], F32, ctx) for b in range(2)]
    p_turn = k.ps("m_turn", ctx, (K, GROUP), BF16)
    ps = [k.ps(f"m_ps{n}", ctx, (P, 2, 512)) for n in range(2)]
    block = Path()
    idx_d = ins["src_idx"].rearrange("(g p u) -> g p u", p=P, u=TILES)
    row_d = ins["dst_idx"].rearrange("(g n) -> g n", n=GROUP)

    @block.sync
    def _(sp):
        def load(g, b):
            sp.dma_start(idx[b][:], idx_d[g]).then_inc(loaded[b], 16)
            sp.dma_start(row[b][:], row_d[g].partition_broadcast(P)).then_inc(loaded[b], 16)

        sp.dma_start(pick_f[:], ins["pick"]).then_inc(filled, 16)
        load(0, 0)
        load(1, 1)
        for u in range(QUAD):
            sp.dma_start(rows_of(t.l3_max[u]), blank(t.lowest, HEADS)).then_inc(filled, 16)
        sp.wait_ge(filled, 16 * (QUAD + 1))
        sp.sem_inc(put, 16)
        sp.wait_ge(gathered[0], 16 * TILES)
        sp.wait_ge(neq_done, 1)
        load(2, 0)
        with sp.Fori(0, NITER) as i:
            for b in range(2):
                g = i * 2 + b
                w = sp.value_load(t.base[0:1, bass.ds(g, 1)], min_val=0, max_val=N)
                sp.wait_ge(put, (g + 1) * 16)
                waited(sp, sp_tick)
                sp.dma_start(cur[b][:], t.l3_max[0][bass.ds(w, P), :]).then_inc(read, 16)
                sp.wait_ge(gathered[1 - b], (i + (b + 1)) * (16 * TILES))
                waited(sp, sp_tick)
                sp.wait_ge(neq_done, g + 2)
                waited(sp, sp_tick)
                load(g + 3, 1 - b)
                sp.wait_ge(new_done, g + 1)
                waited(sp, sp_tick)
                sp.dma_start(t.l3_max[0][bass.ds(w, P), :], red[b][:]).then_inc(put, 16)
        sp.wait_ge(put, 16 * (NG + 1))
        for b in range(2):
            sp.wait_ge(loaded[b], 16 * LOADS * (NITER + 2 - b))

    @block.gpsimd
    def _(pool):
        def gather(b):
            for u in range(TILES):
                pool.indirect_dma_start(
                    out=xg[b][:, u, :], out_offset=None, in_=t.x3[:],
                    in_offset=bass.IndirectOffsetOnAxis(ap=idx[b][:, u:u + 1], axis=0)).then_inc(gathered[b], 16)

        for b in range(2):
            pool.wait_ge(loaded[b], 16 * LOADS)
            gather(b)
        with pool.Fori(0, NITER) as i:
            for b in range(2):
                pool.wait_ge(loaded[b], (i + 2) * (16 * LOADS))
                pool.wait_ge(split_done[b], i + 1)
                pool.wait_ge(kept[b], i + 1)
                waited(pool, tick)
                gather(b)
        for b in range(2):
            pool.wait_ge(gathered[b], 16 * TILES * (NITER + 1))

    @block.vector
    def _(dve):
        step = chained(consts)
        dve.wait_ge(filled, 16 * (QUAD + 1))
        step(dve, dve.tensor_scalar(low[:], t.ident[:], LOWEST, None, ALU.mult))
        step(dve, dve.tensor_copy(ident[:], t.ident[:]))
        step(dve, dve.memset(pick[:], 0.0))
        step(dve, dve.tensor_copy(pick[0:K], over(pick_f[:].unsqueeze(2), [K, HEADS, P])))
        for b in range(2):
            step(dve, dve.memset(aT[b][:], 0.0))
        STEPS = 4

        def prepare(g, b, turn, count):
            def step(ins_):
                count[0] += 1
                ins_.then_inc(dve_step, 1)
                dve.wait_ge(dve_step, g * STEPS + count[0])

            a, pt = xg[b][:, :, D:W], parts[b]
            dve.wait_ge(gathered[b], turn * (16 * TILES))
            step(dve.tensor_copy(pt[:, :, 0, :], a))
            step(dve.tensor_tensor(rest[:, 0], a, pt[:, :, 0, :], ALU.subtract))
            step(dve.tensor_copy(pt[:, :, 1, :], rest[:, 0]))
            step(dve.tensor_tensor(rest[:, 1], rest[:, 0], pt[:, :, 1, :], ALU.subtract))
            dve.tensor_copy(pt[:, :, 2, :], rest[:, 1]).then_inc(split_done[b], 1)

        prepare(0, 0, 1, [0])
        with dve.Fori(0, NITER) as i:
            for b in range(2):
                g = i * 2 + b
                for h in range(HEADS):
                    dve.wait_ge(mm_done, g * HEADS + (h + 1))
                    dve.tensor_reduce(red[b][:, h:h + 1], ps[h % 2][:].rearrange("p a e -> p (a e)"), AX.X,
                                      ALU.max).then_inc(red_done, 1)
                    if h == 2:
                        prepare(g + 1, 1 - b, i + (b + 1), [0])
                dve.wait_ge(red_done, (g + 1) * HEADS + 2)
                dve.wait_ge(read, (g + 1) * 16)
                dve.tensor_tensor(red[b][:], red[b][:], cur[b][:], ALU.max).then_inc(new_done, 1)

    @block.scalar
    def _(act):
        def differ(g, b, turn):
            act.wait_ge(loaded[b], turn * (16 * LOADS))
            act.activation(neq[b][:].rearrange("p u e -> p e u"), row[b][:].rearrange("p (e u) -> p e u", u=TILES),
                           ACT.Square, bias=t.node_neg[:, bass.ds(g, 1)]).then_inc(neq_done, 1)

        differ(0, 0, 1)
        act.wait_ge(consts, 6)
        act.wait_ge(turned, 1)
        act.copy(aT[0][0:K], p_turn[:]).then_inc(copied, 1)
        with act.Fori(0, NITER) as i:
            for b in range(2):
                g = i * 2 + b
                act.wait_ge(gathered[b], (i + 1) * (16 * TILES))
                act.copy(t.x_edge[:, bass.ds(g * TILES, TILES), :], xg[b][:]).then_inc(kept[b], 1)
                act.wait_ge(mm_done, g * HEADS + 1)
                differ(g + 1, 1 - b, i + (b + 1))
                act.wait_ge(turned, g + 2)
                act.copy(aT[1 - b][0:K], p_turn[:]).then_inc(copied, 1)

    @block.tensor
    def _(pe):
        pe.wait_ge(consts, 6)
        pe.sem_inc(red_done, 2)

        def turn(b, nth):
            pe.wait_ge(split_done[b], nth)
            for u in range(TILES):
                mm = pe.transpose(p_turn[:, u * P:(u + 1) * P], parts[b][:, u].rearrange("p a h -> p (a h)"), ident[:])
            mm.then_inc(turned, 1)

        turn(0, 1)
        with pe.Fori(0, NITER) as i:
            for b in range(2):
                g = i * 2 + b
                pe.wait_ge(copied, g + 1)
                pe.wait_ge(neq_done, g + 1)
                for h in range(HEADS):
                    if h == 5:
                        turn(1 - b, i + (b + 1))
                    pe.wait_ge(red_done, g * HEADS + (h + 1))
                    for half in range(2):
                        pe.matmul(ps[h % 2][:, half, :], pick[:, h, :], aT[b][:, half * 512:(half + 1) * 512],
                                  start=True, stop=False)
                        mm = pe.matmul(ps[h % 2][:, half, :], low[:],
                                       neq[b][:, half * 4:half * 4 + 4, :].rearrange("p u e -> p (u e)"),
                                       start=False, stop=True)
                    mm.then_inc(mm_done, 1)

    return block


def l3_bounds(k, t, a_all, self_w):
    nc = k.nc
    loaded, dve_step, done, stored, exp_done = (
        k.sem("l3b_loaded"), k.sem("l3b_dve"), k.sem("l3b_done"), k.sem("l3b_stored"), k.sem("l3b_exp"))
    with ExitStack() as ctx:
        mx = [k.sb(f"l3b_mx{u}", [P, NB, HEADS], F32, ctx) for u in range(QUAD)]
        dm = k.sb("l3b_dm", [P, NB, 2 * HEADS], F32, ctx)
        dm_parts = k.sb("l3b_dm_parts", [P, NB, 3, 2 * HEADS], BF16, ctx)
        rest = k.sb("l3b_rest", [P, 2, NB, 2 * HEADS], F32, ctx)
        block = ctx.enter_context(nc.Block())

        @block.sync
        def _(sp):
            for u in range(QUAD):
                sp.dma_start(mx[u][:], rows_of(t.l3_max[u])).then_inc(loaded, 16)
            sp.wait_ge(done, 1)
            sp.dma_start(rows_of(t.l3_dm), dm[:]).then_inc(stored, 16)
            sp.dma_start(rows_of(t.l3_dm_parts), dm_parts[:].rearrange("p j a d -> p j (a d)")).then_inc(stored, 16)
            sp.wait_ge(stored, 32)

        @block.vector
        def _(dve):
            step = chained(dve_step)
            dve.wait_ge(loaded, 16 * QUAD)
            step(dve, dve.tensor_tensor(mx[0][:], mx[0][:], mx[1][:], ALU.max))
            step(dve, dve.tensor_tensor(mx[2][:], mx[2][:], mx[3][:], ALU.max))
            step(dve, dve.tensor_tensor(mx[0][:], mx[0][:], mx[2][:], ALU.max))
            step(dve, dve.tensor_tensor(mx[0][:], mx[0][:], a_all[:, :, 0:HEADS], ALU.max))
            step(dve, dve.tensor_tensor(mx[0][:], mx[0][:], a_all[:, :, HEADS:2 * HEADS], ALU.add))
            step(dve, dve.tensor_copy(dm[:, :, 0:HEADS], a_all[:, :, HEADS:2 * HEADS]))
            step(dve, dve.scalar_tensor_tensor(out=dm[:, :, HEADS:2 * HEADS], in0=mx[0][:], scalar=0.2, in1=mx[0][:],
                                               op0=ALU.mult, op1=ALU.max))
            step(dve, dve.tensor_tensor(mx[1][:], a_all[:, :, 0:HEADS], a_all[:, :, HEADS:2 * HEADS], ALU.add))
            step(dve, dve.scalar_tensor_tensor(out=mx[1][:], in0=mx[1][:], scalar=0.2, in1=mx[1][:],
                                               op0=ALU.mult, op1=ALU.max))
            step(dve, dve.tensor_tensor(mx[1][:], mx[1][:], dm[:, :, HEADS:2 * HEADS], ALU.subtract))
            in_parts(dve, step, dm[:], dm_parts, rest)
            dve.sem_inc(done, 1)

        @block.scalar
        def _(act):
            act.wait_ge(done, 1)
            act.activation(self_w[:], mx[1][:], ACT.Exp).then_inc(exp_done, 1)
            act.wait_ge(exp_done, 1)


def l3_edges_general(k, t, ctx):
    nc, ins = k.nc, k.ins
    loaded, tick, sp_tick = k.sems("l3_loaded", 2), k.sem("l3_tick"), k.sem("l3_sp_tick")
    gathered, used, mm_done = k.sems("l3_gathered", 4), k.sems("l3_used", 4), k.sems("l3_mm", 4)
    rows_ready, rows_free, eq_done = k.sems("l3_rows", 4), k.sems("l3_rows_free", 4), k.sems("l3_eq", 2)
    exp_done, msg_done, dve_step = k.sem("l3_exp"), k.sem("l3_msg"), k.sem("l3_dve")
    added = k.sem("l3_added")
    LOADS = 2
    W = HEADS * D + HEADS
    STEPS = 2
    idx = [k.sb(f"l3_idx{b}", [P, TILES], I32, ctx) for b in range(2)]
    row = [k.sb(f"l3_row{b}", [P, GROUP], I32, ctx) for b in range(2)]
    eq = [k.sb(f"l3_eq{b}", [P, TILES, P], F32, ctx) for b in range(2)]
    to = [k.sb(f"l3_to{b}", [P, TILES], I32, ctx) for b in range(2)]
    dm = [k.sb(f"l3_dm{q}", [P, QUAD, 2 * HEADS], F32, ctx) for q in range(4)]
    al = k.sb("l3_al", [P, QUAD, HEADS], F32, ctx)
    ea = k.sb("l3_ea", [P, QUAD, HEADS], F32, ctx)
    msg = [k.sb(f"l3_msg{n}", [P, QUAD, W], F32, ctx) for n in range(2)]
    rows = [k.sb(f"l3_rows{q}", [P, QUAD, W], F32, ctx) for q in range(4)]
    ps = [k.ps(f"l3_ps{n}", ctx, (P, QUAD, 512)) for n in range(2)]
    block = Path()
    idx_d = ins["dst_idx"].rearrange("(g p u) -> g p u", p=P, u=TILES)
    row_d = ins["dst_idx"].rearrange("(g n) -> g n", n=GROUP)

    @block.sync
    def _(sp):
        def load(g, b):
            sp.dma_start(idx[b][:], idx_d[g]).then_inc(loaded[b], 16)
            sp.dma_start(row[b][:], row_d[g].partition_broadcast(P)).then_inc(loaded[b], 16)

        load(0, 0)
        load(1, 1)
        with sp.Fori(0, NITER) as i:
            for b in range(2):
                sp.wait_ge(gathered[2 * b], (i + 1) * (16 * QUAD))
                sp.wait_ge(gathered[2 * b + 1], (i + 1) * (16 * QUAD))
                sp.wait_ge(eq_done[b], i + 1)
                waited(sp, sp_tick)
                load(i * 2 + (2 + b), b)
        for b in range(2):
            sp.wait_ge(loaded[b], 16 * LOADS * (NITER + 1))

    @block.gpsimd
    def _(pool):
        def gather(q, u):
            c = QUAD * (q % 2) + u
            pool.indirect_dma_start(
                out=dm[q][:, u, :], out_offset=None, in_=t.l3_dm[:],
                in_offset=bass.IndirectOffsetOnAxis(ap=idx[q // 2][:, c:c + 1], axis=0)).then_inc(gathered[q], 16)

        pool.dma_start(rows_of(t.l3_dst), blank(t.zero, W)).then_inc(added, 16)
        pool.wait_ge(loaded[0], 16 * LOADS)
        for q in range(2):
            for u in range(QUAD):
                gather(q, u)
        with pool.Fori(0, NITER) as i:
            for q in range(4):
                ahead = (q + 2) % 4
                pool.wait_ge(loaded[ahead // 2], (i + (2 if q >= 2 else 1)) * (16 * LOADS))
                pool.wait_ge(used[ahead], i + (2 if q >= 2 else 1))
                waited(pool, tick)
                for u in range(QUAD):
                    gather(ahead, u)
                    if u == 0:
                        pool.wait_ge(rows_ready[q], i + 2)
                    c = QUAD * (q % 2) + u
                    pool.wait_ge(added, (i * (4 * QUAD) + (q * QUAD + u + 1)) * 16)
                    if u == 0:
                        pool.sem_inc(rows_free[(q - 1) % 4], 1)
                    else:
                        waited(pool, tick)
                    pool.indirect_dma_start(
                        out=t.l3_dst[:], out_offset=bass.IndirectOffsetOnAxis(ap=to[q // 2][:, c:c + 1], axis=0),
                        in_=rows[q][:, u, :], in_offset=None, compute_op=ALU.add).then_inc(added, 16)
        pool.wait_ge(added, 16 * (NG * TILES + 1))
        for q in range(2):
            pool.wait_ge(gathered[q], 16 * QUAD * (NITER + 1))

    @block.vector
    def _(dve):
        for q in range(4):
            dve.sem_inc(used[q], 1)
        dve.sem_inc(msg_done, 1)
        with dve.Fori(0, NITER) as i:
            for q in range(4):
                b = q // 2
                count = [0]

                def step(ins_):
                    count[0] += 1
                    ins_.then_inc(dve_step, 1)
                    dve.wait_ge(dve_step, i * (4 * 3) + (q * 3 + count[0]))

                x = t.x_edge[:, bass.ds(i * 16 + q * QUAD, QUAD), :]
                dve.wait_ge(gathered[q], (i + 1) * (16 * QUAD))
                step(dve.tensor_tensor(al[:], x[:, :, D:D + HEADS], dm[q][:, :, 0:HEADS], ALU.add))
                step(dve.scalar_tensor_tensor(out=al[:], in0=al[:], scalar=0.2, in1=al[:], op0=ALU.mult, op1=ALU.max))
                step(dve.tensor_tensor(al[:], al[:], dm[q][:, :, HEADS:2 * HEADS], ALU.subtract))
                dve.sem_inc(used[q], 1)
                if q % 2 == 0:
                    dve.wait_ge(loaded[b], (i + 1) * (16 * LOADS))
                    dve.wait_ge(mm_done[2 * b + 1], i + 1)
                    dve.wait_ge(rows_free[2 * b + 1], i + 1)
                    dve.tensor_copy(to[b][:], t.to_dst[:, i * 2 + b, :])
                    dve.tensor_tensor(eq[b][:], row[b][:].rearrange("p (e u) -> p u e", u=TILES),
                                      over(idx[b][:].unsqueeze(2), [P, TILES, P]), ALU.is_equal).then_inc(eq_done[b], 1)
                dve.wait_ge(exp_done, i * 4 + (q + 1))
                dve.wait_ge(mm_done[(q - 2) % 4], i + (1 if q < 2 else 2))
                m = msg[q % 2]
                dve.tensor_copy(m[:, :, HEADS * D:W], ea[:])
                for u in range(QUAD):
                    ins_ = dve.tensor_tensor(m[:, u, 0:HEADS * D].rearrange("p (h d) -> p h d", d=D),
                                             over(x[:, u, 0:D].unsqueeze(1), [P, HEADS, D]),
                                             over(ea[:, u, :].unsqueeze(2), [P, HEADS, D]), ALU.mult)
                ins_.then_inc(msg_done, 1)

    @block.scalar
    def _(act):
        for q in range(4):
            act.sem_inc(rows_ready[q], 1)
        for q in range(3):
            act.sem_inc(rows_free[q], 1)
        with act.Fori(0, NITER) as i:
            for q in range(4):
                act.wait_ge(dve_step, i * 12 + (q * 3 + 3))
                act.wait_ge(msg_done, i * 4 + (q + 1))
                act.activation(ea[:], al[:], ACT.Exp).then_inc(exp_done, 1)
                act.wait_ge(mm_done[q], i + 2)
                act.wait_ge(rows_free[q], i + 1)
                act.copy(rows[q][:], ps[q % 2][:, :, 0:W]).then_inc(rows_ready[q], 1)

    @block.tensor
    def _(pe):
        for q in range(4):
            pe.sem_inc(mm_done[q], 1)
        with pe.Fori(0, NITER) as i:
            for q in range(4):
                pe.wait_ge(msg_done, i * 4 + (q + 2))
                pe.wait_ge(rows_ready[(q - 2) % 4], i + (1 if q < 2 else 2))
                for u in range(QUAD):
                    mm = pe.matmul(ps[q % 2][:, u, 0:W], eq[q // 2][:, QUAD * (q % 2) + u, :],
                                   msg[q % 2][:, u, :], start=True, stop=True)
                mm.then_inc(mm_done[q], 1)

    return block


def l3_edges_windows(k, t, ctx):
    nc, ins = k.nc, k.ins
    loaded, sp_tick = k.sems("w3_loaded", 2), k.sem("w3_sp_tick")
    at_done, of_done, fetched = k.sem("w3_at"), k.sem("w3_of"), k.sem("w3_fetched")
    al_done, exp_done, msg_done, mm_done = k.sem("w3_al"), k.sem("w3_exp"), k.sem("w3_msg"), k.sem("w3_mm")
    rows_ready, rows_free, added, dve_step = (
        k.sem("w3_rows"), k.sem("w3_rows_free"), k.sem("w3_added"), k.sem("w3_dve"))
    LOADS = 2
    W = HEADS * D + HEADS
    STEPS = 2
    row = [k.sb(f"w3_row{b}", [P, GROUP], I32, ctx) for b in range(2)]
    win = [k.sb(f"w3_win{b}", [P, 3, 2 * HEADS], BF16, ctx) for b in range(2)]
    at = [k.sb(f"w3_at{b}", [P, TILES, P], BF16, ctx) for b in range(2)]
    of = [k.sb(f"w3_of{b}", [P, TILES, P], F32, ctx) for b in range(2)]
    off, act_step = k.sb("w3_off", [P, TILES, P], F32, ctx), k.sem("w3_act")
    al = k.sb("w3_al", [P, TILES, HEADS], F32, ctx)
    msg = [k.sb(f"w3_msg{b}", [P, TILES, W], F32, ctx) for b in range(2)]
    rows = [k.sb(f"w3_rows{b}", [P, W], F32, ctx) for b in range(2)]
    p_dm = [k.ps(f"w3_p_dm{b}", ctx) for b in range(2)]
    p_sum = [k.ps(f"w3_p_sum{b}", ctx) for b in range(2)]
    block = Path()
    row_d = ins["dst_idx"].rearrange("(g n) -> g n", n=GROUP)

    @block.sync
    def _(sp):
        def load(g, b):
            w = sp.value_load(t.base[0:1, bass.ds(g, 1)], min_val=0, max_val=N)
            sp.dma_start(win[b][:].rearrange("p a d -> p (a d)"), t.l3_dm_parts[bass.ds(w, P), :]).then_inc(loaded[b], 16)
            sp.dma_start(row[b][:], row_d[g].partition_broadcast(P)).then_inc(loaded[b], 16)

        load(0, 0)
        load(1, 1)
        with sp.Fori(0, NITER) as i:
            for b in range(2):
                sp.wait_ge(fetched, i * 2 + (b + 1))
                waited(sp, sp_tick)
                load(i * 2 + (2 + b), b)
        for b in range(2):
            sp.wait_ge(loaded[b], 16 * LOADS * (NITER + 1))

    @block.gpsimd
    def _(pool):
        pool.dma_start(rows_of(t.l3_dst), blank(t.zero, W)).then_inc(added, 16)
        with pool.Fori(0, NITER) as i:
            for b in range(2):
                g = i * 2 + b
                w = pool.value_load(t.base[0:1, bass.ds(g, 1)], min_val=0, max_val=N)
                pool.wait_ge(rows_ready, g + 3)
                pool.wait_ge(added, (g + 1) * 16)
                pool.sem_inc(rows_free, 1)
                pool.dma_start(t.l3_dst[bass.ds(w, P), :], rows[b][:], accum_op=ALU.add).then_inc(added, 16)
        pool.wait_ge(added, 16 * (NG + 1))

    @block.vector
    def _(dve):
        def match_of(g, b):
            dve.tensor_tensor(of[b][:], over(t.iota[:].unsqueeze(1), [P, TILES, P]),
                              over(t.rel[:, bass.ds(g, 1), :].rearrange("p g u -> p u g"), [P, TILES, P]),
                              ALU.is_equal).then_inc(of_done, 1)

        match_of(0, 0)
        with dve.Fori(0, NITER) as i:
            for b in range(2):
                g = i * 2 + b
                count = [0]

                def step(ins_):
                    count[0] += 1
                    ins_.then_inc(dve_step, 1)
                    dve.wait_ge(dve_step, g * STEPS + count[0])

                x = t.x_edge[:, bass.ds(g * TILES, TILES), :]
                dm = p_dm[b][:, 0:TILES * 2 * HEADS].rearrange("p (u a) -> p u a", u=TILES)
                dve.wait_ge(fetched, g + 1)
                step(dve.tensor_tensor(al[:], x[:, :, D:D + HEADS], dm[:, :, 0:HEADS], ALU.add))
                step(dve.scalar_tensor_tensor(out=al[:], in0=al[:], scalar=0.2, in1=al[:], op0=ALU.mult, op1=ALU.max))
                dve.tensor_tensor(al[:], al[:], dm[:, :, HEADS:2 * HEADS], ALU.subtract).then_inc(al_done, 1)
                dve.wait_ge(exp_done, g + 1)
                m = msg[b]
                for h in range(HEADS):
                    ins_ = dve.tensor_tensor(m[:, :, h * D:(h + 1) * D], x[:, :, 0:D],
                                             over(m[:, :, HEADS * D + h:HEADS * D + h + 1], [P, TILES, D]), ALU.mult)
                ins_.then_inc(msg_done, 1)
                dve.wait_ge(mm_done, g + 1)
                match_of(g + 1, 1 - b)

    @block.scalar
    def _(act):
        act.sem_inc(rows_ready, 2)
        act.sem_inc(rows_free, 1)

        def weights(g, b):
            act.wait_ge(al_done, g + 1)
            act.activation(msg[b][:, :, HEADS * D:W], al[:], ACT.Exp).then_inc(exp_done, 1)

        def sums(g, b):
            act.wait_ge(mm_done, g + 2)
            act.wait_ge(rows_free, g + 1)
            act.copy(rows[b][:], p_sum[b][:, 0:W]).then_inc(rows_ready, 1)

        def match_at(g, b, turn):
            def step(ins_):
                ins_.then_inc(act_step, 1)
                act.wait_ge(act_step, g + 1)

            act.wait_ge(loaded[b], turn * (16 * LOADS))
            act_match_at(act, t, at[b], row[b], g, off, step).then_inc(at_done, 1)

        match_at(0, 0, 1)
        act.wait_ge(at_done, 1)
        match_at(1, 1, 1)
        weights(0, 0)
        with act.Fori(0, NITER - 1) as i:
            for b in range(2):
                act.wait_ge(at_done, i * 2 + (b + 2))
                match_at(i * 2 + (b + 2), b, i + 2)
                weights(i * 2 + (b + 1), 1 - b)
                sums(i * 2 + b, b)
        act.wait_ge(at_done, NG)
        match_at(NG, 0, NITER + 1)
        weights(NG - 1, 1)
        sums(NG - 2, 0)
        sums(NG - 1, 1)

    @block.tensor
    def _(pe):
        pe.sem_inc(mm_done, 1)

        def fetch(b, nth):
            pe.wait_ge(at_done, nth)
            for u in range(TILES):
                for part in range(3):
                    mm = pe.matmul(p_dm[b][:, u * 2 * HEADS:(u + 1) * 2 * HEADS], at[b][:, u, :], win[b][:, part, :],
                                   start=(part == 0), stop=(part == 2))
            mm.then_inc(fetched, 1)

        fetch(0, 1)
        with pe.Fori(0, NITER) as i:
            for b in range(2):
                g = i * 2 + b
                fetch(1 - b, g + 2)
                pe.wait_ge(of_done, g + 1)
                pe.wait_ge(msg_done, g + 1)
                pe.wait_ge(rows_ready, g + 1)
                for u in range(TILES):
                    mm = pe.matmul(p_sum[b][:, 0:W], of[b][:, u, :], msg[b][:, u, :],
                                   start=(u == 0), stop=(u == TILES - 1))
                mm.then_inc(mm_done, 1)

    return block


def l3_attend(k, t, h, self_w):
    nc, ins = k.nc, k.ins
    loaded, dve_step, norm_done = k.sem("l3a_loaded"), k.sem("l3a_dve"), k.sem("l3a_norm")
    picked, turned, copied, mm_done, out_done = (
        k.sem("l3a_picked"), k.sem("l3a_turned"), k.sem("l3a_copied"), k.sem("l3a_mm"), k.sem("l3a_out"))
    var_ready, std_ready = k.sem("l3a_var"), k.sem("l3a_std")
    HC = HEADS * D
    with ExitStack() as ctx:
        a = [k.sb(f"l3a_s{n}", [P, NB, HC + HEADS], F32, ctx) for n in range(2)]
        wg = k.sb("l3a_wg", [P, 2, D], F32, ctx)
        vecs = k.sb("l3a_vecs", [P, 3, D], F32, ctx)
        part = k.sb("l3a_part", [P, CH, HC], F32, ctx)
        aT = k.sb("l3a_aT", [P, CH * 2, P], F32, ctx)
        c, q, st = (k.sb("l3a_c", [P, NB, D], F32, ctx), k.sb("l3a_q", [P, NB, D], F32, ctx),
                    k.sb("l3a_st", [P, 4, NB], F32, ctx))
        pt, po = k.ps("l3a_pt", ctx, (P, CH * 2, P)), k.ps("l3a_po", ctx)
        block = ctx.enter_context(nc.Block())
        LOADS = 1 + HEADS + 3

        @block.sync
        def _(sp):
            sp.dma_start(a[0][:], rows_of(t.l3_dst)).then_inc(loaded, 16)
            for hd in range(HEADS):
                sp.dma_start(wg[D * (hd % 4):D * (hd % 4 + 1), hd // 4, :],
                             ins["L3_W_gat"][:, hd * D:(hd + 1) * D]).then_inc(loaded, 16)
            for n, name in enumerate(("bias_gat", "g1", "be1")):
                sp.dma_start(vecs[:, n, :], ins[f"L3_{name}"].partition_broadcast(P)).then_inc(loaded, 16)

        @block.vector
        def _(dve):
            step = chained(dve_step)
            dve.wait_ge(loaded, 16 * LOADS)
            den = a[0][:, :, HC:HC + HEADS]
            step(dve, dve.tensor_tensor(den, den, self_w[:], ALU.add))
            for hd in range(HEADS):
                step(dve, dve.tensor_tensor(a[1][:, :, hd * D:(hd + 1) * D], t.x[:],
                                            over(self_w[:, :, hd:hd + 1], [P, NB, D]), ALU.mult))
            step(dve, dve.tensor_tensor(a[0][:, :, 0:HC], a[0][:, :, 0:HC], a[1][:, :, 0:HC], ALU.add))
            step(dve, dve.tensor_scalar(den, den, 1e-16, None, ALU.add))
            step(dve, dve.reciprocal(den, den))
            step(dve, dve.tensor_scalar(den, den, 1.0 / HEADS, None, ALU.mult))
            for hd in range(HEADS):
                step(dve, dve.tensor_tensor(a[1][:, :, hd * D:(hd + 1) * D], a[0][:, :, hd * D:(hd + 1) * D],
                                            over(a[0][:, :, HC + hd:HC + hd + 1], [P, NB, D]), ALU.mult))
            dve.sem_inc(norm_done, 1)
            dve.sem_inc(out_done, 1)
            with dve.Fori(0, NB // CH) as n:
                dve.wait_ge(mm_done, n + 2)
                dve.tensor_copy(h[:, bass.ds(n * CH, CH), :],
                                po[:, 0:CH * D].rearrange("p (b d) -> p b d", b=CH)).then_inc(out_done, 1)
            dve.wait_ge(out_done, NB // CH + 1)
            step(dve, dve.tensor_tensor(h[:], h[:], over(vecs[:, 0:1, :], [P, NB, D]), ALU.add))
            step(dve, dve.tensor_tensor(h[:], h[:], t.x[:], ALU.add))
            layer_norm(dve, step, h[:], h[:], c[:], q[:], st, var_ready, std_ready, 1)
            step(dve, dve.tensor_tensor(h[:], h[:], over(vecs[:, 1:2, :], [P, NB, D]), ALU.mult))
            step(dve, dve.tensor_tensor(h[:], h[:], over(vecs[:, 2:3, :], [P, NB, D]), ALU.add))

        @block.scalar
        def _(act):
            act.wait_ge(norm_done, 1)
            with act.Fori(0, NB // CH) as n:
                act.wait_ge(mm_done, n + 1)
                act.copy(part[:], a[1][:, bass.ds(n * CH, CH), 0:HC]).then_inc(picked, 1)
                act.wait_ge(turned, n + 1)
                act.copy(aT[:], pt[:]).then_inc(copied, 1)
            std_of(act, st, var_ready, std_ready, 1)

        @block.tensor
        def _(pe):
            pe.sem_inc(mm_done, 1)
            with pe.Fori(0, NB // CH) as n:
                pe.wait_ge(picked, n + 1)
                for b in range(CH):
                    for half in range(2):
                        mm = pe.transpose(pt[:, 2 * b + half, :], part[:, b, half * P:(half + 1) * P], t.ident[:])
                mm.then_inc(turned, 1)
                pe.wait_ge(copied, n + 1)
                pe.wait_ge(out_done, n + 1)
                for b in range(CH):
                    for half in range(2):
                        mm = pe.matmul(po[:, b * D:(b + 1) * D], aT[:, 2 * b + half, :], wg[:, half, :],
                                       start=(half == 0), stop=(half == 1))
                mm.then_inc(mm_done, 1)


def finish(k, t, h, ff, out):
    nc, ins = k.nc, k.ins
    loaded, dve_step, var_ready, std_ready, done, stored = (
        k.sem("fin_loaded"), k.sem("fin_dve"), k.sem("fin_var"), k.sem("fin_std"), k.sem("fin_done"), k.sem("fin_stored"))
    with ExitStack() as ctx:
        vecs = k.sb("fin_vecs", [P, 2, D], F32, ctx)
        c, q, st = (k.sb("fin_c", [P, NB, D], F32, ctx), k.sb("fin_q", [P, NB, D], F32, ctx),
                    k.sb("fin_st", [P, 4, NB], F32, ctx))
        block = ctx.enter_context(nc.Block())
        whole = N // P

        @block.sync
        def _(sp):
            for n, name in enumerate(("g2", "be2")):
                sp.dma_start(vecs[:, n, :], ins[f"L3_{name}"].partition_broadcast(P)).then_inc(loaded, 16)
            sp.wait_ge(done, 1)
            sp.dma_start(out[0:whole * P].rearrange("(j p) d -> p j d", p=P), t.x[:, 0:whole, :]).then_inc(stored, 16)
            sp.dma_start(out[whole * P:N], t.x[0:N - whole * P, whole, :]).then_inc(stored, 16)
            sp.wait_ge(stored, 32)

        @block.scalar
        def _(act):
            for n in (1, 2):
                std_of(act, st, var_ready, std_ready, n)

        @block.vector
        def _(dve):
            step = chained(dve_step)
            dve.wait_ge(loaded, 32)
            step(dve, dve.tensor_tensor(h[:], h[:], ff[:], ALU.add))
            layer_norm(dve, step, h[:], h[:], c[:], q[:], st, var_ready, std_ready, 1)
            step(dve, dve.tensor_tensor(h[:], h[:], over(vecs[:, 0:1, :], [P, NB, D]), ALU.mult))
            step(dve, dve.tensor_tensor(h[:], h[:], over(vecs[:, 1:2, :], [P, NB, D]), ALU.add))
            step(dve, dve.tensor_tensor(h[:], h[:], t.x[:], ALU.add))
            layer_norm(dve, step, h[:], t.x[:], c[:], q[:], st, var_ready, std_ready, 2)
            dve.sem_inc(done, 1)


def l3(k, t, out):
    t.l3_max = [k.dram(f"l3_max{u}", [NT, HEADS]) for u in range(QUAD)]
    t.l3_dm = k.dram("l3_dm", [NT, 2 * HEADS])
    t.l3_dm_parts = k.dram("l3_dm_parts", [NT, 3 * 2 * HEADS], BF16)
    t.l3_dst = k.dram("l3_dst", [NT, HEADS * D + HEADS])
    outer = k.ctx.enter_context(ExitStack())
    with ExitStack() as ctx:
        self_w = k.sb("self_w", [P, NB, HEADS], F32, outer)
        t.x_edge = k.sb("x_edge", [P, NG * TILES, D + HEADS], F32, ctx)
        with ExitStack() as c0:
            a_all = k.sb("a_all", [P, NB, 2 * HEADS], F32, c0)
            with ExitStack() as c1:
                xT = k.sb("l3_xT", [D, NT], F32, c1)
                turn_nodes(k, "l3t", t, t.x, xT)
                l3_scores(k, t, xT, a_all)
            k.next_layer()
            either(k, t, l3_max_windows, l3_max_general)
            l3_bounds(k, t, a_all, self_w)
            k.next_layer()
        either(k, t, l3_edges_windows, l3_edges_general)
    with ExitStack() as ctx:
        h, ff = k.sb("l3_h", [P, NB, D], F32, ctx), k.sb("l3_ff", [P, NB, D], F32, ctx)
        l3_attend(k, t, h, self_w)
        xT = k.sb("l3_hT", [D, NT], F32, ctx)
        turn_nodes(k, "l3u", t, h, xT)
        mlp(k, "l3f", None, xT, [("L3_w1", "L3_b1", "L3_w2", "L3_b2", ff)])
        finish(k, t, h, ff, out)


class Tables:
    pass


def program(nc, ins, out, upto=99):
    with ExitStack() as ctx:
        k = Kit(nc, ctx, ins)
        t = Tables()
        t.ident, t.tri = k.sb("ident", [P, P]), k.sb("tri", [P, P])
        t.spill = k.sb("spill", [P, 1])
        t.zero, t.lowest = k.sb("zero", [P, 264]), k.sb("lowest", [P, HEADS])
        t.x = k.sb("x", [P, NB, D])
        t.nvec = k.sb("nvec", [P, NGL, TILES * 3])
        t.wgt, t.wgain = k.sb("wgt", [P, NGL, TILES]), k.sb("wgain", [P, NGL, TILES])
        t.to_dst, t.to_src = k.sb("to_dst", [P, NG, TILES], I32), k.sb("to_src", [P, NG, TILES], I32)
        t.h2, t.x1, t.x2, t.x3 = (k.dram("t_h2", [NT, D]), k.dram("t_x1", [NT, D]), k.dram("t_x2", [NT, D]),
                                  k.dram("t_x3", [NT, D + HEADS]))
        t.x1_parts = k.dram("t_x1_parts", [NT, 3 * D], BF16)
        t.l0_dst, t.l0_src = k.dram("l0_dst", [NT, 2 * D]), [k.dram(f"l0_src{n}", [NT, 2 * D]) for n in range(4)]
        t.l1_dst = k.dram("l1_dst", [NT, D])
        t.l2_src = [k.dram(f"l2_src{n}", [NT, D + 1]) for n in range(4)]
        t.flag = k.sb("flag", [P, 1], I32)
        t.base, t.node = k.sb("base", [P, NGL], I32), k.sb("node", [P, NGL], I32)
        t.rel, t.iota = k.sb("rel", [P, NGL, TILES], I32), k.sb("iota", [P, P], I32)
        t.node_neg, t.rel_neg = k.sb("node_neg", [P, NGL]), k.sb("rel_neg", [P, NGL, TILES])
        t.iota_f = k.sb("iota_f", [P, P])
        setup(k, t)
        windows(k, t)
        hid_ctx = ExitStack()
        t.hid = k.sb("hid", [P, NG * TILES, MUL], F32, hid_ctx)
        with ExitStack() as c0:
            t.h1, h2 = k.sb("h1", [P, NB, D], F32, c0), k.sb("h2", [P, NB, D], F32, c0)
            mlp(k, "l0m", "xT", None, [("L0_W1a", "L0_b1a", "L0_W2a", "L0_b2a", t.h1),
                                       ("L0_W1b", "L0_b1b", "L0_W2b", "L0_b2b", h2)])
            store_rows(k, "l0s", [(t.h2, h2[:])])
            k.next_layer()
            either(k, t, l0_edges_windows, l0_edges_general)
            l0_nodes(k, t)
        k.next_layer()
        if upto > 1:
            either(k, t, l1_edges_windows, l1_edges_general)
            residual_nodes(k, "l1n", t, [t.l1_dst], lambda dve, step, sums: None, t.x2)
        hid_ctx.close()
        if upto > 2:
            k.next_layer()
            either(k, t, l2_edges_windows, l2_edges_general)

            def laplacian(dve, step, sums):
                a, b = sums[0:2]
                for other in sums[1:]:
                    step(dve, dve.tensor_tensor(a[:], a[:], other[:], ALU.add))
                step(dve, dve.tensor_tensor(b[:, :, 0:D], t.x[:], over(a[:, :, D:D + 1], [P, NB, D]), ALU.mult))
                step(dve, dve.tensor_tensor(a[:, :, 0:D], a[:, :, 0:D], b[:, :, 0:D], ALU.subtract))

            residual_nodes(k, "l2n", t, t.l2_src, laplacian, None)
        if upto > 3:
            k.next_layer()
            l3(k, t, out)
        else:
            done = k.sem("done")
            with nc.Block() as block:
                @block.sync
                def _(sp):
                    sp.dma_start(out[0:24 * P].rearrange("(j p) d -> p j d", p=P), t.x[:, 0:24, :]).then_inc(done, 16)
                    sp.dma_start(out[24 * P:N], t.x[0:N - 24 * P, 24, :]).then_inc(done, 16)
                    sp.wait_ge(done, 32)


def layouts(inputs):
    def a(name):
        return np.ascontiguousarray(np.asarray(inputs[name]))

    def padded(x, n, value):
        full = np.full((n,) + x.shape[1:], value, x.dtype)
        full[:x.shape[0]] = x
        return full

    el = NGL * GROUP
    x = padded(a("x"), NT, 0)
    emb = padded(a("edge_attr_10"), el, 0)
    out = {
        "x_rows": x, "xT": np.ascontiguousarray(x.T),
        "src_idx": padded(a("src"), el, N), "dst_idx": padded(a("dst"), el, N),
        "edge_feat": padded(a("edge_attr_32"), el, 0), "edge_vec": padded(a("edge_attr_3"), el, 1),
        "edge_w": padded(a("edge_weight"), el, 0),
        "embT": np.ascontiguousarray(emb.reshape(NGL, P, TILES, 10).transpose(0, 3, 2, 1).reshape(NGL, 10, GROUP)),
        "iota": np.arange(P, dtype=np.int32), "pick": np.tile(np.eye(HEADS, dtype=np.float32), (3, 1)),
        "ident": np.eye(P, dtype=np.float32), "tri": np.tril(np.ones((P, P), np.float32), -1),
        "spill": (SPILL + np.arange(P, dtype=np.float32))[:, None],
    }
    for name in ("W1a", "b1a", "W2a", "b2a", "W1b", "b1b", "W2b", "b2b"):
        out[f"L0_{name}"] = a(f"L0_gnn_{name}")
    out["L1_W1"] = a("L1_gnn_W1")
    out["L1_W2"] = np.ascontiguousarray(a("L1_gnn_W2").reshape(MUL, 7, MUL, MOUT).transpose(1, 2, 3, 0))
    for name in ("W_gat", "att_src", "att_dst", "bias_gat", "w1", "b1", "w2", "b2", "g1", "be1", "g2", "be2"):
        out[f"L3_{name}"] = a(f"L3_gnn_{name}")
    return out


def kernel(**inputs):
    import concourse.bacc as bacc
    from concourse.bass_utils import run_bass_kernel_spmd

    nc = bacc.Bacc("TRN2", target_bir_lowering=False, num_devices=1)
    arrays = {f"in_{name}": array for name, array in layouts(inputs).items()}
    ins = {name[3:]: nc.dram_tensor(name, a.shape, mybir.dt.from_np(a.dtype), kind="ExternalInput").ap()
           for name, a in arrays.items()}
    out = nc.dram_tensor("out_0", (N, D), F32, kind="ExternalOutput").ap()
    program(nc, ins, out)
    return run_bass_kernel_spmd(nc, [arrays], core_ids=[0]).results[0]["out_0"]
```
